# Optimizing a Trainium2 kernel written in Bass

```python
import numpy as np
import jax
import jax.numpy as jnp

def _softmax(x, axis=-1):
    return jax.nn.softmax(x, axis=axis)

def _gelu(x):
    return jax.nn.gelu(x, approximate=True)

def _silu(x):
    return jax.nn.silu(x)

def _sigmoid(x):
    return jax.nn.sigmoid(x)

def _layernorm(x, axis=-1, eps=1e-05):
    m = jnp.mean(x, axis=axis, keepdims=True)
    v = jnp.var(x, axis=axis, keepdims=True)
    return (x - m) / jnp.sqrt(v + eps)

def _scatter_add(tgt, idx, src, axis=0):
    return tgt.at[idx].add(src)

def _segment_sum(src, seg, n):
    return jax.ops.segment_sum(src, seg, n)
kernel_name = 'mk_vit_tower_d1_tok_img256_r4_409429'

def setup_inputs(seed: int=0):
    np.random.seed(seed)
    _w = jnp.asarray

    def _rec_inputs():
        import jax
        import jax.numpy as jnp
        _rk = jax.random.key(seed)
        x = -0.000596345 + 1.00056 * jax.random.normal(jax.random.fold_in(_rk, 1), (32, 64, 64, 3), jnp.float32)
        return x
    x = _rec_inputs()

    def _L0_tok_setup():
        import jax, jax.numpy as jnp
        import numpy as np
        from jax import lax
        NEG_SLOPE = 0.01

        def leaky(v):
            return jnp.where(v >= 0, v, NEG_SLOPE * v)
        key = jax.random.key(seed)
        ks = jax.random.split(key, 12)
        B, H, W = (16, 64, 64)
        width, mx, my, L, nl = (32, 16, 16, 3, 4)
        scale = 1.0 / (width * width)
        return {'x': jax.random.normal(ks[0], (B, H, W, 3), jnp.float32), 'input_grid': jax.random.uniform(ks[1], (H, W, 2), jnp.float32), 'P_w': jax.random.normal(ks[2], (5, width), jnp.float32) * 0.3, 'P_b': jax.random.normal(ks[3], (width,), jnp.float32) * 0.05, 'spec_wr': jax.random.uniform(ks[4], (nl, width, width, mx, my), jnp.float32) * scale, 'spec_wi': jax.random.uniform(ks[5], (nl, width, width, mx, my), jnp.float32) * scale, 'conv_w': jax.random.normal(ks[6], (nl, width, width, L, L), jnp.float32) * 0.05, 'conv_b': jax.random.normal(ks[7], (nl, width), jnp.float32) * 0.05, 'Q1_w': jax.random.normal(ks[8], (width, width), jnp.float32) * 0.15, 'Q1_b': jax.random.normal(ks[9], (width,), jnp.float32) * 0.05, 'Q2_w': jax.random.normal(ks[10], (width, 1), jnp.float32) * 0.15, 'Q2_b': jax.random.normal(ks[11], (1,), jnp.float32) * 0.05}
    _L0_tok_all = _L0_tok_setup()
    _L0_tok_in = {k: v for k, v in _L0_tok_all.items() if k in ('input_grid', 'P_w', 'P_b', 'spec_wr', 'spec_wi', 'conv_w', 'conv_b', 'Q1_w', 'Q1_b', 'Q2_w', 'Q2_b')}
    del _L0_tok_all

    def _L0_attn_setup():
        import jax, jax.numpy as jnp
        import numpy as np
        key = jax.random.key(seed)
        k1, k2 = jax.random.split(key)
        B, N, F = (4, 1024, 64)
        nodes = jax.random.normal(k1, (B, N, F), dtype=jnp.float32)
        limit = np.sqrt(6.0 / (F + F)).astype(np.float32)
        W = jax.random.uniform(k2, (F, F), dtype=jnp.float32, minval=-limit, maxval=limit)
        return {'nodes': nodes, 'W': W}
    _L0_attn_all = _L0_attn_setup()
    _L0_attn_in = {k: v for k, v in _L0_attn_all.items() if k in ('W',)}
    del _L0_attn_all

    def _L0_ffn_setup():
        import jax, jax.numpy as jnp
        import numpy as np
        B, S, H, NH, NE = (4, 256, 64, 4, 4)
        D = H // NH
        EPS = 1e-08

        def layernorm(x, g, b):
            m = jnp.mean(x, axis=-1, keepdims=True)
            v = jnp.mean((x - m) ** 2, axis=-1, keepdims=True)
            return (x - m) / jnp.sqrt(v + EPS) * g + b
        key = jax.random.key(seed)
        ks = jax.random.split(key, 18)
        sc = 0.05
        return {'x': jax.random.normal(ks[0], (B, S, H), jnp.float32), 'hl_w': jax.random.normal(ks[1], (NH, D, H), jnp.float32) * sc, 'hl_b': jax.random.normal(ks[2], (NH, D), jnp.float32) * sc, 'wq': jax.random.normal(ks[3], (NH, NE, D, D), jnp.float32) * sc, 'wk': jax.random.normal(ks[4], (NH, D, D), jnp.float32) * sc, 'wv': jax.random.normal(ks[5], (NH, D, D), jnp.float32) * sc, 'gate_w': jax.random.normal(ks[6], (NH, NE, NE * D), jnp.float32) * sc, 'gate_b': jax.random.normal(ks[7], (NH, NE), jnp.float32) * sc, 'ln_g': jnp.ones((D,), jnp.float32), 'ln_b': jnp.zeros((D,), jnp.float32), 'fc1_w': jax.random.normal(ks[8], (D, D), jnp.float32) * sc, 'fc1_b': jax.random.normal(ks[9], (D,), jnp.float32) * sc, 'fc2_w': jax.random.normal(ks[10], (D, D), jnp.float32) * sc, 'fc2_b': jax.random.normal(ks[11], (D,), jnp.float32) * sc, 'fnorm_g': jnp.ones((D,), jnp.float32), 'fnorm_b': jnp.zeros((D,), jnp.float32), 'fgate_w': jax.random.normal(ks[12], (NH, H), jnp.float32) * sc}
    _L0_ffn_all = _L0_ffn_setup()
    _L0_ffn_in = {k: v for k, v in _L0_ffn_all.items() if k in ('hl_w', 'hl_b', 'wq', 'wk', 'wv', 'gate_w', 'gate_b', 'ln_g', 'ln_b', 'fc1_w', 'fc1_b', 'fc2_w', 'fc2_b', 'fnorm_g', 'fnorm_b', 'fgate_w')}
    del _L0_ffn_all
    return {'x': x, 'L0_tok_input_grid': _L0_tok_in['input_grid'], 'L0_tok_P_w': _L0_tok_in['P_w'], 'L0_tok_P_b': _L0_tok_in['P_b'], 'L0_tok_spec_wr': _L0_tok_in['spec_wr'], 'L0_tok_spec_wi': _L0_tok_in['spec_wi'], 'L0_tok_conv_w': _L0_tok_in['conv_w'], 'L0_tok_conv_b': _L0_tok_in['conv_b'], 'L0_tok_Q1_w': _L0_tok_in['Q1_w'], 'L0_tok_Q1_b': _L0_tok_in['Q1_b'], 'L0_tok_Q2_w': _L0_tok_in['Q2_w'], 'L0_tok_Q2_b': _L0_tok_in['Q2_b'], 'L0_attn_W': _L0_attn_in['W'], 'L0_ffn_hl_w': _L0_ffn_in['hl_w'], 'L0_ffn_hl_b': _L0_ffn_in['hl_b'], 'L0_ffn_wq': _L0_ffn_in['wq'], 'L0_ffn_wk': _L0_ffn_in['wk'], 'L0_ffn_wv': _L0_ffn_in['wv'], 'L0_ffn_gate_w': _L0_ffn_in['gate_w'], 'L0_ffn_gate_b': _L0_ffn_in['gate_b'], 'L0_ffn_ln_g': _L0_ffn_in['ln_g'], 'L0_ffn_ln_b': _L0_ffn_in['ln_b'], 'L0_ffn_fc1_w': _L0_ffn_in['fc1_w'], 'L0_ffn_fc1_b': _L0_ffn_in['fc1_b'], 'L0_ffn_fc2_w': _L0_ffn_in['fc2_w'], 'L0_ffn_fc2_b': _L0_ffn_in['fc2_b'], 'L0_ffn_fnorm_g': _L0_ffn_in['fnorm_g'], 'L0_ffn_fnorm_b': _L0_ffn_in['fnorm_b'], 'L0_ffn_fgate_w': _L0_ffn_in['fgate_w']}

def reference(x, L0_tok_input_grid, L0_tok_P_w, L0_tok_P_b, L0_tok_spec_wr, L0_tok_spec_wi, L0_tok_conv_w, L0_tok_conv_b, L0_tok_Q1_w, L0_tok_Q1_b, L0_tok_Q2_w, L0_tok_Q2_b, L0_attn_W, L0_ffn_hl_w, L0_ffn_hl_b, L0_ffn_wq, L0_ffn_wk, L0_ffn_wv, L0_ffn_gate_w, L0_ffn_gate_b, L0_ffn_ln_g, L0_ffn_ln_b, L0_ffn_fc1_w, L0_ffn_fc1_b, L0_ffn_fc2_w, L0_ffn_fc2_b, L0_ffn_fnorm_g, L0_ffn_fnorm_b, L0_ffn_fgate_w):
    import jax
    import jax.numpy as jnp

    def _L0_tok_ref(x, input_grid, P_w, P_b, spec_wr, spec_wi, conv_w, conv_b, Q1_w, Q1_b, Q2_w, Q2_b):
        import jax, jax.numpy as jnp
        import numpy as np
        from jax import lax
        NEG_SLOPE = 0.01

        def leaky(v):
            return jnp.where(v >= 0, v, NEG_SLOPE * v)
        B, H, W, _ = x.shape
        nl, _, _, mx, my = spec_wr.shape
        grid = jnp.broadcast_to(input_grid[None], (B, H, W, input_grid.shape[-1]))
        h = jnp.concatenate([grid, x], axis=-1) @ P_w + P_b
        h = jnp.transpose(h, (0, 3, 1, 2))
        dn = ('NCHW', 'OIHW', 'NCHW')
        for i in range(nl):
            h_ft = jnp.fft.rfft2(h)
            w_c = spec_wr[i] + 1j * spec_wi[i]
            out_modes = jnp.einsum('bixy,ioxy->boxy', h_ft[:, :, :mx, :my], w_c)
            spec = jnp.fft.irfft2(out_modes, s=(H, W))
            conv = lax.conv_general_dilated(h, conv_w[i], (1, 1), 'SAME', dimension_numbers=dn)
            conv = conv + conv_b[i][None, :, None, None]
            h = leaky(spec + conv)
        h = jnp.transpose(h, (0, 2, 3, 1))
        h = leaky(h @ Q1_w + Q1_b)
        out = (h @ Q2_w + Q2_b)[..., 0]
        return out

    def _L0_attn_ref(nodes, W):
        import jax, jax.numpy as jnp
        import numpy as np
        F = nodes.shape[-1]
        norm_const = 1.0 / jnp.sqrt(jnp.asarray(F, dtype=nodes.dtype))
        x = jnp.einsum('bnf,fg->bng', nodes, W)
        prods = jnp.einsum('bnf,bmf->bnm', x, nodes)
        att_scores = jax.nn.softmax(prods * norm_const, axis=-1)
        messgs = jnp.einsum('bnm,bmf->bnf', att_scores, nodes)
        return messgs

    def _L0_ffn_ref(x, hl_w, hl_b, wq, wk, wv, gate_w, gate_b, ln_g, ln_b, fc1_w, fc1_b, fc2_w, fc2_b, fnorm_g, fnorm_b, fgate_w):
        import jax, jax.numpy as jnp
        import numpy as np
        B, S, H, NH, NE = (4, 256, 64, 4, 4)
        D = H // NH
        EPS = 1e-08

        def layernorm(x, g, b):
            m = jnp.mean(x, axis=-1, keepdims=True)
            v = jnp.mean((x - m) ** 2, axis=-1, keepdims=True)
            return (x - m) / jnp.sqrt(v + EPS) * g + b
        b, s, h = x.shape
        nh, d, _ = wk.shape
        ne = wq.shape[1]
        sx = jnp.einsum('bsh,ndh->bnsd', x, hl_w) + hl_b[None, :, None, :]
        pad = sx == 0
        q = jnp.einsum('bnsd,neod->bneso', sx, wq)
        k = jnp.einsum('bnsd,nod->bnso', sx, wk)
        v = jnp.einsum('bnsd,nod->bnso', sx, wv)
        causal = jnp.where(jnp.tril(jnp.ones((s, s), bool)), 0.0, -jnp.inf).astype(x.dtype)
        scores = jnp.einsum('bnesd,bntd->bnest', q, k) * d ** 0.5 + causal
        att = jax.nn.softmax(scores, axis=-1)
        qkv = jnp.einsum('bnest,bntd->bnesd', att, v)
        qkv = jnp.where(pad[:, :, None], 0.0, qkv)
        out = jnp.transpose(qkv, (0, 1, 3, 2, 4)).reshape(b, nh, s, ne * d)
        gs = jax.nn.softmax(jnp.einsum('bnsf,nef->bnse', out, gate_w) + gate_b[None, :, None, :], axis=-1)
        mixed = jnp.einsum('bnsed,bnse->bnsd', out.reshape(b, nh, s, ne, d), gs)
        resid = sx[jnp.arange(nh), jnp.arange(nh)]
        hn = layernorm(mixed + resid, ln_g, ln_b)
        f_n = jnp.transpose(hn, (0, 2, 1, 3)).reshape(b, s, h)
        fx = f_n.reshape(b, s, nh, d)
        pm = fx == 0
        hx = jnp.where(pm, 0.0, fx @ fc1_w.T + fc1_b)
        hx = jax.nn.relu(hx)
        hx = jnp.where(pm, 0.0, hx @ fc2_w.T + fc2_b)
        hx = layernorm(hx + fx, fnorm_g, fnorm_b)
        fout = hx.reshape(b, s, h)
        fg = jax.nn.softmax(fout @ fgate_w.T, axis=-1)
        return (fout.reshape(b, s, nh, d) * fg[..., None]).reshape(b, s, h)
    h = _L0_tok_ref(x, L0_tok_input_grid, L0_tok_P_w, L0_tok_P_b, L0_tok_spec_wr, L0_tok_spec_wi, L0_tok_conv_w, L0_tok_conv_b, L0_tok_Q1_w, L0_tok_Q1_b, L0_tok_Q2_w, L0_tok_Q2_b)
    h = h + _L0_attn_ref(_layernorm(h, axis=-1), L0_attn_W)
    h = h + _L0_ffn_ref(_layernorm(h, axis=-1), L0_ffn_hl_w, L0_ffn_hl_b, L0_ffn_wq, L0_ffn_wk, L0_ffn_wv, L0_ffn_gate_w, L0_ffn_gate_b, L0_ffn_ln_g, L0_ffn_ln_b, L0_ffn_fc1_w, L0_ffn_fc1_b, L0_ffn_fc2_w, L0_ffn_fc2_b, L0_ffn_fnorm_g, L0_ffn_fnorm_b, L0_ffn_fgate_w)
    return h

_drawn_inputs = setup_inputs


def setup_inputs(seed=0):
    import zlib

    import numpy as np

    out = dict(_drawn_inputs(seed))
    spreads = {'L0_ffn_ln_g': (1.0, 0.2),
     'L0_ffn_ln_b': (0.0, 0.1),
     'L0_ffn_fnorm_g': (1.0, 0.2),
     'L0_ffn_fnorm_b': (0.0, 0.1)}
    factors = {'L0_tok_spec_wr': 8.0,
     'L0_tok_spec_wi': 8.0,
     'L0_ffn_wq': 8.0,
     'L0_ffn_wk': 8.0,
     'L0_ffn_gate_w': 38.296,
     'L0_ffn_gate_b': 27.52,
     'L0_ffn_fc1_w': 3.335,
     'L0_ffn_fc1_b': 8.0}
    for name, (base, spread) in spreads.items():
        noise = np.random.default_rng([zlib.crc32(name.encode()), seed]).standard_normal(out[name].shape)
        drawn = base * np.exp(spread * noise) if base else spread * noise
        out[name] = jnp.asarray(drawn.astype(out[name].dtype))
    for name, factor in factors.items():
        out[name] = (out[name] * factor).astype(out[name].dtype)
    return out
```

```python
from contextlib import ExitStack

import numpy as np

import concourse.bass as bass
from concourse import mybir

F32 = mybir.dt.float32
F32R = mybir.dt.float32r
ALU = mybir.AluOpType
ACT = mybir.ActivationFunctionType
AX = mybir.AxisListType
ds = bass.ds

B, H, W = 32, 64, 64
C = 32
NL = 4
MODES = 16
G = 32
PITCH = G + 1
AREA = PITCH * PITCH
PAIRS = B // 2
HALF = G * G // 2
XIN = 20


def dft_constants():
    th = 2 * np.pi / H
    ex = np.zeros((2, 2, G, 2, 2, MODES))
    ey = np.zeros((2, 2, G, 2, 2, MODES, 2))
    iy = np.zeros((4, MODES, 2, 2, 2, 4, 16, 2))
    ix = np.zeros((4, 2, 2, 4, 2, 2, 2, 2, G))
    k, g = np.arange(MODES), np.arange(G)
    for s in range(2):
        a = th * np.outer(2 * g + s, k)
        for r in range(2):
            ex[s, r, :, r, 0] = np.cos(a)
            ex[s, r, :, r, 1] = -np.sin(a)
    for r in range(2):
        a = th * np.outer(2 * g + r, k)
        for b in range(2):
            ey[b, r, :, 0, b, :, 0] = np.cos(a)
            ey[b, r, :, 0, b, :, 1] = -np.sin(a)
            ey[b, r, :, 1, b, :, 0] = np.sin(a)
            ey[b, r, :, 1, b, :, 1] = np.cos(a)
    ih = np.arange(16)
    for q in range(4):
        for il in range(2):
            for r in range(2):
                a = th * np.outer(k, 4 * ih + 2 * il + r)
                iy[q, :, 0, 0, il, q, :, r] = np.cos(a)
                iy[q, :, 1, 0, il, q, :, r] = -np.sin(a)
                iy[q, :, 0, 1, il, q, :, r] = np.sin(a)
                iy[q, :, 1, 1, il, q, :, r] = np.cos(a)
        for kyb in range(4):
            ky = 4 * kyb + q
            w = (1.0 if ky == 0 else 2.0) / (H * W)
            for s in range(2):
                a = th * ky * (2 * g + s)
                for b in range(2):
                    for il in range(2):
                        ix[q, 0, il, kyb, b, s, b, il] = w * np.cos(a)
                        ix[q, 1, il, kyb, b, s, b, il] = -w * np.sin(a)
    parts = [ex.reshape(128, 64), ey.reshape(128, 128), iy.reshape(128, 512), ix.reshape(128, 256)]
    return np.concatenate(parts, axis=1).astype(np.float32)


def build(nc, xin_d, pw_d, pb_d, dft_d, spec_d, conv_d, convb_d, q1w_d, q1b_d, q2w_d, q2b_d, tail_d, onehot_d, causal_d, out_d):
    x_d = nc.dram_tensor("activations", [B, 128, G * PITCH], F32, kind="Internal").ap()
    h_d = nc.dram_tensor("tower_out", [B, 4, G * G], F32, kind="Internal").ap()

    build_tower(nc, xin_d, pw_d, pb_d, dft_d, spec_d, conv_d, convb_d, q1w_d, q1b_d, q2w_d, q2b_d, x_d, h_d)
    build_tail(nc, h_d, tail_d, onehot_d, causal_d, out_d)


def build_tower(nc, xin_d, pw_d, pb_d, dft_d, spec_d, conv_d, convb_d, q1w_d, q1b_d, q2w_d, q2b_d, x_d, h_d):
    with ExitStack() as ctx:
        def sb(name, shape, dt=F32):
            return ctx.enter_context(nc.sbuf_tensor(name, shape, dt))

        def sem(name):
            return ctx.enter_context(nc.semaphore(name))

        dft = sb("dft", [128, 960])
        ex = dft[:, 0:64]
        ey = dft[:, 64:192].rearrange("p (a n) -> p a n", a=2)
        iy = dft[:, 192:704].rearrange("p (m n) -> p m n", m=4)
        ix = dft[:, 704:960].rearrange("p (s b n) -> p s b n", s=2, b=2)
        pw = sb("pw", [128, 128])
        pb = sb("pb", [128, 1])
        q1w = sb("q1w", [128, 128])
        q1b = sb("q1b", [128, 1])
        q2w = sb("q2w", [128, 4])
        q2b = sb("q2b", [128, 1])
        conv_bias = sb("conv_bias", [128, NL])
        bias_now = sb("bias_now", [128, 1])
        conv_stage = sb("conv_stage", [128, 4, 128])
        conv_hi = sb("conv_hi", [128, 4, 128], F32R)
        conv_lo = sb("conv_lo", [128, 4, 128], F32R)
        xin = sb("xin", [128, 2, 2, G * G])
        x_now = sb("x_now", [128, 2, 2, G, PITCH])
        halo = sb("halo", [128, 2, AREA])
        halo_hi = sb("halo_hi", [128, 2, AREA], F32R)
        halo_lo = sb("halo_lo", [128, 2, AREA], F32R)
        xt = sb("xt", [128, 2, G, C])
        ft = sb("ft", [128, 2 * MODES, C])
        spec = sb("spec", [128, 4, 2 * MODES, B])
        wspec = sb("wspec", [128, 4 * MODES, 3, C])
        zt = sb("zt", [128, 4, B, C])
        vt = sb("vt", [128, 2, 16, 2, C])
        biased = sb("biased", [128, 2, HALF])
        hbiased = sb("hbiased", [128, 2, HALF])
        hid = sb("hid", [128, 4, HALF])
        h_now = sb("h_now", [128, 2, HALF])

        psum = ctx.enter_context(nc.psum_tensor("psum", [128, 8, HALF], F32))
        acc = [psum[:, 0, :], psum[:, 1, :]]
        vp = psum[:, 2:4, :].rearrange("p a b -> p (a b)")
        fxp = psum[:, 4:6, :]
        ap_ = psum[:, 6, 0:256]
        yp = psum[:, 7, :]
        zp = psum[:, :, :].rearrange("p a b -> p (a b)")

        s_const = sem("s_const")
        s_zero = sem("s_zero")
        s_past = sem("s_past")
        s_xin = [sem("s_xin0"), sem("s_xin1")]
        s_acc = sem("s_acc")
        s_bias = sem("s_bias")
        s_x = sem("s_x")
        s_store = [[sem(f"s_store{k}{m}") for m in range(2)] for k in range(2)]
        s_raw = [sem("s_raw0"), sem("s_raw1")]
        s_hi = sem("s_hi")
        s_lo = sem("s_lo")
        s_xt = sem("s_xt")
        s_fx = sem("s_fx")
        s_ft = sem("s_ft")
        s_fy = sem("s_fy")
        s_spec = sem("s_spec")
        s_w = sem("s_w")
        s_neg = sem("s_neg")
        s_cw = sem("s_cw")
        s_cwhi = sem("s_cwhi")
        s_cwlo = sem("s_cwlo")
        s_mix = sem("s_mix")
        s_zt = sem("s_zt")
        s_v = sem("s_v")
        s_vt = sem("s_vt")
        s_h1 = sem("s_h1")
        s_h1b = sem("s_h1b")
        s_hid = sem("s_hid")
        s_y = sem("s_y")
        s_h = sem("s_h")
        s_hst = [sem("s_hst0"), sem("s_hst1")]

        block = ctx.enter_context(nc.Block())
        NCONST = 9

        def reached(eng, which, n):
            if not (isinstance(n, int) and n <= 0):
                eng.wait_ge(which, n)

        def over_pairs(eng, pair, after=None):
            pair(0, 0, True)
            pair(1, 1, False)
            with eng.Fori(1, PAIRS // 2) as it:
                pair(it * 2, 0, False)
                pair(it * 2 + 1, 1, False)

        def over_layers(eng, layer):
            with eng.Fori(0, NL - 1) as l:
                layer(l, False)
            layer(NL - 1, True)

        @block.sync
        def _(sp):
            for dst, src in ((dft[:], dft_d), (pw[:], pw_d), (pb[:], pb_d), (q1w[:], q1w_d), (q1b[:], q1b_d),
                             (q2w[:], q2w_d), (q2b[:], q2b_d), (conv_bias[:], convb_d)):
                sp.dma_start(dst, src).then_inc(s_const, 16)
            sp.dma_start(wspec[:, :, 1:3, :], spec_d[0]).then_inc(s_w, 16)
            sp.dma_start(conv_stage[:], conv_d[0]).then_inc(s_cw, 16)
            sp.wait_ge(s_zero, 1)

            def load_pair(p, k):
                for m in range(2):
                    sp.dma_start(xin[0:XIN, k, m:m + 1, :],
                                 xin_d[:, ds(p * 2 + m, 1), :]).then_inc(s_xin[k], 16)

            load_pair(0, 0)
            load_pair(1, 1)
            with sp.Fori(1, PAIRS // 2) as it:
                for k in range(2):
                    sp.wait_ge(s_acc, it * 8 + (4 * k - 4))
                    load_pair(it * 2 + k, k)

            def load_halo(l, b, m):
                for s in range(2):
                    for r in range(2):
                        n = G * PITCH - (s and r)
                        off = r * PITCH + s
                        d = (1 - s) * 64 + (1 - r) * 32
                        g = s * 64 + r * 32
                        sp.dma_start(halo[d:d + 32, m, off:off + n],
                                     x_d[ds(b, 1), g:g + 32, 0:n].rearrange("a p n -> (a p) n")
                                     ).then_inc(s_raw[m], 16)

            def layer(l, last):
                for k in range(2):
                    for m in range(2):
                        sp.wait_ge(s_store[k][m], (l + 1) * (16 * PAIRS // 2))
                sp.sem_inc(s_past, 1)
                sp.wait_ge(s_acc, (l + 1) * (4 * PAIRS))
                load_halo(l, 0, 0)
                load_halo(l, 1, 1)
                if not last:
                    sp.wait_ge(s_mix, l * 4 + 4)
                    sp.dma_start(wspec[:, :, 1:3, :],
                                 spec_d[ds(l + 1, 1)].rearrange("a p n t o -> (a p) n t o")).then_inc(s_w, 16)
                    sp.wait_ge(s_cwlo, l + 1)
                    sp.wait_ge(s_cwhi, l + 1)
                    sp.dma_start(conv_stage[:],
                                 conv_d[ds(l + 1, 1)].rearrange("a p s n -> (a p) s n")).then_inc(s_cw, 16)
                with sp.Fori(1, PAIRS) as p:
                    for m in range(2):
                        sp.wait_ge(s_hi, l * B + p * 2 + (m - 1))
                        sp.wait_ge(s_lo, l * B + p * 2 + (m - 1))
                        load_halo(l, p * 2 + m, m)

            over_layers(sp, layer)

        @block.gpsimd
        def _(pool):
            nc.gpsimd.memset(xin[:], 0.0)
            nc.gpsimd.memset(x_now[:], 0.0)
            nc.gpsimd.memset(halo[:], 0.0).then_inc(s_zero, 1)

            def store_pair(T, b, k):
                for m in range(2):
                    pool.wait_ge(s_x, T * 4 + 2 * m + 2)
                    pool.dma_start(x_d[ds(b + m, 1)].rearrange("a p n -> (a p) n"),
                                   x_now[:, k, m].rearrange("p i j -> p (i j)")).then_inc(s_store[k][m], 16)

            def negate(l):
                pool.wait_ge(s_w, (l + 1) * 16)
                pool.sem_inc(s_past, 1)
                nc.gpsimd.tensor_scalar(wspec[:, :, 0, :], wspec[:, :, 2, :], -1.0, None,
                                        ALU.mult).then_inc(s_neg, 1)

            negate(0)
            with pool.Fori(0, PAIRS // 2) as it:
                for k in range(2):
                    store_pair(it * 2 + k, it * 4 + 2 * k, k)
            with pool.Fori(0, NL - 1) as l:
                negate(l + 1)
                with pool.Fori(0, PAIRS // 2) as it:
                    for k in range(2):
                        store_pair(l * PAIRS + (it * 2 + (k + PAIRS)), it * 4 + 2 * k, k)
            with pool.Fori(0, PAIRS // 2) as it:
                for k in range(2):
                    pool.wait_ge(s_h, it * 2 + k + 1)
                    for u in range(4):
                        pool.dma_start(h_d[ds(it * 4 + (2 * k + u // 2), 1), :,
                                           (u % 2) * HALF:(u % 2 + 1) * HALF].rearrange("a p n -> (a p) n"),
                                       h_now[32 * u:32 * u + 4, k, :]).then_inc(s_hst[k], 16)

            for k in range(2):
                pool.wait_ge(s_hst[k], PAIRS // 2 * 4 * 16)
                for m in range(2):
                    pool.wait_ge(s_store[k][m], NL * PAIRS // 2 * 16)

        @block.tensor
        def _(pe):
            mm = nc.tensor.matmul

            def rows_forward(T):
                pe.wait_ge(s_xt, T * 2 + 2)
                reached(pe, s_ft, T)
                for m in range(2):
                    for h in range(2):
                        z = mm(fxp[64 * m:64 * m + 64, h, :], ex, xt[:, m, 16 * h:16 * h + 16, :],
                               start=True, stop=True)
                z.then_inc(s_fx, 1)

            def columns_forward(T):
                pe.wait_ge(s_ft, T + 1)
                reached(pe, s_spec, T)
                for kyb in range(4):
                    for ri in range(2):
                        for h in range(2):
                            k0 = ri * MODES + 4 * kyb + 2 * h
                            z = mm(ap_[64 * h:64 * h + 64, 64 * kyb:64 * kyb + 64],
                                   ft[:, k0:k0 + 2, :].rearrange("p a c -> p (a c)"), ey[:, ri, :],
                                   start=(ri == 0), stop=(ri == 1))
                z.then_inc(s_fy, 1)

            def project(T, k, first):
                pe.wait_ge(s_xin[k], (T + (2 - k)) * 16)
                for u in range(4):
                    if not (first and u < 2):
                        pe.wait_ge(s_x, T * 4 + (u - 1))
                    mm(acc[u % 2], pw[:], xin[:, k, u // 2, (u % 2) * HALF:(u % 2 + 1) * HALF],
                       start=True, stop=True).then_inc(s_acc, 1)
                    if u == 1 and not first:
                        rows_forward(T - 1)
                if not first:
                    columns_forward(T - 1)

            pe.wait_ge(s_const, 16 * (NCONST - 1))
            pe.wait_ge(s_zero, 1)
            over_pairs(pe, project)
            rows_forward(PAIRS - 1)
            columns_forward(PAIRS - 1)

            def mix(l):
                pe.wait_ge(s_spec, (l + 1) * PAIRS)
                pe.wait_ge(s_neg, l + 1)
                pe.wait_ge(s_x, (l + 1) * (4 * PAIRS))
                pe.sem_inc(s_past, 1)
                for kyb in range(4):
                    for n in range(MODES):
                        for q in range(4):
                            kx = (n + 4 * q) % MODES
                            col = (kyb * MODES + kx) * 64
                            g = slice(32 * q, 32 * q + 32)
                            for ri in range(2):
                                z = mm(zp[g, col:col + 64], spec[g, kyb, 2 * kx + ri, :],
                                       wspec[g, kyb * MODES + kx, 1 - ri:3 - ri, :],
                                       start=(ri == 0), stop=(ri == 1))
                    z.then_inc(s_mix, 1)

            def columns_back(l, p):
                for m in range(4):
                    z = mm(vp[:, 256 * m:256 * m + 256], iy[:, m, :],
                           zt[:, :, ds(p * 2, 2), :].rearrange("p k b o -> p k (b o)"), start=True, stop=True)
                z.then_inc(s_v, 1)

            def conv_image(l, p, k, m):
                T = l * PAIRS + p
                pe.wait_ge(s_hi, T * 2 + m + 1)
                pe.wait_ge(s_lo, T * 2 + m + 1)
                for h in range(2):
                    u = 2 * m + h
                    pe.wait_ge(s_x, T * 4 + (4 * PAIRS + u - 1))
                    first = True
                    for wts, img in ((conv_hi, halo_hi), (conv_lo, halo_hi), (conv_hi, halo_lo)):
                        grid = img[:, m, :].rearrange("p (i j) -> p i j", i=PITCH)
                        for t in range(4):
                            di, dj = t // 2, t % 2
                            mm(acc[u % 2], wts[:, t, :], grid[:, 16 * h + di:16 * h + di + 16, dj:dj + G],
                               start=first, stop=False, skip_group_check=True)
                            first = False
                    if u == 0:
                        pe.wait_ge(s_vt, T + 1)
                    for ih in range(8):
                        for s in range(2):
                            z = mm(acc[u % 2][64 * s:64 * s + 64, 64 * ih:64 * ih + 64],
                                   vt[:, k, 8 * h + ih].rearrange("p r o -> p (r o)"), ix[:, s, m, :],
                                   start=False, stop=True, skip_group_check=True)
                    z.then_inc(s_acc, 1)

            def head_hidden(p, k):
                for u in range(4):
                    pe.wait_ge(s_x, p * 4 + (NL * PAIRS * 4 + u + 1))
                    if u >= 2:
                        pe.wait_ge(s_hid, p * 4 + (u - 1))
                    mm(fxp[:, u % 2, :], q1w[:], x_now[:, k, u // 2, 16 * (u % 2):16 * (u % 2) + 16, 0:G],
                       start=True, stop=True).then_inc(s_h1, 1)

            def head_out(p):
                pe.wait_ge(s_hid, p * 4 + 4)
                reached(pe, s_h, p)
                for u in range(4):
                    z = mm(yp[32 * u:32 * u + 4, :], q2w[:], hid[:, u, :], start=True, stop=True)
                z.then_inc(s_y, 1)

            def layer(l, last):
                mix(l)
                pe.wait_ge(s_zt, l * 4 + 4)
                pe.wait_ge(s_cwhi, l + 1)
                pe.wait_ge(s_cwlo, l + 1)

                def pair(p, k, first):
                    columns_back(l, p)
                    conv_image(l, p, k, 0)
                    if last and not first:
                        head_hidden(p - 1, 1 - k)
                    elif not first:
                        rows_forward(l * PAIRS + p + (PAIRS - 1))
                    conv_image(l, p, k, 1)
                    if last and not first:
                        head_out(p - 1)
                    elif not first:
                        columns_forward(l * PAIRS + p + (PAIRS - 1))

                over_pairs(pe, pair)
                if last:
                    head_hidden(PAIRS - 1, 1)
                    head_out(PAIRS - 1)
                else:
                    rows_forward(l * PAIRS + (2 * PAIRS - 1))
                    columns_forward(l * PAIRS + (2 * PAIRS - 1))

            over_layers(pe, layer)

        @block.scalar
        def _(act):
            copy = nc.scalar.activation

            def spectrum(T, b):
                act.wait_ge(s_fy, T + 1)
                copy(spec[:, :, :, ds(b, 2)],
                     ap_.rearrange("p (k b f) -> p k f b", k=4, b=2), ACT.Identity).then_inc(s_spec, 1)

            def project(T, k, first):
                for u in range(4):
                    act.wait_ge(s_acc, T * 4 + u + 1)
                    if u % 2 == 0 and not (first or (isinstance(T, int) and T < 2)):
                        act.wait_ge(s_store[k][u // 2], (T - k) * 8)
                        act.wait_ge(s_xt, T * 2 + (u // 2 - 3))
                    copy(x_now[:, k, u // 2, 16 * (u % 2):16 * (u % 2) + 16, 0:G],
                         acc[u % 2].rearrange("p (i j) -> p i j", j=G), ACT.Identity,
                         bias=pb[:]).then_inc(s_x, 1)
                if not first:
                    spectrum(T - 1, T * 2 - 2)

            act.wait_ge(s_const, 16 * (NCONST - 1))
            act.wait_ge(s_zero, 1)
            over_pairs(act, project)
            spectrum(PAIRS - 1, B - 2)

            def split_hi(T, m):
                act.wait_ge(s_raw[m], (T + 1) * 64)
                act.wait_ge(s_acc, T * 4 + (4 * PAIRS + 2 * m - 2))
                copy(halo_hi[:, m, :], halo[:, m, :], ACT.Identity).then_inc(s_hi, 1)

            def add_bias(T, u):
                act.wait_ge(s_acc, T * 4 + (4 * PAIRS + u + 1))
                copy(biased[:, u % 2, :], acc[u % 2], ACT.Identity, bias=bias_now[:]).then_inc(s_bias, 1)

            def head_bias(p, u):
                act.wait_ge(s_h1, p * 4 + u + 1)
                copy(hbiased[:, u % 2, :], fxp[:, u % 2, :], ACT.Identity, bias=q1b[:]).then_inc(s_h1b, 1)

            def head_read(p, k, early):
                act.wait_ge(s_y, p + 1)
                if not early:
                    act.wait_ge(s_hst[k], (p - k) * 32)
                for u in range(4):
                    z = copy(h_now[32 * u:32 * u + 4, k, :], yp[32 * u:32 * u + 4, :], ACT.Identity,
                             bias=q2b[32 * u:32 * u + 4, :])
                z.then_inc(s_h, 1)

            def layer(l, last):
                act.wait_ge(s_cw, (l + 1) * 16)
                act.wait_ge(s_acc, (l + 1) * (4 * PAIRS))
                copy(conv_hi[:], conv_stage[:], ACT.Identity).then_inc(s_cwhi, 1)
                act.wait_ge(s_cwlo, l + 1)
                split_hi(l * PAIRS, 0)

                def pair(p, k, first, more=True):
                    T = l * PAIRS + p
                    split_hi(T, 1)
                    add_bias(T, 0)
                    add_bias(T, 1)
                    if last and not first:
                        for u in range(4):
                            head_bias(p - 1, u)
                    if more:
                        split_hi(T + 1, 0)
                    add_bias(T, 2)
                    add_bias(T, 3)
                    if last and not first:
                        head_read(p - 1, 1 - k, isinstance(p, int) and p < 3)
                    elif not first:
                        spectrum(T + (PAIRS - 1), p * 2 - 2)

                pair(0, 0, True)
                pair(1, 1, False)
                with act.Fori(1, PAIRS // 2 - 1) as it:
                    pair(it * 2, 0, False)
                    pair(it * 2 + 1, 1, False)
                pair(PAIRS - 2, 0, False)
                pair(PAIRS - 1, 1, False, more=False)
                if last:
                    for u in range(4):
                        head_bias(PAIRS - 1, u)
                    head_read(PAIRS - 1, 1, False)
                else:
                    spectrum(l * PAIRS + (2 * PAIRS - 1), B - 2)

            over_layers(act, layer)

        @block.vector
        def _(dve):
            vec = nc.vector

            def turn_x(T, k, m):
                dve.wait_ge(s_x, T * 4 + 2 * m + 2)
                reached(dve, s_fx, T)
                vec.transpose(xt[:, m], x_now[:, k, m, :, 0:G]).then_inc(s_xt, 1)

            def turn_rows(T):
                dve.wait_ge(s_fx, T + 1)
                reached(dve, s_fy, T)
                vec.transpose(ft[:].rearrange("p k c -> p c k"),
                              fxp.rearrange("p a b -> p (a b)").rearrange("p (i c) -> p c i", c=C)
                              ).then_inc(s_ft, 1)

            def project(T, k, first):
                turn_x(T, k, 0)
                if not first:
                    turn_rows(T - 1)
                turn_x(T, k, 1)

            over_pairs(dve, project)
            turn_rows(PAIRS - 1)

            def split_lo(T, m):
                dve.wait_ge(s_hi, T * 2 + m + 1)
                dve.wait_ge(s_acc, T * 4 + (4 * PAIRS + 2 * m - 2))
                vec.tensor_tensor(halo_lo[:, m, :], halo[:, m, :], halo_hi[:, m, :].bitcast(F32),
                                  ALU.subtract).then_inc(s_lo, 1)

            def leaky(out, src, **kw):
                return vec.scalar_tensor_tensor(out=out, in0=src, scalar=0.01, in1=src, op0=ALU.mult, op1=ALU.max)

            def activate(T, l, last, p, k, u):
                m = u // 2
                dve.wait_ge(s_bias, T * 4 + u + 1)
                if u % 2 == 0:
                    early = isinstance(p, int) and p < 2
                    if not last or early:
                        dve.wait_ge(s_store[k][m], (T + (PAIRS - k)) * 8)
                    else:
                        dve.wait_ge(s_h1, p * 4 + (2 * m - 6))
                leaky(x_now[:, k, m, 16 * (u % 2):16 * (u % 2) + 16, 0:G],
                      biased[:, u % 2, :].rearrange("p (i j) -> p i j", j=G)).then_inc(s_x, 1)

            def head_activate(p, u):
                dve.wait_ge(s_h1b, p * 4 + u + 1)
                reached(dve, s_y, p)
                leaky(hid[:, u, :], hbiased[:, u % 2, :]).then_inc(s_hid, 1)

            dve.wait_ge(s_const, 16 * (NCONST - 1))

            def layer(l, last):
                dve.wait_ge(s_cwhi, l + 1)
                vec.tensor_copy(bias_now[:], conv_bias[:, ds(l, 1)])
                vec.tensor_tensor(conv_lo[:], conv_stage[:], conv_hi[:].bitcast(F32),
                                  ALU.subtract).then_inc(s_cwlo, 1)
                split_lo(l * PAIRS, 0)
                for kyb in range(4):
                    dve.wait_ge(s_mix, l * 4 + kyb + 1)
                    dve.wait_ge(s_acc, (l + 1) * (4 * PAIRS))
                    vec.transpose(zt[:, kyb].rearrange("p b o -> p o b"),
                                  zp[:, 1024 * kyb:1024 * kyb + 1024].rearrange("p (f o) -> p o f", o=C)
                                  ).then_inc(s_zt, 1)

                def pair(p, k, first, more=True):
                    T = l * PAIRS + p
                    split_lo(T, 1)
                    dve.wait_ge(s_v, T + 1)
                    dve.wait_ge(s_acc, T * 4 + (4 * PAIRS - 4))
                    vec.transpose(vt[:, k].rearrange("p h r o -> p (h r) o").rearrange("p y o -> p o y"),
                                  vp.rearrange("p (f o) -> p o f", o=C)).then_inc(s_vt, 1)
                    activate(T, l, last, p, k, 0)
                    activate(T, l, last, p, k, 1)
                    if not last:
                        turn_x(T + PAIRS, k, 0)
                        if not first:
                            turn_rows(T + (PAIRS - 1))
                    elif not first:
                        for u in range(4):
                            head_activate(p - 1, u)
                    if more:
                        split_lo(T + 1, 0)
                    activate(T, l, last, p, k, 2)
                    activate(T, l, last, p, k, 3)
                    if not last:
                        turn_x(T + PAIRS, k, 1)

                pair(0, 0, True)
                pair(1, 1, False)
                with dve.Fori(1, PAIRS // 2 - 1) as it:
                    pair(it * 2, 0, False)
                    pair(it * 2 + 1, 1, False)
                pair(PAIRS - 2, 0, False)
                pair(PAIRS - 1, 1, False, more=False)
                if last:
                    for u in range(4):
                        head_activate(PAIRS - 1, u)
                else:
                    turn_rows(l * PAIRS + (2 * PAIRS - 1))

            over_layers(dve, layer)


NH, NE, D = 4, 4, 16
TOKENS = B * H // 128 * W
NEG = -1e30
TAIL = [("ident", 128), ("w_attn", 128), ("hl", 128), ("hl_b", 1), ("wq", 256), ("wk", 64), ("wvi", 128),
        ("kmask", 4), ("vmask", 4), ("gate", 32), ("gate_b", 16), ("fc1", 128), ("fc1_b", D), ("fc2", 128),
        ("fc2_b", D), ("ln_g", D), ("ln_b", D), ("fnorm_g", D), ("fnorm_b", D), ("fgate", 8), ("fold", 64)]


def build_tail(nc, h_d, tail_d, onehot_d, causal_d, out_d):
    with ExitStack() as ctx:
        def sb(name, shape, dt=F32):
            return ctx.enter_context(nc.sbuf_tensor(name, shape, dt))

        def sem(name):
            return ctx.enter_context(nc.semaphore(name))

        consts = sb("t_consts", [128, sum(n for _, n in TAIL)])
        at, c = 0, {}
        for name, n in TAIL:
            c[name] = consts[:, at:at + n]
            at += n
        ident = c["ident"]

        h_in = sb("t_h_in", [128, 16, 2, G])
        h0 = sb("t_h0", [128, 16, W])
        h1 = sb("t_h1", [128, 16, W])
        z = sb("t_z", [128, 16, W])
        xc = sb("t_xc", [128, 16, W])
        sq = sb("t_sq", [128, 16, W])
        small = sb("t_small", [128, 6, 64])
        zT = sb("t_zT", [128, 8, 128])
        uT = sb("t_uT", [128, 8, 128])
        dif = sb("t_dif", [128, 2, 512])
        ebd = sb("t_ebd", [128, 16, 128])
        ebdT = sb("t_ebdT", [128, 16, 128])
        sxT = sb("t_sxT", [64, B, H])
        lq = sb("t_lq", [128, B, NE, H])
        kr = sb("t_kr", [128, B, NH, H])
        vbd = sb("t_vbd", [128, B, 2, 34])
        sx = sb("t_sx", [128, B, NH * D])
        prob = sb("t_prob", [128, 2, 512])
        probT = sb("t_probT", [128, 2, 512])
        o_all = sb("t_o", [128, B, 4, 34])
        gs = sb("t_gs", [128, B, NH, NE])
        gsel = sb("t_gsel", [128, B, 2, NH])
        qkv = lq
        qT = kr
        psum = ctx.enter_context(nc.psum_tensor("t_psum", [128, 8, 512], F32))
        bank = lambda a, n=1: psum[:, a:a + n, :].rearrange("p a b -> p (a b)")

        s_load = sem("t_load")
        s_const = sem("t_const")
        s_zero = sem("t_zero")
        s_dve = sem("t_dve")
        s_var = sem("t_var")
        s_std = sem("t_std")
        s_norm = sem("t_norm")
        s_turn = sem("t_turn")
        s_turned = sem("t_turned")
        s_u = sem("t_u")
        s_uc = sem("t_uc")
        s_s1 = sem("t_s1")
        s_dif = sem("t_dif_ready")
        s_exp = sem("t_exp")
        s_tr = sem("t_tr")
        s_trc = sem("t_trc")
        s_msg = sem("t_msg")
        s_mm = sem("t_mm")
        s_mc = sem("t_mc")
        s_vc = sem("t_vc")
        s_sc = sem("t_sc")
        s_df = sem("t_df")
        s_pr = sem("t_pr")
        s_pt = sem("t_pt")
        s_pc = sem("t_pc")
        s_av = sem("t_av")
        s_oc = sem("t_oc")
        s_q = sem("t_q")
        s_qt = sem("t_qt")
        s_qc = sem("t_qc")
        s_g = sem("t_g")
        s_gd = sem("t_gd")
        s_ge = sem("t_ge")
        s_mx = sem("t_mx")
        s_fold = sem("t_fold")
        s_f = sem("t_f")
        s_fe = sem("t_fe")
        s_fee = sem("t_fee")
        s_out = sem("t_out")
        s_stored = sem("t_stored")

        block = ctx.enter_context(nc.Block())
        CHUNK = 8

        @block.sync
        def _(sp):
            for b2 in range(2):
                for s in range(2):
                    for r in range(2):
                        rows = slice(64 * b2 + r, 64 * b2 + 64, 2)
                        sp.dma_start(h_in[rows, :, s, :],
                                     h_d[b2:B:2, 2 * s + r, :].rearrange("b (i j) -> i b j", j=G)
                                     ).then_inc(s_load, 16)
            sp.dma_start(consts[:], tail_d).then_inc(s_const, 16)
            sp.dma_start(lq[64:128].rearrange("p b e s -> p b (e s)"), onehot_d).then_inc(s_const, 16)
            sp.dma_start(kr[64:128].rearrange("p b n t -> p b (n t)"), causal_d).then_inc(s_const, 16)
            sp.wait_ge(s_out, 1)
            for b2 in range(2):
                sp.dma_start(out_d[b2:B:2].rearrange("b y x -> y b x"),
                             h1[64 * b2:64 * b2 + 64]).then_inc(s_stored, 16)
            sp.wait_ge(s_stored, 32)

        @block.gpsimd
        def _(pool):
            nc.gpsimd.memset(ebd[:], 0.0).then_inc(s_zero, 1)

        @block.tensor
        def _(pe):
            mm = nc.tensor.matmul

            def turn(src, n, free=None):
                pe.wait_ge(s_norm, n)
                if free:
                    pe.wait_ge(*free)
                for k in range(8):
                    t = nc.tensor.transpose(bank(0, 2)[:, 128 * k:128 * k + 128],
                                            src[:, 2 * k:2 * k + 2, :].rearrange("p a b -> p (a b)"), ident)
                t.then_inc(s_turn, 1)
                pe.wait_ge(s_turned, n)

            pe.wait_ge(s_const, 48)
            turn(z, 1)
            for h in range(2):
                t = mm(bank(2 + h), c["w_attn"], zT[:, 4 * h:4 * h + 4, :], start=True, stop=True)
            t.then_inc(s_u, 1)
            pe.wait_ge(s_uc, 1)
            for bp in range(16):
                for b2 in range(2):
                    g = slice(64 * (bp % 2), 64 * (bp % 2) + 64)
                    k, col = bp // 2, slice(64 * b2, 64 * b2 + 64)
                    t = mm(bank(4 + bp % 2)[64 * b2:64 * b2 + 64, 64 * k:64 * k + 64], uT[g, k, col], zT[g, k, col],
                           start=True, stop=True)
            t.then_inc(s_s1, 1)
            pe.wait_ge(s_exp, 1)
            for bp in range(16):
                t = nc.tensor.transpose(bank(0, 4)[:, 128 * bp:128 * bp + 128], ebd[:, bp, :], ident)
            t.then_inc(s_tr, 1)
            pe.wait_ge(s_trc, 1)
            for bp in range(16):
                t = mm(bank(6, 2)[:, 64 * bp:64 * bp + 64], ebdT[:, bp, :], z[:, bp, :], start=True, stop=True)
            t.then_inc(s_msg, 1)

            turn(z, 2)
            for k in range(4):
                mm(bank(2 + k)[0:64, :], c["hl"][:, 64 * (k // 2):64 * (k // 2) + 64],
                   zT[:, 4 * (k % 2):4 * (k % 2) + 4, :], start=True, stop=True).then_inc(s_mm, 1)
            pe.wait_ge(s_mc, 4)
            toks = lambda k: sxT[:, CHUNK * k:CHUNK * k + CHUNK, :]
            for k in range(4):
                for e in range(NE):
                    n = 4 * k + e
                    if n >= 4:
                        pe.wait_ge(s_mc, n + 1)
                    mm(bank((6 + e) % 8)[0:64, :], c["wq"][0:64, 64 * e:64 * e + 64], toks(k),
                       start=True, stop=True).then_inc(s_mm, 1)
                mm(bank(2 + k)[0:64, :], c["wk"][0:64, :], toks(k), start=True, stop=True).then_inc(s_mm, 1)
            pe.wait_ge(s_vc, 4)
            for k in range(8):
                if k >= 4:
                    pe.wait_ge(s_vc, k + 1)
                for i in range(4):
                    img = 4 * k + i
                    for dup in range(2):
                        t = mm(bank(2 + k % 4)[64 * dup:64 * dup + 64, 128 * i:128 * i + 128],
                               sxT[:, img, :], c["wvi"][0:64, :], start=True, stop=True)
                t.then_inc(s_mm, 1)
            pe.wait_ge(s_mc, 20)
            pe.wait_ge(s_vc, 12)
            for i in range(B + 2):
                if i < B:
                    if i >= 2:
                        pe.wait_ge(s_df, i - 1)
                    for eh in range(2):
                        t = mm(bank(i % 2)[:, 256 * eh:256 * eh + 256],
                               lq[:, i, 2 * eh:2 * eh + 2, :].rearrange("p a b -> p (a b)"),
                               kr[:, i].rearrange("p a b -> p (a b)"), start=True, stop=True)
                    t.then_inc(s_sc, 1)
                if 1 <= i <= B:
                    pe.wait_ge(s_pr, i)
                    if i >= 3:
                        pe.wait_ge(s_pc, i - 2)
                    for k in range(4):
                        t = nc.tensor.transpose(bank(2 + (i - 1) % 2)[:, 128 * k:128 * k + 128],
                                                prob[:, (i - 1) % 2, 128 * k:128 * k + 128], ident)
                    t.then_inc(s_pt, 1)
                if i >= 2:
                    j = i - 2
                    pe.wait_ge(s_pc, j + 1)
                    if j >= 2:
                        pe.wait_ge(s_oc, j - 1)
                    for k in range(4):
                        t = mm(bank(4 + j % 2)[:, 34 * k:34 * k + 34], probT[:, j % 2, 128 * k:128 * k + 128],
                               vbd[:, j, k % 2, :], start=True, stop=True)
                    t.then_inc(s_av, 1)

            pe.wait_ge(s_q, 1)
            for k in range(8):
                if k >= 4:
                    pe.wait_ge(s_qc, k - 3)
                for i in range(4):
                    t = nc.tensor.transpose(bank(k % 4)[:, 128 * i:128 * i + 128],
                                            qkv[:, 4 * k + i, 0:2, :].rearrange("p a b -> p (a b)"), ident)
                t.then_inc(s_qt, 1)
            pe.wait_ge(s_qc, 8)
            for img in range(B):
                for dup in range(2):
                    for e2 in range(2):
                        t = mm(bank(6)[64 * dup:64 * dup + 64, 16 * img:16 * img + 16],
                               qT[:, img, e2, :], c["gate"][:, 16 * e2:16 * e2 + 16],
                               start=(e2 == 0), stop=(e2 == 1))
            t.then_inc(s_g, 1)
            pe.wait_ge(s_mx, 1)
            for k in range(2):
                for b2 in range(2):
                    t = mm(bank(4 + k)[64 * b2:64 * b2 + 64, :], c["fold"],
                           o_all[:].rearrange("p b a n -> p (b a n)")[:, 0:B * 64]
                           .rearrange("p (k c b n) -> p k c b n", k=2, b=2, n=64)[:, k, :, b2, :],
                           start=True, stop=True)
            t.then_inc(s_fold, 1)

            for n, (w, width) in enumerate((("fc1", 128), ("fc2", 128), ("fgate", 8))):
                turn(z if n != 1 else xc, 3 + n)
                for k in range(8):
                    t = mm(bank(2, 2)[:, width * k:width * k + width], zT[:, k, :], c[w], start=True, stop=True)
                t.then_inc(s_f, 1)

        @block.scalar
        def _(act):
            copy = nc.scalar.activation

            def root(n, m):
                act.wait_ge(s_var, n)
                copy(small[:, 3, 0:m], small[:, 2, 0:m], ACT.Sqrt).then_inc(s_std, 1)

            def turned(n):
                act.wait_ge(s_turn, n)
                copy(zT[:].rearrange("p a b -> p (a b)"), bank(0, 2), ACT.Identity).then_inc(s_turned, 1)

            act.wait_ge(s_const, 48)
            root(1, 16)
            turned(1)
            act.wait_ge(s_dif, 1)
            act.wait_ge(s_zero, 1)
            for b2 in range(2):
                g = slice(64 * b2, 64 * b2 + 64)
                t = copy(ebd[g, :, g], dif[g].rearrange("p a (b m) -> p (a b) m", m=H), ACT.Exp,
                         scale=float(W) ** -0.5)
            t.then_inc(s_exp, 1)
            act.wait_ge(s_tr, 1)
            copy(ebdT[:].rearrange("p a b -> p (a b)"), bank(0, 4), ACT.Identity).then_inc(s_trc, 1)
            root(2, 16)
            turned(2)
            for k in range(4):
                act.wait_ge(s_mm, k + 1)
                copy(sxT[:, CHUNK * k:CHUNK * k + CHUNK, :],
                     bank(2 + k)[0:64, :].rearrange("p (b s) -> p b s", s=H), ACT.Identity,
                     bias=c["hl_b"][0:64, :]).then_inc(s_mc, 1)
            for k in range(4):
                for e in range(NE):
                    act.wait_ge(s_mm, 4 + 5 * k + e + 1)
                    copy(lq[0:64, CHUNK * k:CHUNK * k + CHUNK, e, :],
                         bank((6 + e) % 8)[0:64, :].rearrange("p (b s) -> p b s", s=H),
                         ACT.Identity).then_inc(s_mc, 1)
            for i in range(B + 1):
                if i < B:
                    act.wait_ge(s_df, i + 1)
                    if i >= 2:
                        act.wait_ge(s_pt, i - 1)
                    copy(prob[:, i % 2, :], dif[:, i % 2, :], ACT.Exp, scale=float(D) ** 0.5).then_inc(s_pr, 1)
                if i >= 1:
                    j = i - 1
                    act.wait_ge(s_pt, j + 1)
                    if j >= 2:
                        act.wait_ge(s_av, j - 1)
                    copy(probT[:, j % 2, :], bank(2 + j % 2), ACT.Identity).then_inc(s_pc, 1)
            for k in range(8):
                act.wait_ge(s_qt, k + 1)
                copy(qT[:, 4 * k:4 * k + 4, 0:2, :].rearrange("p b a s -> p b (a s)"),
                     bank(k % 4).rearrange("p (b n) -> p b n", b=4), ACT.Identity).then_inc(s_qc, 1)
            act.wait_ge(s_gd, 1)
            copy(gs[:], gs[:], ACT.Exp).then_inc(s_ge, 1)
            root(3, 64)
            turned(3)
            turned(4)
            root(4, 64)
            turned(5)
            act.wait_ge(s_fe, 1)
            copy(gs[:, 0:4].rearrange("p a b c -> p (a b c)"), gs[:, 0:4].rearrange("p a b c -> p (a b c)"),
                 ACT.Exp).then_inc(s_fee, 1)

        @block.vector
        def _(dve):
            vec = nc.vector
            chain = [0]

            def link(ins):
                chain[0] += 1
                ins.then_inc(s_dve, 1)
                dve.wait_ge(s_dve, chain[0])

            def wide(a, n):
                return a.unsqueeze(2).to_broadcast([128, a.shape[1], n])

            def normalise(src, out, n, m, eps, count, last=True):
                total, mean, var, root, inv = (small[:, k, 0:m] for k in range(5))
                cen = xc[:].rearrange("p a b -> p (a b)").rearrange("p (m n) -> p m n", n=n)
                sqv = sq[:].rearrange("p a b -> p (a b)").rearrange("p (m n) -> p m n", n=n)
                link(vec.tensor_reduce(total, src, AX.X, ALU.add))
                link(vec.tensor_scalar(mean, total, 1.0 / n, None, ALU.mult))
                link(vec.tensor_tensor(cen, src, wide(mean, n), ALU.subtract))
                link(vec.tensor_tensor(sqv, cen, cen, ALU.mult))
                link(vec.tensor_reduce(total, sqv, AX.X, ALU.add))
                vec.tensor_scalar(var, total, 1.0 / n, eps, ALU.mult, ALU.add).then_inc(s_var, 1)
                dve.wait_ge(s_std, count)
                link(vec.reciprocal(inv, root))
                ins = vec.tensor_tensor(out, cen, wide(inv, n), ALU.mult)
                if last:
                    ins.then_inc(s_norm, 1)
                link_free(ins) if not last else None

            def link_free(ins):
                link(ins)

            dve.wait_ge(s_load, 8 * 16)
            link(vec.tensor_copy(h0[:].rearrange("p b (j s) -> p b s j", s=2), h_in[:]))
            normalise(h0[:], z[:], W, 16, 1e-5, 1)
            dve.wait_ge(s_u, 1)
            vec.tensor_copy(uT[:].rearrange("p a b -> p (a b)"), bank(2, 2)).then_inc(s_uc, 1)
            dve.wait_ge(s_s1, 1)
            for g in range(2):
                scores = bank(4 + g).rearrange("p (c m) -> p c m", m=H)
                link(vec.tensor_reduce(small[:, 5, 8 * g:8 * g + 8], scores, AX.X, ALU.max))
                t = vec.tensor_tensor(dif[:].rearrange("p a (b m) -> p (a b) m", m=H)[:, g:16:2, :], scores,
                                      wide(small[:, 5, 8 * g:8 * g + 8], H), ALU.subtract)
            t.then_inc(s_dif, 1)
            dve.wait_ge(s_exp, 1)
            link(vec.tensor_reduce(small[:, 0, 0:16], ebd[:], AX.X, ALU.add))
            link(vec.reciprocal(small[:, 1, 0:16], small[:, 0, 0:16]))
            dve.wait_ge(s_msg, 1)
            link(vec.tensor_tensor(sq[:], bank(6, 2).rearrange("p (b m) -> p b m", m=W),
                                   wide(small[:, 1, 0:16], W), ALU.mult))
            link(vec.tensor_tensor(h1[:], h0[:], sq[:], ALU.add))
            normalise(h1[:], z[:], W, 16, 1e-5, 2)

            dve.wait_ge(s_const, 48)
            for k in range(4):
                dve.wait_ge(s_mm, 4 + 5 * k + 5)
                keys = bank(2 + k)[0:64, :].rearrange("p (b t) -> p b t", t=H)
                for n in range(NH):
                    t = vec.tensor_scalar(kr[0:64, CHUNK * k:CHUNK * k + CHUNK, n, :], keys,
                                          c["kmask"][0:64, n:n + 1], None, ALU.mult)
                t.then_inc(s_vc, 1)
            for k in range(2):
                vec.tensor_copy(vbd[:, :, k, 32:34], c["vmask"][:, 0:2].unsqueeze(1).to_broadcast([128, B, 2]))
            for k in range(8):
                dve.wait_ge(s_mm, 24 + k + 1)
                both = bank(2 + k % 4).rearrange("p (b n) -> p b n", b=4)
                for nl in range(2):
                    vec.tensor_scalar(vbd[:, 4 * k:4 * k + 4, :, 16 * nl:16 * nl + 16],
                                      both[:, :, 0:64].rearrange("p b (h l d) -> p b h l d", h=2, l=2)[:, :, :, nl, :],
                                      c["vmask"][:, nl:nl + 1], None, ALU.mult)
                vec.tensor_copy(sx[:, 4 * k:4 * k + 4, :], both[:, :, 64:128]).then_inc(s_vc, 1)

            for i in range(B + 2):
                if i < B:
                    dve.wait_ge(s_sc, i + 1)
                    s4 = bank(i % 2).rearrange("p (a t) -> p a t", t=H)
                    link(vec.tensor_reduce(small[:, i % 2, 0:8], s4, AX.X, ALU.max))
                    if i >= 2:
                        dve.wait_ge(s_pr, i - 1)
                    vec.tensor_tensor(dif[:, i % 2, :].rearrange("p (a t) -> p a t", t=H), s4,
                                      wide(small[:, i % 2, 0:8], H), ALU.subtract).then_inc(s_df, 1)
                if i >= 2:
                    j = i - 2
                    dve.wait_ge(s_av, j + 1)
                    vec.tensor_copy(o_all[:, j].rearrange("p a n -> p (a n)"),
                                    bank(4 + j % 2)[:, 0:136]).then_inc(s_oc, 1)
            dve.wait_ge(s_oc, B)
            den = ebd[:].rearrange("p a b -> p (a b)")[:, 0:256]
            link(vec.reciprocal(den.rearrange("p (a n) -> p a n", n=2),
                                o_all[:].rearrange("p b a n -> p (b a) n")[:, :, 32:34]))
            den4 = den.rearrange("p (a n) -> p a n", n=2)
            for img in range(0, B, 8):
                nl = 2
                for l2 in range(nl):
                    o3 = o_all[:, img:img + 8].rearrange("p b a n -> p (b a) n")[:, :, 16 * l2:16 * l2 + 16]
                    dst = qkv[:, img:img + 8, 0:2, :].rearrange("p b e (h l d) -> p b (e h) l d", h=2, l=2)[:, :, :, l2, :]
                    t = vec.tensor_tensor(dst, o3.rearrange("p (b a) d -> p b a d", a=4),
                                          den4[:, 4 * img:4 * img + 32, l2].rearrange("p (b a) -> p b a", a=4)
                                          .unsqueeze(3).to_broadcast([128, 8, 4, D]), ALU.mult)
            link(t)
            q3 = qkv[:, :, 0:2, :]
            for e in range(2):
                t = vec.scalar_tensor_tensor(out=qkv[:, :, e, :], in0=sx[:], scalar=0.0, in1=qkv[:, :, e, :],
                                             op0=ALU.not_equal, op1=ALU.mult)
            t.then_inc(s_q, 1)
            resid = c["wk"]
            for n in range(NH):
                img = (n // 2 % 2) * 16 + (n // 4) * 2 + n % 2
                t = vec.tensor_copy(resid[:, D * n:D * n + D], sx[:, img, D * n:D * n + D])

            dve.wait_ge(s_g, 1)
            gl = gs[:].rearrange("p b n e -> p b (n e)")
            link(vec.tensor_tensor(gl, bank(6).rearrange("p (b n) -> p b n", b=B),
                                   c["gate_b"].unsqueeze(1).to_broadcast([128, B, 16]), ALU.add))
            g3 = gs[:].rearrange("p b n e -> p (b n) e")
            gm = ebd[:].rearrange("p a b -> p (a b)")[:, 256:384]
            link(vec.tensor_reduce(gm, g3, AX.X, ALU.max))
            vec.tensor_tensor(g3, g3, wide(gm, NE), ALU.subtract).then_inc(s_gd, 1)
            dve.wait_ge(s_ge, 1)
            link(vec.tensor_reduce(gm, g3, AX.X, ALU.add))
            link(vec.reciprocal(gm, gm))
            link(vec.tensor_tensor(g3, g3, wide(gm, NE), ALU.mult))
            for e2 in range(2):
                g = slice(64 * e2, 64 * e2 + 64)
                for eh in range(2):
                    t = vec.tensor_copy(gsel[g, :, eh, :], gs[g, :, :, 2 * eh + e2])
            link(t)
            for eh in range(2):
                q4 = qkv[:, :, eh, :].rearrange("p b (n d) -> p b n d", d=D)
                t = vec.tensor_tensor(q4, q4, gsel[:, :, eh, :].unsqueeze(3).to_broadcast([128, B, NH, D]), ALU.mult)
            link(t)
            mixed = o_all[:].rearrange("p b a n -> p (b a n)")[:, 0:B * 64].rearrange("p (b n) -> p b n", n=64)
            vec.tensor_tensor(mixed, qkv[:, :, 0, :], qkv[:, :, 1, :], ALU.add).then_inc(s_mx, 1)

            dve.wait_ge(s_fold, 1)
            y = h_in[:].rearrange("p b s j -> p b (s j)")
            for k in range(2):
                t = vec.tensor_tensor(y[:, k:16:2, :], bank(4 + k).rearrange("p (c n) -> p c n", n=64),
                                      resid.unsqueeze(1).to_broadcast([128, 8, 64]), ALU.add)
            link(t)

            rows = lambda a: a.rearrange("p b (n d) -> p (b n) d", d=D)
            vecs = lambda name: c[name].unsqueeze(1).to_broadcast([128, 64, D])
            fx = rows(z[:])
            t3 = rows(sq[:])
            ffp = bank(2, 2).rearrange("p (m d) -> p m d", d=D)
            normalise(rows(y), fx, D, 64, 1e-8, 3, last=False)
            link(vec.tensor_tensor(fx, fx, vecs("ln_g"), ALU.mult))
            vec.tensor_tensor(fx, fx, vecs("ln_b"), ALU.add).then_inc(s_norm, 1)

            dve.wait_ge(s_f, 1)
            link(vec.tensor_tensor(t3, ffp, vecs("fc1_b"), ALU.add))
            link(vec.scalar_tensor_tensor(out=t3, in0=fx, scalar=0.0, in1=t3, op0=ALU.not_equal, op1=ALU.mult))
            vec.tensor_scalar(rows(xc[:]), t3, 0.0, None, ALU.max).then_inc(s_norm, 1)
            dve.wait_ge(s_f, 2)
            link(vec.tensor_tensor(t3, ffp, vecs("fc2_b"), ALU.add))
            link(vec.scalar_tensor_tensor(out=t3, in0=fx, scalar=0.0, in1=t3, op0=ALU.not_equal, op1=ALU.mult))
            hy = rows(h0[:])
            link(vec.tensor_tensor(hy, t3, fx, ALU.add))
            normalise(hy, fx, D, 64, 1e-8, 4, last=False)
            link(vec.tensor_tensor(fx, fx, vecs("fnorm_g"), ALU.mult))
            vec.tensor_tensor(fx, fx, vecs("fnorm_b"), ALU.add).then_inc(s_norm, 1)

            dve.wait_ge(s_f, 3)
            fg = gs[:, 0:4].rearrange("p a b c -> p (a b c)")
            fl = fg.rearrange("p (m n) -> p m n", n=NH)
            lg = bank(2, 2)[:, 0:64].rearrange("p (m n) -> p m n", n=NH)
            fm = small[:, 0, 0:16]
            link(vec.tensor_reduce(fm, lg, AX.X, ALU.max))
            vec.tensor_tensor(fl, lg, wide(fm, NH), ALU.subtract).then_inc(s_fe, 1)
            dve.wait_ge(s_fee, 1)
            link(vec.tensor_reduce(fm, fl, AX.X, ALU.add))
            link(vec.reciprocal(fm, fm))
            link(vec.tensor_tensor(fl, fl, wide(fm, NH), ALU.mult))
            link(vec.tensor_tensor(fx, fx, wide(fg, D), ALU.mult))
            vec.tensor_tensor(h1[:], h1[:], z[:], ALU.add).then_inc(s_out, 1)


def tail_inputs(t):
    t = {k: np.asarray(v) for k, v in t.items()}

    def diag(w, n, rows=128):
        a, b = w.shape
        out = np.zeros((rows, n * b), np.float32)
        for k in range(n):
            out[a * k:a * k + a, b * k:b * k + b] = w
        return out

    def heads(ws, rows=128):
        a, b = ws[0].shape
        out = np.zeros((rows, len(ws) * b), np.float32)
        for k, w in enumerate(ws):
            out[a * k:a * k + a, b * k:b * k + b] = w
        return out

    p = {}
    p["ident"] = np.eye(128, dtype=np.float32)
    p["w_attn"] = diag(t["L0_attn_W"], 2)
    p["hl"] = diag(t["L0_ffn_hl_w"].reshape(64, 64).T, 2)
    hl_b = np.zeros((128, 1), np.float32)
    hl_b[0:64, 0] = t["L0_ffn_hl_b"].reshape(64)
    p["hl_b"] = hl_b
    wq = t["L0_ffn_wq"]
    p["wq"] = np.concatenate([heads([wq[n, e].T for n in range(NH)]) for e in range(NE)], axis=1)
    p["wk"] = heads([w.T for w in t["L0_ffn_wk"]])
    eye64 = np.zeros((128, 64), np.float32)
    eye64[0:64] = np.eye(64)
    p["wvi"] = np.concatenate([heads([w.T for w in t["L0_ffn_wv"]]), eye64], axis=1)
    kmask = np.zeros((128, 4), np.float32)
    for n in range(NH):
        kmask[D * n:D * n + D, n] = 1
    p["kmask"] = kmask
    vmask = np.zeros((128, 4), np.float32)
    vmask[0:64, 0] = 1
    vmask[64:128, 1] = 1
    p["vmask"] = vmask
    gw = t["L0_ffn_gate_w"].reshape(NH, NE, 2, 2, D)
    gate = np.zeros((2, NH, D, 2, NH, NE), np.float32)
    for n in range(NH):
        gate[:, n, :, :, n, :] = gw[n].transpose(1, 3, 2, 0)
    p["gate"] = gate.reshape(128, 32)
    row = lambda a: np.tile(a.reshape(1, -1), (128, 1))
    p["gate_b"] = row(t["L0_ffn_gate_b"])
    p["fc1"] = diag(t["L0_ffn_fc1_w"].T, 8)
    p["fc2"] = diag(t["L0_ffn_fc2_w"].T, 8)
    p["fgate"] = diag(t["L0_ffn_fgate_w"].T, 2)
    for a in ("fc1_b", "fc2_b", "ln_g", "ln_b", "fnorm_g", "fnorm_b"):
        p[a] = row(t["L0_ffn_" + a])
    p["fold"] = np.tile(np.eye(64, dtype=np.float32), (2, 1))
    onehot = np.tile(np.eye(64, dtype=np.float32)[:, None, :], (1, B, NE)).reshape(64, B, NE * H)
    causal = np.where(np.tri(H, dtype=bool), 0.0, NEG).astype(np.float32)
    causal = np.tile(causal[:, None, :], (1, B, NH)).reshape(64, B, NH * H)
    return {"tail": np.concatenate([p[n] for n, _ in TAIL], axis=1), "onehot": onehot, "causal": causal}


def tower_inputs(t):
    x = np.ascontiguousarray(t["x"])
    grid = np.ascontiguousarray(t["L0_tok_input_grid"])
    xin = np.empty((2, 2, 5, B, G, G), np.float32)
    xin[:, :, 0:2] = grid.reshape(G, 2, G, 2, 2).transpose(3, 1, 4, 0, 2)[:, :, :, None]
    xin[:, :, 2:5] = x.reshape(B, G, 2, G, 2, 3).transpose(4, 2, 5, 0, 1, 3)

    def per_pixel(w, rows=128):
        n, m = w.shape
        out = np.zeros((rows, 4 * m), np.float32)
        for g in range(4):
            out[n * g:n * g + n, m * g:m * g + m] = w
        return out

    conv_w = np.asarray(t["L0_tok_conv_w"])
    conv = np.zeros((NL, 2, 2, C, 2, 2, 2, 2, C), np.float32)
    for di in range(2):
        for dj in range(2):
            for r1 in range(2):
                for s1 in range(2):
                    for r in range(2):
                        for s in range(2):
                            ky, kx = 2 * di + r1 - r, 2 * dj + s1 - s
                            if 0 <= ky < 3 and 0 <= kx < 3:
                                conv[:, s1, r1, :, di, dj, s, r, :] = conv_w[:, :, :, ky, kx].transpose(0, 2, 1)
    spec = np.stack([np.asarray(t["L0_tok_spec_wr"]), np.asarray(t["L0_tok_spec_wi"])])
    spec = spec.reshape(2, NL, C, C, MODES, 4, 4).transpose(1, 6, 2, 5, 4, 0, 3)
    four = lambda b: np.tile(np.asarray(b).reshape(-1), 4).reshape(128, 1)
    return {
        "xin": xin.reshape(XIN, B, G * G),
        "pw": per_pixel(np.asarray(t["L0_tok_P_w"])),
        "pb": four(t["L0_tok_P_b"]),
        "dft": dft_constants(),
        "spec": np.ascontiguousarray(spec).reshape(NL, 128, 4 * MODES, 2, C),
        "conv": conv.reshape(NL, 128, 4, 128),
        "convb": np.ascontiguousarray(np.tile(np.asarray(t["L0_tok_conv_b"]), (1, 4)).T),
        "q1w": per_pixel(np.asarray(t["L0_tok_Q1_w"])),
        "q1b": four(t["L0_tok_Q1_b"]),
        "q2w": per_pixel(np.asarray(t["L0_tok_Q2_w"])),
        "q2b": np.tile(np.asarray(t["L0_tok_Q2_b"]).reshape(-1), 128).reshape(128, 1),
    }


def kernel(**inputs):
    import concourse.bacc as bacc
    from concourse.bass_utils import run_bass_kernel_spmd

    nc = bacc.Bacc("TRN2", target_bir_lowering=False, num_devices=1)
    laid = {**tower_inputs(inputs), **tail_inputs(inputs)}
    arrays, args = {}, []
    for name, a in laid.items():
        arrays[f"in_{name}"] = np.ascontiguousarray(a)
        args.append(nc.dram_tensor(f"in_{name}", a.shape, mybir.dt.from_np(a.dtype), kind="ExternalInput").ap())
    args.append(nc.dram_tensor("out", (B, H, W), F32, kind="ExternalOutput").ap())
    build(nc, *args)
    r = run_bass_kernel_spmd(nc, [arrays], core_ids=[0])
    return r.results[0]["out"]
```

```python
from contextlib import ExitStack

import numpy as np

import concourse.bass as bass
from concourse import mybir

F32 = mybir.dt.float32
F32R = mybir.dt.float32r
ALU = mybir.AluOpType
ACT = mybir.ActivationFunctionType
AX = mybir.AxisListType
ds = bass.ds

B, H, W = 32, 64, 64
C = 32
NL = 4
MODES = 16
G = 32
PITCH = G + 1
ROW = 2 * PITCH
AREA = PITCH * ROW
PAIRS = B // 2
HALF = G * G // 2
XIN = 20


def dft_constants():
    th = 2 * np.pi / H
    ex = np.zeros((2, 2, G, 2, 2, MODES))
    ey = np.zeros((2, 2, G, 2, 2, MODES, 2))
    iy = np.zeros((4, MODES, 2, 2, 2, 4, 16, 2))
    ix = np.zeros((4, 2, 2, 4, 2, 2, 2, 2, G))
    k, g = np.arange(MODES), np.arange(G)
    for s in range(2):
        a = th * np.outer(2 * g + s, k)
        for r in range(2):
            ex[s, r, :, r, 0] = np.cos(a)
            ex[s, r, :, r, 1] = -np.sin(a)
    for r in range(2):
        a = th * np.outer(2 * g + r, k)
        for b in range(2):
            ey[b, r, :, 0, b, :, 0] = np.cos(a)
            ey[b, r, :, 0, b, :, 1] = -np.sin(a)
            ey[b, r, :, 1, b, :, 0] = np.sin(a)
            ey[b, r, :, 1, b, :, 1] = np.cos(a)
    ih = np.arange(16)
    for q in range(4):
        for il in range(2):
            for r in range(2):
                a = th * np.outer(k, 4 * ih + 2 * il + r)
                iy[q, :, 0, 0, il, q, :, r] = np.cos(a)
                iy[q, :, 1, 0, il, q, :, r] = -np.sin(a)
                iy[q, :, 0, 1, il, q, :, r] = np.sin(a)
                iy[q, :, 1, 1, il, q, :, r] = np.cos(a)
        for kyb in range(4):
            ky = 4 * q + kyb
            w = (1.0 if ky == 0 else 2.0) / (H * W)
            for s in range(2):
                a = th * ky * (2 * g + s)
                for b in range(2):
                    for il in range(2):
                        ix[q, 0, il, kyb, b, s, il, b] = w * np.cos(a)
                        ix[q, 1, il, kyb, b, s, il, b] = -w * np.sin(a)
    parts = [ex.reshape(128, 64), ey.reshape(128, 128), iy.reshape(128, 512), ix.reshape(128, 256)]
    return np.concatenate(parts, axis=1).astype(np.float32)


def build(nc, xin_d, pw_d, pb_d, dft_d, spec_d, conv_d, convb_d, q1w_d, q1b_d, q2w_d, q2b_d, tail_d, onehot_d, causal_d, out_d):
    x_d = nc.dram_tensor("activations", [PAIRS, 128, G * ROW], F32, kind="Internal").ap()
    h_d = nc.dram_tensor("tower_out", [PAIRS, 4, 2 * G * G], F32, kind="Internal").ap()

    build_tower(nc, xin_d, pw_d, pb_d, dft_d, spec_d, conv_d, convb_d, q1w_d, q1b_d, q2w_d, q2b_d, x_d, h_d)
    build_tail(nc, h_d, tail_d, onehot_d, causal_d, out_d)


def build_tower(nc, xin_d, pw_d, pb_d, dft_d, spec_d, conv_d, convb_d, q1w_d, q1b_d, q2w_d, q2b_d, x_d, h_d):
    with ExitStack() as ctx:
        def sb(name, shape, dt=F32):
            return ctx.enter_context(nc.sbuf_tensor(name, shape, dt))

        def sem(name):
            return ctx.enter_context(nc.semaphore(name))

        dft = sb("dft", [128, 960])
        ex = dft[:, 0:64]
        ey = dft[:, 64:192].rearrange("p (a n) -> p a n", a=2)
        iy = dft[:, 192:704].rearrange("p (m n) -> p m n", m=4)
        ix = dft[:, 704:960].rearrange("p (s n) -> p s n", s=2)
        pw = sb("pw", [128, 128])
        pb = sb("pb", [128, 1])
        q1w = sb("q1w", [128, 128])
        q1b = sb("q1b", [128, 1])
        q2w = sb("q2w", [128, 4])
        q2b = sb("q2b", [128, 1])
        conv_bias = sb("conv_bias", [128, NL])
        bias_now = sb("bias_now", [128, 1])
        conv_stage = sb("conv_stage", [128, 4, 128])
        conv_hi = sb("conv_hi", [128, 4, 128], F32R)
        conv_lo = sb("conv_lo", [128, 4, 128], F32R)
        shared = sb("shared", [128, 4 * B * C])
        xin = shared[:].rearrange("p (k m n) -> p k m n", k=2, m=2)
        x_now = sb("x_now", [128, 2, 2 * G, PITCH])
        halo = sb("halo", [128, AREA])
        halo_hi = sb("halo_hi", [128, 2, AREA], F32R)
        halo_lo = sb("halo_lo", [128, 2, AREA], F32R)
        xt = sb("xt", [128, 2 * G, C])
        ft = sb("ft", [128, 2 * MODES, C])
        spec = sb("spec", [128, 4, 2 * MODES, 4, B])
        wspec = sb("wspec", [128, 4 * MODES, 3, C])
        zt = shared[:].rearrange("p (k b o) -> p k b o", k=4, b=B)
        vt = sb("vt", [128, 2, 16, 2, C])
        biased = sb("biased", [128, 2, HALF])
        hbiased = ft[:].rearrange("p a c -> p (a c)").rearrange("p (u n) -> p u n", u=2)
        hid = xt[:].rearrange("p i c -> p (i c)").rearrange("p (u n) -> p u n", u=4)
        h_now = sb("h_now", [128, 2, HALF])

        psum = ctx.enter_context(nc.psum_tensor("psum", [128, 8, HALF], F32))
        acc = [psum[:, 0, :], psum[:, 1, :]]
        vp = psum[:, 2:4, :].rearrange("p a b -> p (a b)")
        fxp = psum[:, 4:6, :]
        ap_ = psum[:, 6, 0:256]
        yp = psum[:, 7, :]
        zp = psum[:, :, :].rearrange("p a b -> p (a b)")

        s_const = sem("s_const")
        s_const2 = sem("s_const2")
        s_zero = sem("s_zero")
        s_past = sem("s_past")
        s_zhalo = sem("s_zhalo")
        s_zxin = sem("s_zxin")
        s_zspec = sem("s_zspec")
        s_xin = [sem("s_xin0"), sem("s_xin1")]
        s_acc = sem("s_acc")
        s_bias = sem("s_bias")
        s_x = sem("s_x")
        s_store = [sem("s_store0"), sem("s_store1")]
        s_raw = sem("s_raw")
        s_hi = sem("s_hi")
        s_lo = sem("s_lo")
        s_xt = sem("s_xt")
        s_fx = sem("s_fx")
        s_ft = sem("s_ft")
        s_fy = sem("s_fy")
        s_spec = sem("s_spec")
        s_w = sem("s_w")
        s_neg = sem("s_neg")
        s_cw = sem("s_cw")
        s_cwhi = sem("s_cwhi")
        s_cwlo = sem("s_cwlo")
        s_mix = sem("s_mix")
        s_zt = sem("s_zt")
        s_v = sem("s_v")
        s_vt = sem("s_vt")
        s_h1 = sem("s_h1")
        s_h1b = sem("s_h1b")
        s_hid = sem("s_hid")
        s_y = sem("s_y")
        s_h = sem("s_h")
        s_hst = [sem("s_hst0"), sem("s_hst1")]

        block = ctx.enter_context(nc.Block())
        parts = [slice(0, AREA // 2), slice(AREA // 2, AREA)]

        def reached(eng, which, n):
            if not (isinstance(n, int) and n <= 0):
                eng.wait_ge(which, n)

        def over_pairs(eng, pair, after=None):
            pair(0, 0, True)
            pair(1, 1, False)
            with eng.Fori(1, PAIRS // 2) as it:
                pair(it * 2, 0, False)
                pair(it * 2 + 1, 1, False)

        def over_layers(eng, layer):
            with eng.Fori(0, NL - 1) as l:
                layer(l, False)
            layer(NL - 1, True)

        @block.sync
        def _(sp):
            for dst, src in ((pw[:], pw_d), (pb[:], pb_d), (dft[:], dft_d)):
                sp.dma_start(dst, src).then_inc(s_const, 16)
            sp.wait_ge(s_zxin, 1)

            def load_pair(p, k):
                for m in range(2):
                    sp.dma_start(xin[0:XIN, k, m:m + 1, :],
                                 xin_d[:, ds(p * 2 + m, 1), :]).then_inc(s_xin[k], 16)

            load_pair(0, 0)
            load_pair(1, 1)
            for dst, src in ((q1w[:], q1w_d), (q1b[:], q1b_d), (q2w[:], q2w_d), (q2b[:], q2b_d),
                             (conv_bias[:], convb_d)):
                sp.dma_start(dst, src).then_inc(s_const2, 16)
            sp.dma_start(wspec[:, :, 1:3, :], spec_d[0]).then_inc(s_w, 16)
            sp.dma_start(conv_stage[:], conv_d[0]).then_inc(s_cw, 16)
            with sp.Fori(1, PAIRS // 2) as it:
                for k in range(2):
                    sp.wait_ge(s_acc, it * 8 + (4 * k - 4))
                    load_pair(it * 2 + k, k)

            def load_halo(p):
                for s in range(2):
                    for r in range(2):
                        n = G * ROW - (s and r)
                        off = r * ROW + s
                        d = (1 - s) * 64 + (1 - r) * 32
                        g = s * 64 + r * 32
                        sp.dma_start(halo[d:d + 32, off:off + n],
                                     x_d[ds(p, 1), g:g + 32, 0:n].rearrange("a p n -> (a p) n")
                                     ).then_inc(s_raw, 16)

            def layer(l, last):
                for k in range(2):
                    sp.wait_ge(s_store[k], (l + 1) * (16 * PAIRS // 2))
                sp.sem_inc(s_past, 1)
                sp.wait_ge(s_acc, (l + 1) * (4 * PAIRS))
                sp.wait_ge(s_zhalo, 1)
                load_halo(0)
                if not last:
                    sp.wait_ge(s_mix, l + 1)
                    sp.dma_start(wspec[:, :, 1:3, :],
                                 spec_d[ds(l + 1, 1)].rearrange("a p n t o -> (a p) n t o")).then_inc(s_w, 16)
                    sp.wait_ge(s_cwlo, l + 1)
                    sp.wait_ge(s_cwhi, l + 1)
                    sp.dma_start(conv_stage[:],
                                 conv_d[ds(l + 1, 1)].rearrange("a p s n -> (a p) s n")).then_inc(s_cw, 16)
                with sp.Fori(1, PAIRS) as p:
                    sp.wait_ge(s_hi, l * B + p * 2)
                    sp.wait_ge(s_lo, l * B + p * 2)
                    load_halo(p)

            over_layers(sp, layer)

        @block.gpsimd
        def _(pool):
            nc.gpsimd.memset(x_now[:, :, :, G:PITCH], 0.0).then_inc(s_zero, 1)
            nc.gpsimd.memset(spec[:, :, 0:MODES], 0.0).then_inc(s_zspec, 1)
            nc.gpsimd.memset(halo[:], 0.0).then_inc(s_zhalo, 1)

            def store_pair(T, p, k):
                pool.wait_ge(s_x, T * 4 + 4)
                pool.dma_start(x_d[ds(p, 1)].rearrange("a p n -> (a p) n"),
                               x_now[:, k].rearrange("p i j -> p (i j)")).then_inc(s_store[k], 16)

            def negate(l):
                pool.wait_ge(s_w, (l + 1) * 16)
                pool.sem_inc(s_past, 1)
                nc.gpsimd.tensor_scalar(wspec[:, :, 0, :], wspec[:, :, 2, :], -1.0, None,
                                        ALU.mult).then_inc(s_neg, 1)

            negate(0)
            with pool.Fori(0, PAIRS // 2) as it:
                for k in range(2):
                    store_pair(it * 2 + k, it * 2 + k, k)
            with pool.Fori(0, NL - 1) as l:
                negate(l + 1)
                with pool.Fori(0, PAIRS // 2) as it:
                    for k in range(2):
                        store_pair(l * PAIRS + (it * 2 + (k + PAIRS)), it * 2 + k, k)
            with pool.Fori(0, PAIRS // 2) as it:
                for k in range(2):
                    pool.wait_ge(s_h, it * 2 + k + 1)
                    for u in range(4):
                        pool.dma_start(h_d[ds(it * 2 + k, 1), :, HALF * u:HALF * u + HALF]
                                       .rearrange("a p n -> (a p) n"),
                                       h_now[32 * u:32 * u + 4, k, :]).then_inc(s_hst[k], 16)

            for k in range(2):
                pool.wait_ge(s_hst[k], PAIRS // 2 * 4 * 16)
                pool.wait_ge(s_store[k], NL * PAIRS // 2 * 16)

        @block.tensor
        def _(pe):
            mm = nc.tensor.matmul

            def rows_forward(T):
                pe.wait_ge(s_xt, T * 2 + 2)
                reached(pe, s_ft, T)
                for m in range(2):
                    for h in range(2):
                        z = mm(fxp[64 * m:64 * m + 64, h, :], ex, xt[:, 32 * h + m:32 * h + 32:2, :],
                               start=True, stop=True)
                z.then_inc(s_fx, 1)

            def columns_forward(T):
                pe.wait_ge(s_ft, T + 1)
                reached(pe, s_spec, T)
                for kyb in range(4):
                    for ri in range(2):
                        for h in range(2):
                            k0 = ri * MODES + 4 * kyb + 2 * h
                            z = mm(ap_[64 * h:64 * h + 64, 64 * kyb:64 * kyb + 64],
                                   ft[:, k0:k0 + 2, :].rearrange("p a c -> p (a c)"), ey[:, ri, :],
                                   start=(ri == 0), stop=(ri == 1))
                z.then_inc(s_fy, 1)

            def project(T, k, first):
                pe.wait_ge(s_xin[k], (T + (2 - k)) * 16)
                for u in range(4):
                    if not (first and u < 2):
                        pe.wait_ge(s_x, T * 4 + (u - 1))
                    mm(acc[u % 2], pw[:], xin[:, k, :, 256 * u:256 * u + 256].rearrange("p m (i j) -> p i m j", j=G),
                       start=True, stop=True).then_inc(s_acc, 1)
                    if u == 1 and not first:
                        rows_forward(T - 1)
                if not first:
                    columns_forward(T - 1)

            pe.wait_ge(s_const, 16 * 3)
            pe.wait_ge(s_zxin, 1)
            over_pairs(pe, project)
            rows_forward(PAIRS - 1)
            columns_forward(PAIRS - 1)

            pe.wait_ge(s_const2, 16 * 5)

            def mix(l):
                pe.wait_ge(s_spec, (l + 1) * PAIRS)
                pe.wait_ge(s_neg, l + 1)
                pe.wait_ge(s_x, (l + 1) * (4 * PAIRS))
                pe.sem_inc(s_past, 1)
                for kx in range(MODES):
                    for im in range(2):
                        col = (2 * kx + im) * 128
                        for ri in range(2):
                            for kyb in range(4):
                                z = mm(zp[32 * kyb:32 * kyb + 32, col:col + 128],
                                       wspec[:, kyb * MODES + kx, 1 + im - ri, :],
                                       spec[:, kyb, 2 * kx + ri].rearrange("p q b -> p (q b)"),
                                       start=(ri == 0), stop=(ri == 1))
                z.then_inc(s_mix, 1)

            def columns_back(l, p):
                for m in range(4):
                    z = mm(vp[:, 256 * m:256 * m + 256], iy[:, m, :],
                           zt[:, :, ds(p * 2, 2), :].rearrange("p k b o -> p k (b o)"), start=True, stop=True)
                z.then_inc(s_v, 1)

            def conv_units(l, p, k, units):
                T = l * PAIRS + p
                for u in units:
                    pe.wait_ge(s_x, T * 4 + (4 * PAIRS + u - 1))
                    if u == 0:
                        pe.wait_ge(s_hi, T * 2 + 2)
                        pe.wait_ge(s_lo, T * 2 + 2)
                    first = True
                    for wts, img in ((conv_hi, halo_hi), (conv_lo, halo_hi), (conv_hi, halo_lo)):
                        grid = img[:, k].rearrange("p (i j) -> p i j", j=PITCH)
                        for t in range(4):
                            di, dj = t // 2, t % 2
                            mm(acc[u % 2], wts[:, t, :], grid[:, 16 * u + 2 * di:16 * u + 2 * di + 16, dj:dj + G],
                               start=first, stop=False, skip_group_check=True)
                            first = False
                    if u == 0:
                        pe.wait_ge(s_vt, T + 1)
                    for ih in range(4):
                        for s in range(2):
                            z = mm(acc[u % 2][64 * s:64 * s + 64, 128 * ih:128 * ih + 128],
                                   vt[:, k, 4 * u + ih].rearrange("p r o -> p (r o)"), ix[:, s, :],
                                   start=False, stop=True, skip_group_check=True)
                    z.then_inc(s_acc, 1)

            def head_hidden(p, k):
                for u in range(4):
                    pe.wait_ge(s_x, p * 4 + (NL * PAIRS * 4 + u + 1))
                    if u >= 2:
                        pe.wait_ge(s_hid, p * 4 + (u - 1))
                    mm(fxp[:, u % 2, :], q1w[:], x_now[:, k, 16 * u:16 * u + 16, 0:G],
                       start=True, stop=True).then_inc(s_h1, 1)

            def head_out(p):
                pe.wait_ge(s_hid, p * 4 + 4)
                reached(pe, s_h, p)
                for u in range(4):
                    z = mm(yp[32 * u:32 * u + 4, :], q2w[:], hid[:, u, :], start=True, stop=True)
                z.then_inc(s_y, 1)

            def layer(l, last):
                mix(l)
                pe.wait_ge(s_zt, l * 4 + 4)
                pe.wait_ge(s_cwhi, l + 1)
                pe.wait_ge(s_cwlo, l + 1)

                def pair(p, k, first):
                    columns_back(l, p)
                    conv_units(l, p, k, (0, 1))
                    if last and not first:
                        head_hidden(p - 1, 1 - k)
                    elif not first:
                        rows_forward(l * PAIRS + p + (PAIRS - 1))
                    conv_units(l, p, k, (2, 3))
                    if last and not first:
                        head_out(p - 1)
                    elif not first:
                        columns_forward(l * PAIRS + p + (PAIRS - 1))

                over_pairs(pe, pair)
                if last:
                    head_hidden(PAIRS - 1, 1)
                    head_out(PAIRS - 1)
                else:
                    rows_forward(l * PAIRS + (2 * PAIRS - 1))
                    columns_forward(l * PAIRS + (2 * PAIRS - 1))

            over_layers(pe, layer)

        @block.scalar
        def _(act):
            copy = nc.scalar.activation

            def spectrum(T, b):
                act.wait_ge(s_fy, T + 1)
                for q in range(4):
                    g = slice(32 * q, 32 * q + 32)
                    z = copy(spec[g, :, :, q, ds(b, 2)],
                             ap_[g, :].rearrange("p (k b f) -> p k f b", k=4, b=2), ACT.Identity)
                z.then_inc(s_spec, 1)

            def project(T, k, first):
                for u in range(4):
                    act.wait_ge(s_acc, T * 4 + u + 1)
                    if u == 0 and not (isinstance(T, int) and T < 2):
                        act.wait_ge(s_store[k], (T - k) * 8)
                        act.wait_ge(s_xt, T * 2 - 2)
                    copy(x_now[:, k, 16 * u:16 * u + 16, 0:G],
                         acc[u % 2].rearrange("p (i j) -> p i j", j=G), ACT.Identity,
                         bias=pb[:]).then_inc(s_x, 1)
                if not first:
                    spectrum(T - 1, T * 2 - 2)

            act.wait_ge(s_const, 16 * 3)
            act.wait_ge(s_zero, 1)
            act.wait_ge(s_zspec, 2)
            over_pairs(act, project)
            spectrum(PAIRS - 1, B - 2)

            act.wait_ge(s_const2, 16 * 5)

            def split_hi(T, k, m):
                act.wait_ge(s_raw, (T + 1) * 64)
                act.wait_ge(s_acc, T * 4 + (4 * PAIRS - 4))
                copy(halo_hi[:, k, parts[m]], halo[:, parts[m]], ACT.Identity).then_inc(s_hi, 1)

            def add_bias(T, u):
                act.wait_ge(s_acc, T * 4 + (4 * PAIRS + u + 1))
                copy(biased[:, u % 2, :], acc[u % 2], ACT.Identity, bias=bias_now[:]).then_inc(s_bias, 1)

            def head_bias(p, u):
                act.wait_ge(s_h1, p * 4 + u + 1)
                copy(hbiased[:, u % 2, :], fxp[:, u % 2, :], ACT.Identity, bias=q1b[:]).then_inc(s_h1b, 1)

            def head_read(p, k, early):
                act.wait_ge(s_y, p + 1)
                if not early:
                    act.wait_ge(s_hst[k], (p - k) * 32)
                for u in range(4):
                    z = copy(h_now[32 * u:32 * u + 4, k, :], yp[32 * u:32 * u + 4, :], ACT.Identity,
                             bias=q2b[32 * u:32 * u + 4, :])
                z.then_inc(s_h, 1)

            def layer(l, last):
                act.wait_ge(s_cw, (l + 1) * 16)
                act.wait_ge(s_acc, (l + 1) * (4 * PAIRS))
                copy(conv_hi[:], conv_stage[:], ACT.Identity).then_inc(s_cwhi, 1)
                act.wait_ge(s_cwlo, l + 1)
                split_hi(l * PAIRS, 0, 0)
                split_hi(l * PAIRS, 0, 1)

                def pair(p, k, first, more=True):
                    T = l * PAIRS + p
                    add_bias(T, 0)
                    add_bias(T, 1)
                    if last and not first:
                        for u in range(4):
                            head_bias(p - 1, u)
                    if more:
                        split_hi(T + 1, 1 - k, 0)
                    add_bias(T, 2)
                    add_bias(T, 3)
                    if more:
                        split_hi(T + 1, 1 - k, 1)
                    if last and not first:
                        head_read(p - 1, 1 - k, isinstance(p, int) and p < 3)
                    elif not first:
                        spectrum(T + (PAIRS - 1), p * 2 - 2)

                pair(0, 0, True)
                pair(1, 1, False)
                with act.Fori(1, PAIRS // 2 - 1) as it:
                    pair(it * 2, 0, False)
                    pair(it * 2 + 1, 1, False)
                pair(PAIRS - 2, 0, False)
                pair(PAIRS - 1, 1, False, more=False)
                if last:
                    for u in range(4):
                        head_bias(PAIRS - 1, u)
                    head_read(PAIRS - 1, 1, False)
                else:
                    spectrum(l * PAIRS + (2 * PAIRS - 1), B - 2)

            over_layers(act, layer)

        @block.vector
        def _(dve):
            vec = nc.vector
            vec.memset(shared[:], 0.0).then_inc(s_zxin, 1)
            vec.memset(spec[:, :, MODES:2 * MODES], 0.0).then_inc(s_zspec, 1)

            def turn_x(T, k, h):
                dve.wait_ge(s_x, T * 4 + 2 * h + 2)
                reached(dve, s_fx, T)
                vec.transpose(xt[:, 32 * h:32 * h + 32, :],
                              x_now[:, k, 32 * h:32 * h + 32, 0:G]).then_inc(s_xt, 1)

            def turn_rows(T):
                dve.wait_ge(s_fx, T + 1)
                reached(dve, s_fy, T)
                vec.transpose(ft[:].rearrange("p k c -> p c k"),
                              fxp.rearrange("p a b -> p (a b)").rearrange("p (i c) -> p c i", c=C)
                              ).then_inc(s_ft, 1)

            def project(T, k, first):
                turn_x(T, k, 0)
                if not first:
                    turn_rows(T - 1)
                turn_x(T, k, 1)

            over_pairs(dve, project)
            turn_rows(PAIRS - 1)

            def split_lo(T, k, m):
                dve.wait_ge(s_hi, T * 2 + m + 1)
                dve.wait_ge(s_acc, T * 4 + (4 * PAIRS - 4))
                vec.tensor_tensor(halo_lo[:, k, parts[m]], halo[:, parts[m]], halo_hi[:, k, parts[m]].bitcast(F32),
                                  ALU.subtract).then_inc(s_lo, 1)

            def leaky(out, src, **kw):
                return vec.scalar_tensor_tensor(out=out, in0=src, scalar=0.01, in1=src, op0=ALU.mult, op1=ALU.max)

            def activate(T, l, last, p, k, u):
                dve.wait_ge(s_bias, T * 4 + u + 1)
                if u == 0:
                    early = isinstance(p, int) and p < 2
                    if not last or early:
                        dve.wait_ge(s_store[k], (T + (PAIRS - k)) * 8)
                    else:
                        dve.wait_ge(s_h1, p * 4 - 4)
                leaky(x_now[:, k, 16 * u:16 * u + 16, 0:G],
                      biased[:, u % 2, :].rearrange("p (i j) -> p i j", j=G)).then_inc(s_x, 1)

            def head_activate(p, u):
                dve.wait_ge(s_h1b, p * 4 + u + 1)
                reached(dve, s_y, p)
                leaky(hid[:, u, :], hbiased[:, u % 2, :]).then_inc(s_hid, 1)

            dve.wait_ge(s_const2, 16 * 5)

            def layer(l, last):
                dve.wait_ge(s_cwhi, l + 1)
                vec.tensor_copy(bias_now[:], conv_bias[:, ds(l, 1)])
                vec.tensor_tensor(conv_lo[:], conv_stage[:], conv_hi[:].bitcast(F32),
                                  ALU.subtract).then_inc(s_cwlo, 1)
                split_lo(l * PAIRS, 0, 0)
                split_lo(l * PAIRS, 0, 1)
                dve.wait_ge(s_mix, l + 1)
                dve.wait_ge(s_acc, (l + 1) * (4 * PAIRS))
                for q in range(4):
                    vec.transpose(zt[:, q], zp.rearrange("p (f q b) -> p q b f", q=4, b=B)[:, q]).then_inc(s_zt, 1)

                def pair(p, k, first, more=True):
                    T = l * PAIRS + p
                    dve.wait_ge(s_v, T + 1)
                    dve.wait_ge(s_acc, T * 4 + (4 * PAIRS - 4))
                    vec.transpose(vt[:, k].rearrange("p h r o -> p (h r) o").rearrange("p y o -> p o y"),
                                  vp.rearrange("p (f o) -> p o f", o=C)).then_inc(s_vt, 1)
                    activate(T, l, last, p, k, 0)
                    activate(T, l, last, p, k, 1)
                    if not last:
                        turn_x(T + PAIRS, k, 0)
                        if not first:
                            turn_rows(T + (PAIRS - 1))
                    elif not first:
                        for u in range(4):
                            head_activate(p - 1, u)
                    if more:
                        split_lo(T + 1, 1 - k, 0)
                    activate(T, l, last, p, k, 2)
                    activate(T, l, last, p, k, 3)
                    if more:
                        split_lo(T + 1, 1 - k, 1)
                    if not last:
                        turn_x(T + PAIRS, k, 1)

                pair(0, 0, True)
                pair(1, 1, False)
                with dve.Fori(1, PAIRS // 2 - 1) as it:
                    pair(it * 2, 0, False)
                    pair(it * 2 + 1, 1, False)
                pair(PAIRS - 2, 0, False)
                pair(PAIRS - 1, 1, False, more=False)
                if last:
                    for u in range(4):
                        head_activate(PAIRS - 1, u)
                else:
                    turn_rows(l * PAIRS + (2 * PAIRS - 1))

            over_layers(dve, layer)


NH, NE, D = 4, 4, 16
TOKENS = B * H // 128 * W
NEG = -1e30
TAIL = [("ident", 128), ("w_attn", 128), ("hl", 128), ("hl_b", 1), ("wq", 256), ("wk", 64), ("wvi", 128),
        ("kmask", 4), ("vmask", 4), ("gate", 32), ("gate_b", 16), ("fc1", 128), ("fc1_b", D), ("fc2", 128),
        ("fc2_b", D), ("ln_g", D), ("ln_b", D), ("fnorm_g", D), ("fnorm_b", D), ("fgate", 8), ("fold", 64)]


def build_tail(nc, h_d, tail_d, onehot_d, causal_d, out_d):
    with ExitStack() as ctx:
        def sb(name, shape, dt=F32):
            return ctx.enter_context(nc.sbuf_tensor(name, shape, dt))

        def sem(name):
            return ctx.enter_context(nc.semaphore(name))

        consts = sb("t_consts", [128, sum(n for _, n in TAIL)])
        at, c = 0, {}
        for name, n in TAIL:
            c[name] = consts[:, at:at + n]
            at += n
        ident = c["ident"]

        h_in = sb("t_h_in", [128, 16, 2, G])
        h0 = sb("t_h0", [128, 16, W])
        h1 = sb("t_h1", [128, 16, W])
        z = sb("t_z", [128, 16, W])
        xc = sb("t_xc", [128, 16, W])
        sq = sb("t_sq", [128, 16, W])
        small = sb("t_small", [128, 6, 64])
        zT = sb("t_zT", [128, 8, 128])
        uT = sb("t_uT", [128, 8, 128])
        dif = sb("t_dif", [128, 2, 512])
        ebd = sb("t_ebd", [128, 16, 128])
        ebdT = sb("t_ebdT", [128, 16, 128])
        sxT = sb("t_sxT", [64, B, H])
        lq = sb("t_lq", [128, B, NE, H])
        kr = sb("t_kr", [128, B, NH, H])
        vbd = sb("t_vbd", [128, B, 2, 34])
        sx = sb("t_sx", [128, B, NH * D])
        prob = sb("t_prob", [128, 2, 512])
        probT = sb("t_probT", [128, 2, 512])
        qT = sb("t_qT", [128, 2, 128])
        mixed = sb("t_mixed", [128, B, NH * D])
        gs = sb("t_gs", [128, B, NH, NE])
        gsel = sb("t_gsel", [128, B, 2, NH])
        qkv = sb("t_qkv", [128, B, 2, NH * D])
        psum = ctx.enter_context(nc.psum_tensor("t_psum", [128, 8, 512], F32))
        bank = lambda a, n=1: psum[:, a:a + n, :].rearrange("p a b -> p (a b)")

        s_load = sem("t_load")
        s_const = sem("t_const")
        s_zero = sem("t_zero")
        s_dve = sem("t_dve")
        s_var = sem("t_var")
        s_std = sem("t_std")
        s_norm = sem("t_norm")
        s_turn = sem("t_turn")
        s_turned = sem("t_turned")
        s_u = sem("t_u")
        s_uc = sem("t_uc")
        s_s1 = sem("t_s1")
        s_dif = sem("t_dif_ready")
        s_exp = sem("t_exp")
        s_tr = sem("t_tr")
        s_trc = sem("t_trc")
        s_msg = sem("t_msg")
        s_mm = sem("t_mm")
        s_mc = sem("t_mc")
        s_vc = sem("t_vc")
        s_sc = sem("t_sc")
        s_df = sem("t_df")
        s_pr = sem("t_pr")
        s_pt = sem("t_pt")
        s_pc = sem("t_pc")
        s_av = sem("t_av")
        s_oc = sem("t_oc")
        s_q = sem("t_q")
        s_qt = sem("t_qt")
        s_qc = sem("t_qc")
        s_g = sem("t_g")
        s_gd = sem("t_gd")
        s_ge = sem("t_ge")
        s_mx = sem("t_mx")
        s_fold = sem("t_fold")
        s_f = sem("t_f")
        s_fe = sem("t_fe")
        s_fee = sem("t_fee")
        s_out = sem("t_out")
        s_stored = sem("t_stored")

        def reached(eng, which, n):
            if n > 0:
                eng.wait_ge(which, n)

        block = ctx.enter_context(nc.Block())
        CHUNK = 8

        @block.sync
        def _(sp):
            for b2 in range(2):
                for s in range(2):
                    for r in range(2):
                        rows = slice(64 * b2 + r, 64 * b2 + 64, 2)
                        sp.dma_start(h_in[rows, :, s, :],
                                     h_d[:, 2 * s + r, :].rearrange("b (i m j) -> i b m j", m=2, j=G)[:, :, b2, :]
                                     ).then_inc(s_load, 16)
            sp.dma_start(consts[:], tail_d).then_inc(s_const, 16)
            sp.dma_start(lq[64:128].rearrange("p b e s -> p b (e s)"), onehot_d).then_inc(s_const, 16)
            sp.dma_start(kr[64:128].rearrange("p b n t -> p b (n t)"), causal_d).then_inc(s_const, 16)
            sp.wait_ge(s_out, 1)
            for b2 in range(2):
                sp.dma_start(out_d[b2:B:2].rearrange("b y x -> y b x"),
                             h1[64 * b2:64 * b2 + 64]).then_inc(s_stored, 16)
            sp.wait_ge(s_stored, 32)

        @block.gpsimd
        def _(pool):
            nc.gpsimd.memset(ebd[:], 0.0).then_inc(s_zero, 1)

        @block.tensor
        def _(pe):
            mm = nc.tensor.matmul

            def turn(src, n, free=None):
                pe.wait_ge(s_norm, n)
                if free:
                    pe.wait_ge(*free)
                for k in range(8):
                    t = nc.tensor.transpose(bank(0, 2)[:, 128 * k:128 * k + 128],
                                            src[:, 2 * k:2 * k + 2, :].rearrange("p a b -> p (a b)"), ident)
                t.then_inc(s_turn, 1)
                pe.wait_ge(s_turned, n)

            pe.wait_ge(s_const, 48)
            turn(z, 1)
            for h in range(2):
                t = mm(bank(2 + h), c["w_attn"], zT[:, 4 * h:4 * h + 4, :], start=True, stop=True)
            t.then_inc(s_u, 1)
            pe.wait_ge(s_uc, 1)
            for bp in range(16):
                for b2 in range(2):
                    g = slice(64 * (bp % 2), 64 * (bp % 2) + 64)
                    k, col = bp // 2, slice(64 * b2, 64 * b2 + 64)
                    t = mm(bank(4 + bp % 2)[64 * b2:64 * b2 + 64, 64 * k:64 * k + 64], uT[g, k, col], zT[g, k, col],
                           start=True, stop=True)
            t.then_inc(s_s1, 1)
            pe.wait_ge(s_exp, 1)
            for bp in range(16):
                t = nc.tensor.transpose(bank(0, 4)[:, 128 * bp:128 * bp + 128], ebd[:, bp, :], ident)
            t.then_inc(s_tr, 1)
            pe.wait_ge(s_trc, 1)
            for bp in range(16):
                t = mm(bank(6, 2)[:, 64 * bp:64 * bp + 64], ebdT[:, bp, :], z[:, bp, :], start=True, stop=True)
            t.then_inc(s_msg, 1)

            turn(z, 2)
            for k in range(4):
                mm(bank(2 + k)[0:64, :], c["hl"][:, 64 * (k // 2):64 * (k // 2) + 64],
                   zT[:, 4 * (k % 2):4 * (k % 2) + 4, :], start=True, stop=True).then_inc(s_mm, 1)
            pe.wait_ge(s_mc, 4)
            toks = lambda k: sxT[:, CHUNK * k:CHUNK * k + CHUNK, :]
            for k in range(4):
                for e in range(NE):
                    n = 4 * k + e
                    if n >= 4:
                        pe.wait_ge(s_mc, n + 1)
                    mm(bank((6 + e) % 8)[0:64, :], c["wq"][0:64, 64 * e:64 * e + 64], toks(k),
                       start=True, stop=True).then_inc(s_mm, 1)
                mm(bank(2 + k)[0:64, :], c["wk"][0:64, :], toks(k), start=True, stop=True).then_inc(s_mm, 1)
            pe.wait_ge(s_vc, 4)
            for k in range(8):
                if k >= 4:
                    pe.wait_ge(s_vc, k + 1)
                for i in range(4):
                    img = 4 * k + i
                    for dup in range(2):
                        t = mm(bank(2 + k % 4)[64 * dup:64 * dup + 64, 128 * i:128 * i + 128],
                               sxT[:, img, :], c["wvi"][0:64, :], start=True, stop=True)
                t.then_inc(s_mm, 1)
            pe.wait_ge(s_mc, 20)
            pe.wait_ge(s_vc, 12)
            for i in range(B + 5):
                if i < B:
                    if i >= 2:
                        pe.wait_ge(s_df, i - 1)
                    for eh in range(2):
                        t = mm(bank(i % 2)[:, 256 * eh:256 * eh + 256],
                               lq[:, i, 2 * eh:2 * eh + 2, :].rearrange("p a b -> p (a b)"),
                               kr[:, i].rearrange("p a b -> p (a b)"), start=True, stop=True)
                    t.then_inc(s_sc, 1)
                if 1 <= i <= B:
                    pe.wait_ge(s_pr, i)
                    if i >= 3:
                        pe.wait_ge(s_pc, i - 2)
                    for k in range(4):
                        t = nc.tensor.transpose(bank(2 + (i - 1) % 2)[:, 128 * k:128 * k + 128],
                                                prob[:, (i - 1) % 2, 128 * k:128 * k + 128], ident)
                    t.then_inc(s_pt, 1)
                if 2 <= i <= B + 1:
                    j = i - 2
                    pe.wait_ge(s_pc, j + 1)
                    if j >= 2:
                        pe.wait_ge(s_oc, j - 1)
                    for k in range(4):
                        t = mm(bank(4 + j % 2)[:, 34 * k:34 * k + 34], probT[:, j % 2, 128 * k:128 * k + 128],
                               vbd[:, j, k % 2, :], start=True, stop=True)
                    t.then_inc(s_av, 1)
                if 4 <= i <= B + 3:
                    j = i - 4
                    pe.wait_ge(s_q, j + 1)
                    reached(pe, s_qc, j)
                    nc.tensor.transpose(bank(6)[:, 0:128], qkv[:, j, 0:2, :].rearrange("p a b -> p (a b)"),
                                        ident).then_inc(s_qt, 1)
                if i >= 5:
                    j = i - 5
                    pe.wait_ge(s_qc, j + 1)
                    for e2 in range(2):
                        for dup in range(2):
                            t = mm(bank(7)[64 * dup:64 * dup + 64, 16 * j:16 * j + 16],
                                   qT[:, j % 2, 64 * e2:64 * e2 + 64], c["gate"][:, 16 * e2:16 * e2 + 16],
                                   start=(e2 == 0), stop=(e2 == 1))
                    t.then_inc(s_g, 1)
            pe.wait_ge(s_mx, 1)
            for k in range(2):
                for b2 in range(2):
                    t = mm(bank(4 + k)[64 * b2:64 * b2 + 64, :], c["fold"],
                           mixed[:].rearrange("p (k c b) n -> p k c b n", k=2, b=2)[:, k, :, b2, :],
                           start=True, stop=True)
            t.then_inc(s_fold, 1)

            for n, (w, width) in enumerate((("fc1", 128), ("fc2", 128), ("fgate", 8))):
                turn(z if n != 1 else xc, 3 + n)
                for k in range(8):
                    t = mm(bank(2, 2)[:, width * k:width * k + width], zT[:, k, :], c[w], start=True, stop=True)
                t.then_inc(s_f, 1)

        @block.scalar
        def _(act):
            copy = nc.scalar.activation

            def root(n, m):
                act.wait_ge(s_var, n)
                copy(small[:, 3, 0:m], small[:, 2, 0:m], ACT.Sqrt).then_inc(s_std, 1)

            def turned(n):
                act.wait_ge(s_turn, n)
                copy(zT[:].rearrange("p a b -> p (a b)"), bank(0, 2), ACT.Identity).then_inc(s_turned, 1)

            act.wait_ge(s_const, 48)
            root(1, 16)
            turned(1)
            act.wait_ge(s_dif, 1)
            act.wait_ge(s_zero, 1)
            for b2 in range(2):
                g = slice(64 * b2, 64 * b2 + 64)
                t = copy(ebd[g, :, g], dif[g].rearrange("p a (b m) -> p (a b) m", m=H), ACT.Exp,
                         scale=float(W) ** -0.5)
            t.then_inc(s_exp, 1)
            act.wait_ge(s_tr, 1)
            copy(ebdT[:].rearrange("p a b -> p (a b)"), bank(0, 4), ACT.Identity).then_inc(s_trc, 1)
            root(2, 16)
            turned(2)
            for k in range(4):
                act.wait_ge(s_mm, k + 1)
                copy(sxT[:, CHUNK * k:CHUNK * k + CHUNK, :],
                     bank(2 + k)[0:64, :].rearrange("p (b s) -> p b s", s=H), ACT.Identity,
                     bias=c["hl_b"][0:64, :]).then_inc(s_mc, 1)
            for k in range(4):
                for e in range(NE):
                    act.wait_ge(s_mm, 4 + 5 * k + e + 1)
                    copy(lq[0:64, CHUNK * k:CHUNK * k + CHUNK, e, :],
                         bank((6 + e) % 8)[0:64, :].rearrange("p (b s) -> p b s", s=H),
                         ACT.Identity).then_inc(s_mc, 1)
            for i in range(B + 4):
                if i < B:
                    act.wait_ge(s_df, i + 1)
                    if i >= 2:
                        act.wait_ge(s_pt, i - 1)
                    copy(prob[:, i % 2, :], dif[:, i % 2, :], ACT.Exp, scale=float(D) ** 0.5).then_inc(s_pr, 1)
                if 1 <= i <= B:
                    j = i - 1
                    act.wait_ge(s_pt, j + 1)
                    if j >= 2:
                        act.wait_ge(s_av, j - 1)
                    copy(probT[:, j % 2, :], bank(2 + j % 2), ACT.Identity).then_inc(s_pc, 1)
                if i >= 4:
                    j = i - 4
                    act.wait_ge(s_qt, j + 1)
                    if j >= 2:
                        act.wait_ge(s_g, j - 1)
                    copy(qT[:, j % 2, :], bank(6)[:, 0:128], ACT.Identity).then_inc(s_qc, 1)
            act.wait_ge(s_gd, 1)
            copy(gs[:], gs[:], ACT.Exp).then_inc(s_ge, 1)
            root(3, 64)
            turned(3)
            turned(4)
            root(4, 64)
            turned(5)
            act.wait_ge(s_fe, 1)
            copy(gs[:, 0:4].rearrange("p a b c -> p (a b c)"), gs[:, 0:4].rearrange("p a b c -> p (a b c)"),
                 ACT.Exp).then_inc(s_fee, 1)

        @block.vector
        def _(dve):
            vec = nc.vector
            chain = [0]

            def link(ins):
                chain[0] += 1
                ins.then_inc(s_dve, 1)
                dve.wait_ge(s_dve, chain[0])

            def wide(a, n):
                return a.unsqueeze(2).to_broadcast([128, a.shape[1], n])

            def normalise(src, out, n, m, eps, count, last=True):
                total, mean, var, root, inv = (small[:, k, 0:m] for k in range(5))
                cen = xc[:].rearrange("p a b -> p (a b)").rearrange("p (m n) -> p m n", n=n)
                sqv = sq[:].rearrange("p a b -> p (a b)").rearrange("p (m n) -> p m n", n=n)
                link(vec.tensor_reduce(total, src, AX.X, ALU.add))
                link(vec.tensor_scalar(mean, total, 1.0 / n, None, ALU.mult))
                link(vec.tensor_tensor(cen, src, wide(mean, n), ALU.subtract))
                link(vec.tensor_tensor(sqv, cen, cen, ALU.mult))
                link(vec.tensor_reduce(total, sqv, AX.X, ALU.add))
                vec.tensor_scalar(var, total, 1.0 / n, eps, ALU.mult, ALU.add).then_inc(s_var, 1)
                dve.wait_ge(s_std, count)
                link(vec.reciprocal(inv, root))
                ins = vec.tensor_tensor(out, cen, wide(inv, n), ALU.mult)
                if last:
                    ins.then_inc(s_norm, 1)
                link_free(ins) if not last else None

            def link_free(ins):
                link(ins)

            dve.wait_ge(s_load, 8 * 16)
            link(vec.tensor_copy(h0[:].rearrange("p b (j s) -> p b s j", s=2), h_in[:]))
            normalise(h0[:], z[:], W, 16, 1e-5, 1)
            dve.wait_ge(s_u, 1)
            vec.tensor_copy(uT[:].rearrange("p a b -> p (a b)"), bank(2, 2)).then_inc(s_uc, 1)
            dve.wait_ge(s_s1, 1)
            for g in range(2):
                scores = bank(4 + g).rearrange("p (c m) -> p c m", m=H)
                link(vec.tensor_reduce(small[:, 5, 8 * g:8 * g + 8], scores, AX.X, ALU.max))
                t = vec.tensor_tensor(dif[:].rearrange("p a (b m) -> p (a b) m", m=H)[:, g:16:2, :], scores,
                                      wide(small[:, 5, 8 * g:8 * g + 8], H), ALU.subtract)
            t.then_inc(s_dif, 1)
            dve.wait_ge(s_exp, 1)
            link(vec.tensor_reduce(small[:, 0, 0:16], ebd[:], AX.X, ALU.add))
            link(vec.reciprocal(small[:, 1, 0:16], small[:, 0, 0:16]))
            dve.wait_ge(s_msg, 1)
            link(vec.tensor_tensor(sq[:], bank(6, 2).rearrange("p (b m) -> p b m", m=W),
                                   wide(small[:, 1, 0:16], W), ALU.mult))
            link(vec.tensor_tensor(h1[:], h0[:], sq[:], ALU.add))
            normalise(h1[:], z[:], W, 16, 1e-5, 2)

            dve.wait_ge(s_const, 48)
            for k in range(4):
                dve.wait_ge(s_mm, 4 + 5 * k + 5)
                keys = bank(2 + k)[0:64, :].rearrange("p (b t) -> p b t", t=H)
                for n in range(NH):
                    t = vec.tensor_scalar(kr[0:64, CHUNK * k:CHUNK * k + CHUNK, n, :], keys,
                                          c["kmask"][0:64, n:n + 1], None, ALU.mult)
                t.then_inc(s_vc, 1)
            for k in range(2):
                vec.tensor_copy(vbd[:, :, k, 32:34], c["vmask"][:, 0:2].unsqueeze(1).to_broadcast([128, B, 2]))
            for k in range(8):
                dve.wait_ge(s_mm, 24 + k + 1)
                both = bank(2 + k % 4).rearrange("p (b n) -> p b n", b=4)
                for nl in range(2):
                    vec.tensor_scalar(vbd[:, 4 * k:4 * k + 4, :, 16 * nl:16 * nl + 16],
                                      both[:, :, 0:64].rearrange("p b (h l d) -> p b h l d", h=2, l=2)[:, :, :, nl, :],
                                      c["vmask"][:, nl:nl + 1], None, ALU.mult)
                vec.tensor_copy(sx[:, 4 * k:4 * k + 4, :], both[:, :, 64:128]).then_inc(s_vc, 1)

            for i in range(B + 2):
                if i < B:
                    dve.wait_ge(s_sc, i + 1)
                    s4 = bank(i % 2).rearrange("p (a t) -> p a t", t=H)
                    link(vec.tensor_reduce(small[:, i % 2, 0:8], s4, AX.X, ALU.max))
                    if i >= 2:
                        dve.wait_ge(s_pr, i - 1)
                    vec.tensor_tensor(dif[:, i % 2, :].rearrange("p (a t) -> p a t", t=H), s4,
                                      wide(small[:, i % 2, 0:8], H), ALU.subtract).then_inc(s_df, 1)
                if i >= 2:
                    j = i - 2
                    dve.wait_ge(s_av, j + 1)
                    o4 = bank(4 + j % 2)[:, 0:136].rearrange("p (a n) -> p a n", n=34)
                    den = small[:, 2 + j % 2, 0:8]
                    link(vec.reciprocal(den.rearrange("p (a n) -> p a n", n=2), o4[:, :, 32:34]))
                    q8 = qkv[:, j, 0:2, :].rearrange("p e n -> p (e n)")
                    ins = vec.tensor_tensor(q8.rearrange("p (a d) -> p a d", d=D).rearrange("p (a l) d -> p a l d", l=2),
                                            o4[:, :, 0:32].rearrange("p a (l d) -> p a l d", l=2),
                                            den.rearrange("p (a l) -> p a l", l=2).unsqueeze(3)
                                            .to_broadcast([128, 4, 2, D]), ALU.mult)
                    ins.then_inc(s_oc, 1)
                    dve.wait_ge(s_oc, j + 1)
                    q2 = qkv[:, j, 0:2, :]
                    vec.scalar_tensor_tensor(out=q2, in0=sx[:, j, :].unsqueeze(1).to_broadcast([128, 2, 64]),
                                             scalar=0.0, in1=q2, op0=ALU.not_equal, op1=ALU.mult).then_inc(s_q, 1)
            resid = c["wk"]
            for n in range(NH):
                img = (n // 2 % 2) * 16 + (n // 4) * 2 + n % 2
                t = vec.tensor_copy(resid[:, D * n:D * n + D], sx[:, img, D * n:D * n + D])

            dve.wait_ge(s_g, B)
            gl = gs[:].rearrange("p b n e -> p b (n e)")
            link(vec.tensor_tensor(gl, bank(7).rearrange("p (b n) -> p b n", b=B),
                                   c["gate_b"].unsqueeze(1).to_broadcast([128, B, 16]), ALU.add))
            g3 = gs[:].rearrange("p b n e -> p (b n) e")
            gm = ebd[:].rearrange("p a b -> p (a b)")[:, 256:384]
            link(vec.tensor_reduce(gm, g3, AX.X, ALU.max))
            vec.tensor_tensor(g3, g3, wide(gm, NE), ALU.subtract).then_inc(s_gd, 1)
            dve.wait_ge(s_ge, 1)
            link(vec.tensor_reduce(gm, g3, AX.X, ALU.add))
            link(vec.reciprocal(gm, gm))
            link(vec.tensor_tensor(g3, g3, wide(gm, NE), ALU.mult))
            for e2 in range(2):
                g = slice(64 * e2, 64 * e2 + 64)
                for eh in range(2):
                    t = vec.tensor_copy(gsel[g, :, eh, :], gs[g, :, :, 2 * eh + e2])
            link(t)
            for eh in range(2):
                q4 = qkv[:, :, eh, :].rearrange("p b (n d) -> p b n d", d=D)
                t = vec.tensor_tensor(q4, q4, gsel[:, :, eh, :].unsqueeze(3).to_broadcast([128, B, NH, D]), ALU.mult)
            link(t)
            vec.tensor_tensor(mixed[:], qkv[:, :, 0, :], qkv[:, :, 1, :], ALU.add).then_inc(s_mx, 1)

            dve.wait_ge(s_fold, 1)
            y = h_in[:].rearrange("p b s j -> p b (s j)")
            for k in range(2):
                t = vec.tensor_tensor(y[:, k:16:2, :], bank(4 + k).rearrange("p (c n) -> p c n", n=64),
                                      resid.unsqueeze(1).to_broadcast([128, 8, 64]), ALU.add)
            link(t)

            rows = lambda a: a.rearrange("p b (n d) -> p (b n) d", d=D)
            vecs = lambda name: c[name].unsqueeze(1).to_broadcast([128, 64, D])
            fx = rows(z[:])
            t3 = rows(sq[:])
            ffp = bank(2, 2).rearrange("p (m d) -> p m d", d=D)
            normalise(rows(y), fx, D, 64, 1e-8, 3, last=False)
            link(vec.tensor_tensor(fx, fx, vecs("ln_g"), ALU.mult))
            vec.tensor_tensor(fx, fx, vecs("ln_b"), ALU.add).then_inc(s_norm, 1)

            dve.wait_ge(s_f, 1)
            link(vec.tensor_tensor(t3, ffp, vecs("fc1_b"), ALU.add))
            link(vec.scalar_tensor_tensor(out=t3, in0=fx, scalar=0.0, in1=t3, op0=ALU.not_equal, op1=ALU.mult))
            vec.tensor_scalar(rows(xc[:]), t3, 0.0, None, ALU.max).then_inc(s_norm, 1)
            dve.wait_ge(s_f, 2)
            link(vec.tensor_tensor(t3, ffp, vecs("fc2_b"), ALU.add))
            link(vec.scalar_tensor_tensor(out=t3, in0=fx, scalar=0.0, in1=t3, op0=ALU.not_equal, op1=ALU.mult))
            hy = rows(h0[:])
            link(vec.tensor_tensor(hy, t3, fx, ALU.add))
            normalise(hy, fx, D, 64, 1e-8, 4, last=False)
            link(vec.tensor_tensor(fx, fx, vecs("fnorm_g"), ALU.mult))
            vec.tensor_tensor(fx, fx, vecs("fnorm_b"), ALU.add).then_inc(s_norm, 1)

            dve.wait_ge(s_f, 3)
            fg = gs[:, 0:4].rearrange("p a b c -> p (a b c)")
            fl = fg.rearrange("p (m n) -> p m n", n=NH)
            lg = bank(2, 2)[:, 0:64].rearrange("p (m n) -> p m n", n=NH)
            fm = small[:, 0, 0:16]
            link(vec.tensor_reduce(fm, lg, AX.X, ALU.max))
            vec.tensor_tensor(fl, lg, wide(fm, NH), ALU.subtract).then_inc(s_fe, 1)
            dve.wait_ge(s_fee, 1)
            link(vec.tensor_reduce(fm, fl, AX.X, ALU.add))
            link(vec.reciprocal(fm, fm))
            link(vec.tensor_tensor(fl, fl, wide(fm, NH), ALU.mult))
            link(vec.tensor_tensor(fx, fx, wide(fg, D), ALU.mult))
            vec.tensor_tensor(h1[:], h1[:], z[:], ALU.add).then_inc(s_out, 1)


def tail_inputs(t):
    t = {k: np.asarray(v) for k, v in t.items()}

    def diag(w, n, rows=128):
        a, b = w.shape
        out = np.zeros((rows, n * b), np.float32)
        for k in range(n):
            out[a * k:a * k + a, b * k:b * k + b] = w
        return out

    def heads(ws, rows=128):
        a, b = ws[0].shape
        out = np.zeros((rows, len(ws) * b), np.float32)
        for k, w in enumerate(ws):
            out[a * k:a * k + a, b * k:b * k + b] = w
        return out

    p = {}
    p["ident"] = np.eye(128, dtype=np.float32)
    p["w_attn"] = diag(t["L0_attn_W"], 2)
    p["hl"] = diag(t["L0_ffn_hl_w"].reshape(64, 64).T, 2)
    hl_b = np.zeros((128, 1), np.float32)
    hl_b[0:64, 0] = t["L0_ffn_hl_b"].reshape(64)
    p["hl_b"] = hl_b
    wq = t["L0_ffn_wq"]
    p["wq"] = np.concatenate([heads([wq[n, e].T for n in range(NH)]) for e in range(NE)], axis=1)
    p["wk"] = heads([w.T for w in t["L0_ffn_wk"]])
    eye64 = np.zeros((128, 64), np.float32)
    eye64[0:64] = np.eye(64)
    p["wvi"] = np.concatenate([heads([w.T for w in t["L0_ffn_wv"]]), eye64], axis=1)
    kmask = np.zeros((128, 4), np.float32)
    for n in range(NH):
        kmask[D * n:D * n + D, n] = 1
    p["kmask"] = kmask
    vmask = np.zeros((128, 4), np.float32)
    vmask[0:64, 0] = 1
    vmask[64:128, 1] = 1
    p["vmask"] = vmask
    gw = t["L0_ffn_gate_w"].reshape(NH, NE, 2, 2, D)
    gate = np.zeros((2, NH, D, 2, NH, NE), np.float32)
    for n in range(NH):
        gate[:, n, :, :, n, :] = gw[n].transpose(1, 3, 2, 0)
    p["gate"] = gate.reshape(128, 32)
    row = lambda a: np.tile(a.reshape(1, -1), (128, 1))
    p["gate_b"] = row(t["L0_ffn_gate_b"])
    p["fc1"] = diag(t["L0_ffn_fc1_w"].T, 8)
    p["fc2"] = diag(t["L0_ffn_fc2_w"].T, 8)
    p["fgate"] = diag(t["L0_ffn_fgate_w"].T, 2)
    for a in ("fc1_b", "fc2_b", "ln_g", "ln_b", "fnorm_g", "fnorm_b"):
        p[a] = row(t["L0_ffn_" + a])
    p["fold"] = np.tile(np.eye(64, dtype=np.float32), (2, 1))
    onehot = np.tile(np.eye(64, dtype=np.float32)[:, None, :], (1, B, NE)).reshape(64, B, NE * H)
    causal = np.where(np.tri(H, dtype=bool), 0.0, NEG).astype(np.float32)
    causal = np.tile(causal[:, None, :], (1, B, NH)).reshape(64, B, NH * H)
    return {"tail": np.concatenate([p[n] for n, _ in TAIL], axis=1), "onehot": onehot, "causal": causal}


def tower_inputs(t):
    x = np.ascontiguousarray(t["x"])
    grid = np.ascontiguousarray(t["L0_tok_input_grid"])
    xin = np.empty((2, 2, 5, B, G, G), np.float32)
    xin[:, :, 0:2] = grid.reshape(G, 2, G, 2, 2).transpose(3, 1, 4, 0, 2)[:, :, :, None]
    xin[:, :, 2:5] = x.reshape(B, G, 2, G, 2, 3).transpose(4, 2, 5, 0, 1, 3)

    def per_pixel(w, rows=128):
        n, m = w.shape
        out = np.zeros((rows, 4 * m), np.float32)
        for g in range(4):
            out[n * g:n * g + n, m * g:m * g + m] = w
        return out

    conv_w = np.asarray(t["L0_tok_conv_w"])
    conv = np.zeros((NL, 2, 2, C, 2, 2, 2, 2, C), np.float32)
    for di in range(2):
        for dj in range(2):
            for r1 in range(2):
                for s1 in range(2):
                    for r in range(2):
                        for s in range(2):
                            ky, kx = 2 * di + r1 - r, 2 * dj + s1 - s
                            if 0 <= ky < 3 and 0 <= kx < 3:
                                conv[:, s1, r1, :, di, dj, s, r, :] = conv_w[:, :, :, ky, kx].transpose(0, 2, 1)
    spec = np.stack([np.asarray(t["L0_tok_spec_wr"]), np.asarray(t["L0_tok_spec_wi"])])
    spec = spec.reshape(2, NL, C, C, MODES, 4, 4).transpose(1, 6, 2, 5, 4, 0, 3)
    four = lambda b: np.tile(np.asarray(b).reshape(-1), 4).reshape(128, 1)
    return {
        "xin": xin.reshape(XIN, B, G * G),
        "pw": per_pixel(np.asarray(t["L0_tok_P_w"])),
        "pb": four(t["L0_tok_P_b"]),
        "dft": dft_constants(),
        "spec": np.ascontiguousarray(spec).reshape(NL, 128, 4 * MODES, 2, C),
        "conv": conv.reshape(NL, 128, 4, 128),
        "convb": np.ascontiguousarray(np.tile(np.asarray(t["L0_tok_conv_b"]), (1, 4)).T),
        "q1w": per_pixel(np.asarray(t["L0_tok_Q1_w"])),
        "q1b": four(t["L0_tok_Q1_b"]),
        "q2w": per_pixel(np.asarray(t["L0_tok_Q2_w"])),
        "q2b": np.tile(np.asarray(t["L0_tok_Q2_b"]).reshape(-1), 128).reshape(128, 1),
    }


def kernel(**inputs):
    import concourse.bacc as bacc
    from concourse.bass_utils import run_bass_kernel_spmd

    nc = bacc.Bacc("TRN2", target_bir_lowering=False, num_devices=1)
    laid = {**tower_inputs(inputs), **tail_inputs(inputs)}
    arrays, args = {}, []
    for name, a in laid.items():
        arrays[f"in_{name}"] = np.ascontiguousarray(a)
        args.append(nc.dram_tensor(f"in_{name}", a.shape, mybir.dt.from_np(a.dtype), kind="ExternalInput").ap())
    args.append(nc.dram_tensor("out", (B, H, W), F32, kind="ExternalOutput").ap())
    build(nc, *args)
    r = run_bass_kernel_spmd(nc, [arrays], core_ids=[0])
    return r.results[0]["out"]
```

```python
from contextlib import ExitStack

import numpy as np

import concourse.bass as bass
from concourse import mybir

F32 = mybir.dt.float32
F32R = mybir.dt.float32r
ALU = mybir.AluOpType
ACT = mybir.ActivationFunctionType
AX = mybir.AxisListType
ds = bass.ds

B, H, W = 32, 64, 64
C = 32
NL = 4
MODES = 16
G = 32
PITCH = G + 1
ROW = 2 * PITCH
AREA = PITCH * ROW
PAIRS = B // 2
HALF = G * G // 2
XIN = 20


def dft_constants():
    th = 2 * np.pi / H
    ex = np.zeros((2, 2, G, 2, 2, MODES))
    ey = np.zeros((2, 2, G, 2, 2, MODES, 2))
    iy = np.zeros((4, MODES, 2, 2, 2, 4, 16, 2))
    ix = np.zeros((4, 2, 2, 4, 2, 2, 2, 2, G))
    k, g = np.arange(MODES), np.arange(G)
    for s in range(2):
        a = th * np.outer(2 * g + s, k)
        for r in range(2):
            ex[s, r, :, r, 0] = np.cos(a)
            ex[s, r, :, r, 1] = -np.sin(a)
    for r in range(2):
        a = th * np.outer(2 * g + r, k)
        for b in range(2):
            ey[b, r, :, 0, b, :, 0] = np.cos(a)
            ey[b, r, :, 0, b, :, 1] = -np.sin(a)
            ey[b, r, :, 1, b, :, 0] = np.sin(a)
            ey[b, r, :, 1, b, :, 1] = np.cos(a)
    ih = np.arange(16)
    for q in range(4):
        for il in range(2):
            for r in range(2):
                a = th * np.outer(k, 4 * ih + 2 * il + r)
                iy[q, :, 0, 0, il, q, :, r] = np.cos(a)
                iy[q, :, 1, 0, il, q, :, r] = -np.sin(a)
                iy[q, :, 0, 1, il, q, :, r] = np.sin(a)
                iy[q, :, 1, 1, il, q, :, r] = np.cos(a)
        for kyb in range(4):
            ky = 4 * q + kyb
            w = (1.0 if ky == 0 else 2.0) / (H * W)
            for s in range(2):
                a = th * ky * (2 * g + s)
                for b in range(2):
                    for il in range(2):
                        ix[q, 0, il, kyb, b, s, il, b] = w * np.cos(a)
                        ix[q, 1, il, kyb, b, s, il, b] = -w * np.sin(a)
    parts = [ex.reshape(128, 64), ey.reshape(128, 128), iy.reshape(128, 512), ix.reshape(128, 256)]
    return np.concatenate(parts, axis=1).astype(np.float32)


def build(nc, xin_d, pw_d, pb_d, dft_d, spec_d, conv_d, convb_d, q1w_d, q1b_d, q2w_d, q2b_d, tail_d, onehot_d, causal_d, out_d):
    x_d = nc.dram_tensor("activations", [PAIRS, 128, G * ROW], F32, kind="Internal").ap()
    h_d = nc.dram_tensor("tower_out", [PAIRS, 4, 2 * G * G], F32, kind="Internal").ap()

    build_tower(nc, xin_d, pw_d, pb_d, dft_d, spec_d, conv_d, convb_d, q1w_d, q1b_d, q2w_d, q2b_d, x_d, h_d)
    build_tail(nc, h_d, tail_d, onehot_d, causal_d, out_d)


def build_tower(nc, xin_d, pw_d, pb_d, dft_d, spec_d, conv_d, convb_d, q1w_d, q1b_d, q2w_d, q2b_d, x_d, h_d):
    with ExitStack() as ctx:
        def sb(name, shape, dt=F32):
            return ctx.enter_context(nc.sbuf_tensor(name, shape, dt))

        def sem(name):
            return ctx.enter_context(nc.semaphore(name))

        dft = sb("dft", [128, 960])
        ex = dft[:, 0:64]
        ey = dft[:, 64:192].rearrange("p (a n) -> p a n", a=2)
        iy = dft[:, 192:704].rearrange("p (m n) -> p m n", m=4)
        ix = dft[:, 704:960].rearrange("p (s n) -> p s n", s=2)
        pw = sb("pw", [128, 128])
        pb = sb("pb", [128, 1])
        q1w = sb("q1w", [128, 128])
        q1b = sb("q1b", [128, 1])
        q2w = sb("q2w", [128, 4])
        q2b = sb("q2b", [128, 1])
        conv_bias = sb("conv_bias", [128, NL])
        bias_now = sb("bias_now", [128, 1])
        conv_stage = sb("conv_stage", [128, 4, 128])
        conv_hi = sb("conv_hi", [128, 4, 128], F32R)
        conv_lo = sb("conv_lo", [128, 4, 128], F32R)
        shared = sb("shared", [128, 4 * B * C])
        xin = shared[:].rearrange("p (k m n) -> p k m n", k=2, m=2)
        x_now = sb("x_now", [128, 2, 2 * G, PITCH])
        halo = sb("halo", [128, AREA])
        halo_hi = sb("halo_hi", [128, 2, AREA], F32R)
        halo_lo = sb("halo_lo", [128, 2, AREA], F32R)
        xin_part = [halo_hi[:, k, 0:2 * G * G].rearrange("p (m n) -> p m n", m=2) for k in range(2)]
        pw_part = sb("pw_part", [128, 128], F32R)
        xt = sb("xt", [128, 2 * G, C])
        ft = sb("ft", [128, 2 * MODES, C])
        spec = sb("spec", [128, 4, 2 * MODES, 4, B])
        wspec = sb("wspec", [128, 4 * MODES, 3, C])
        zt = shared[:].rearrange("p (k b o) -> p k b o", k=4, b=B)
        vt = sb("vt", [128, 2, 16, 2, C])
        xt_odd = vt[:].rearrange("p k h r o -> p (k h r o)").rearrange("p (i c) -> p i c", c=C)
        biased = sb("biased", [128, 2, HALF])
        hbiased = ft[:].rearrange("p a c -> p (a c)").rearrange("p (u n) -> p u n", u=2)
        hid = xt[:].rearrange("p i c -> p (i c)").rearrange("p (u n) -> p u n", u=4)
        h_now = sb("h_now", [128, 2, HALF])

        psum = ctx.enter_context(nc.psum_tensor("psum", [128, 8, HALF], F32))
        acc = [psum[:, 0, :], psum[:, 1, :]]
        vp = psum[:, 2:4, :].rearrange("p a b -> p (a b)")
        fxp = psum[:, 4:6, :]
        ap_ = psum[:, 6, 0:256]
        yp = psum[:, 7, :]
        zp = psum[:, :, :].rearrange("p a b -> p (a b)")

        s_const = sem("s_const")
        s_const2 = sem("s_const2")
        s_zero = sem("s_zero")
        s_past = sem("s_past")
        s_zhalo = sem("s_zhalo")
        s_zxin = sem("s_zxin")
        s_zspec = [sem("s_zspec0"), sem("s_zspec1")]
        s_xin = [sem("s_xin0"), sem("s_xin1")]
        s_pw = sem("s_pw")
        s_xhi = sem("s_xhi")
        s_xlo = [sem("s_xlo0"), sem("s_xlo1")]
        s_acc = sem("s_acc")
        s_bias = sem("s_bias")
        s_x = sem("s_x")
        s_store = [sem("s_store0"), sem("s_store1")]
        s_raw = sem("s_raw")
        s_hi = sem("s_hi")
        s_lo = sem("s_lo")
        s_xt = sem("s_xt")
        s_fx = sem("s_fx")
        s_ft = sem("s_ft")
        s_fy = sem("s_fy")
        s_spec = sem("s_spec")
        s_w = sem("s_w")
        s_neg = sem("s_neg")
        s_cw = sem("s_cw")
        s_cwhi = sem("s_cwhi")
        s_cwlo = sem("s_cwlo")
        s_mix = sem("s_mix")
        s_zt = sem("s_zt")
        s_v = sem("s_v")
        s_vt = sem("s_vt")
        s_h1 = sem("s_h1")
        s_h1b = sem("s_h1b")
        s_hid = sem("s_hid")
        s_y = sem("s_y")
        s_h = sem("s_h")
        s_hlast = sem("s_hlast")
        s_hst = [sem("s_hst0"), sem("s_hst1")]

        block = ctx.enter_context(nc.Block())
        parts = [slice(0, AREA // 2), slice(AREA // 2, AREA)]

        def reached(eng, which, n):
            if not (isinstance(n, int) and n <= 0):
                eng.wait_ge(which, n)

        def over_pairs(eng, pair, after=None):
            pair(0, 0, True)
            pair(1, 1, False)
            with eng.Fori(1, PAIRS // 2) as it:
                pair(it * 2, 0, False)
                pair(it * 2 + 1, 1, False)

        def over_layers(eng, layer):
            with eng.Fori(0, NL - 1) as l:
                layer(l, False)
            layer(NL - 1, True)

        @block.sync
        def _(sp):
            for dst, src in ((pw[:], pw_d), (pb[:], pb_d), (dft[:], dft_d)):
                sp.dma_start(dst, src).then_inc(s_const, 16)
            sp.wait_ge(s_zxin, 2)

            def load_pair(p, k):
                for g in range(4):
                    sp.dma_start(xin[32 * g:32 * g + XIN, k], xin_d[:, ds(p * 2, 2), :]).then_inc(s_xin[k], 16)

            load_pair(0, 0)
            load_pair(1, 1)
            for dst, src in ((q1w[:], q1w_d), (q1b[:], q1b_d), (q2w[:], q2w_d), (q2b[:], q2b_d),
                             (conv_bias[:], convb_d)):
                sp.dma_start(dst, src).then_inc(s_const2, 16)
            sp.dma_start(conv_stage[:], conv_d[0]).then_inc(s_cw, 16)

            def load_turn(it):
                for k in range(2):
                    sp.wait_ge(s_xhi, it * 2 + (k - 1))
                    for m in range(2):
                        sp.wait_ge(s_xlo[m], it * 2 + (k - 1))
                    load_pair(it * 2 + k, k)

            with sp.Fori(1, 5) as it:
                load_turn(it)
                sp.dma_start(wspec[:, ds(it * MODES - MODES, MODES), 1:3, :],
                             spec_d[0, :, ds(it * MODES - MODES, MODES)]).then_inc(s_w, 16)
            with sp.Fori(5, PAIRS // 2) as it:
                load_turn(it)

            def load_halo(p):
                for s in range(2):
                    for r in range(2):
                        n = G * ROW - (s and r)
                        off = r * ROW + s
                        d = (1 - s) * 64 + (1 - r) * 32
                        g = s * 64 + r * 32
                        sp.dma_start(halo[d:d + 32, off:off + n],
                                     x_d[ds(p, 1), g:g + 32, 0:n].rearrange("a p n -> (a p) n")
                                     ).then_inc(s_raw, 16)

            def layer(l, last):
                for k in range(2):
                    sp.wait_ge(s_store[k], (l + 1) * (16 * PAIRS // 2))
                sp.sem_inc(s_past, 1)
                sp.wait_ge(s_acc, (l + 1) * (4 * PAIRS))
                sp.wait_ge(s_zhalo, 1)
                load_halo(0)
                if not last:
                    sp.wait_ge(s_mix, l + 1)
                    for q in range(4):
                        n = slice(MODES * q, MODES * q + MODES)
                        sp.dma_start(wspec[:, n, 1:3, :],
                                     spec_d[ds(l + 1, 1), :, n].rearrange("a p n t o -> (a p) n t o")
                                     ).then_inc(s_w, 16)
                    sp.wait_ge(s_cwlo, l + 1)
                    sp.wait_ge(s_cwhi, l + 1)
                    sp.dma_start(conv_stage[:],
                                 conv_d[ds(l + 1, 1)].rearrange("a p s n -> (a p) s n")).then_inc(s_cw, 16)
                with sp.Fori(1, PAIRS) as p:
                    sp.wait_ge(s_hi, l * B + p * 2)
                    sp.wait_ge(s_lo, l * B + p * 2)
                    load_halo(p)

            over_layers(sp, layer)
            sp.wait_ge(s_h, PAIRS)
            for u in range(4):
                sp.dma_start(h_d[PAIRS - 1, :, HALF * u:HALF * u + HALF],
                             h_now[32 * u:32 * u + 4, 1, :]).then_inc(s_hlast, 16)
            sp.wait_ge(s_hlast, 4 * 16)

        @block.gpsimd
        def _(pool):
            nc.gpsimd.memset(xin[:, 0], 0.0).then_inc(s_zxin, 1)
            nc.gpsimd.memset(x_now[:, :, :, G:PITCH], 0.0).then_inc(s_zero, 1)
            nc.gpsimd.memset(halo[:], 0.0).then_inc(s_zhalo, 1)

            def store_pair(T, p, k):
                pool.wait_ge(s_x, T * 4 + 4)
                pool.dma_start(x_d[ds(p, 1)].rearrange("a p n -> (a p) n"),
                               x_now[:, k].rearrange("p i j -> p (i j)")).then_inc(s_store[k], 16)

            def negate(l):
                pool.wait_ge(s_w, (l + 1) * 64)
                pool.sem_inc(s_past, 1)
                nc.gpsimd.tensor_scalar(wspec[:, :, 0, :], wspec[:, :, 2, :], -1.0, None,
                                        ALU.mult).then_inc(s_neg, 1)

            def input_lo(p, k):
                pool.wait_ge(s_xhi, p + 1)
                reached(pool, s_xlo[0], p)
                nc.gpsimd.tensor_tensor(xin_part[k][64:128, 0], xin[64:128, k, 0],
                                        xin_part[k][64:128, 0].bitcast(F32), ALU.subtract).then_inc(s_xlo[0], 1)

            pool.wait_ge(s_zhalo, 1)
            pool.wait_ge(s_zero, 1)
            input_lo(0, 0)
            input_lo(1, 1)
            pool.wait_ge(s_xlo[0], 2)
            nc.gpsimd.memset(spec[:, :, 0:MODES], 0.0).then_inc(s_zspec[0], 1)
            pool.wait_ge(s_zspec[0], 1)
            store_pair(0, 0, 0)
            with pool.Fori(1, PAIRS // 2) as it:
                for k in range(2):
                    input_lo(it * 2 + k, k)
                    store_pair(it * 2 + (k - 1), it * 2 + (k - 1), 1 - k)
            store_pair(PAIRS - 1, PAIRS - 1, 1)
            negate(0)
            with pool.Fori(0, NL - 1) as l:
                negate(l + 1)
                with pool.Fori(0, PAIRS // 2) as it:
                    for k in range(2):
                        store_pair(l * PAIRS + (it * 2 + (k + PAIRS)), it * 2 + k, k)
            def store_h(p, k):
                pool.wait_ge(s_h, p + 1)
                for u in range(4):
                    pool.dma_start(h_d[ds(p, 1), :, HALF * u:HALF * u + HALF].rearrange("a p n -> (a p) n"),
                                   h_now[32 * u:32 * u + 4, k, :]).then_inc(s_hst[k], 16)

            with pool.Fori(0, PAIRS // 2 - 1) as it:
                for k in range(2):
                    store_h(it * 2 + k, k)
            store_h(PAIRS - 2, 0)

            for k in range(2):
                pool.wait_ge(s_hst[k], (PAIRS // 2 - k) * 4 * 16)
                pool.wait_ge(s_store[k], NL * PAIRS // 2 * 16)

        @block.tensor
        def _(pe):
            mm = nc.tensor.matmul

            def stay_busy(n):
                for _ in range(n):
                    mm(yp[:, 0:128], dft[:, 0:128], dft[:, 0:128], start=True, stop=True)

            def rows_forward(T, xt=xt):
                pe.wait_ge(s_xt, T * 2 + 2)
                reached(pe, s_ft, T)
                for h in range(2):
                    for m in range(2):
                        z = mm(fxp[64 * m:64 * m + 64, h, :], ex, xt[:, 32 * h + m:32 * h + 32:2, :],
                               start=True, stop=True)
                z.then_inc(s_fx, 1)

            def columns_forward(T):
                pe.wait_ge(s_ft, T + 1)
                reached(pe, s_spec, T)
                for kyb in range(4):
                    for ri in range(2):
                        for h in range(2):
                            k0 = ri * MODES + 4 * kyb + 2 * h
                            z = mm(ap_[64 * h:64 * h + 64, 64 * kyb:64 * kyb + 64],
                                   ft[:, k0:k0 + 2, :].rearrange("p a c -> p (a c)"), ey[:, ri, :],
                                   start=(ri == 0), stop=(ri == 1))
                z.then_inc(s_fy, 1)

            def project(T, k, first):
                for m in range(2):
                    pe.wait_ge(s_xlo[m], T + 1)
                for u in range(4):
                    if not (first and u < 2):
                        pe.wait_ge(s_x, T * 4 + (u - 1))
                    mm(acc[u % 2], pw_part[:], xin_part[k][:, :, 256 * u:256 * u + 256].rearrange("p m (i j) -> p i m j", j=G),
                       start=True, stop=True).then_inc(s_acc, 1)
                    if u == 1 and not (isinstance(T, int) and T < 2):
                        columns_forward(T - 2)
                if not first:
                    rows_forward(T - 1, (xt_odd, xt)[k])
                    stay_busy(4)

            pe.wait_ge(s_const, 16 * 3)
            pe.wait_ge(s_pw, 2)
            over_pairs(pe, project)
            columns_forward(PAIRS - 2)
            stay_busy(6)
            rows_forward(PAIRS - 1, xt_odd)
            stay_busy(6)
            columns_forward(PAIRS - 1)
            stay_busy(6)

            pe.wait_ge(s_const2, 16 * 5)

            def mix(l):
                pe.wait_ge(s_spec, (l + 1) * PAIRS)
                pe.wait_ge(s_neg, l + 1)
                pe.wait_ge(s_x, (l + 1) * (4 * PAIRS))
                pe.sem_inc(s_past, 1)
                for kx in range(MODES):
                    for im in range(2):
                        col = (2 * kx + im) * 128
                        for ri in range(2):
                            for kyb in range(4):
                                z = mm(zp[32 * kyb:32 * kyb + 32, col:col + 128],
                                       wspec[:, kyb * MODES + kx, 1 + im - ri, :],
                                       spec[:, kyb, 2 * kx + ri].rearrange("p q b -> p (q b)"),
                                       start=(ri == 0), stop=(ri == 1))
                z.then_inc(s_mix, 1)

            def columns_back(l, p):
                for m in range(4):
                    z = mm(vp[:, 256 * m:256 * m + 256], iy[:, m, :],
                           zt[:, :, ds(p * 2, 2), :].rearrange("p k b o -> p k (b o)"), start=True, stop=True)
                z.then_inc(s_v, 1)

            def conv_units(l, p, k, units):
                T = l * PAIRS + p
                for u in units:
                    pe.wait_ge(s_x, T * 4 + (4 * PAIRS + u - 1))
                    if u == 0:
                        pe.wait_ge(s_hi, T * 2 + 2)
                        pe.wait_ge(s_lo, T * 2 + 2)
                    first = True
                    for wts, img in ((conv_hi, halo_hi), (conv_lo, halo_hi), (conv_hi, halo_lo)):
                        grid = img[:, k].rearrange("p (i j) -> p i j", j=PITCH)
                        for t in range(4):
                            di, dj = t // 2, t % 2
                            mm(acc[u % 2], wts[:, t, :], grid[:, 16 * u + 2 * di:16 * u + 2 * di + 16, dj:dj + G],
                               start=first, stop=False, skip_group_check=True)
                            first = False
                    if u == 0:
                        pe.wait_ge(s_vt, T + 1)
                    for ih in range(4):
                        for s in range(2):
                            z = mm(acc[u % 2][64 * s:64 * s + 64, 128 * ih:128 * ih + 128],
                                   vt[:, k, 4 * u + ih].rearrange("p r o -> p (r o)"), ix[:, s, :],
                                   start=False, stop=True, skip_group_check=True)
                    z.then_inc(s_acc, 1)

            def head_hidden(p, k):
                for u in range(4):
                    pe.wait_ge(s_x, p * 4 + (NL * PAIRS * 4 + u + 1))
                    if u >= 2:
                        pe.wait_ge(s_hid, p * 4 + (u - 1))
                    mm(fxp[:, u % 2, :], q1w[:], x_now[:, k, 16 * u:16 * u + 16, 0:G],
                       start=True, stop=True).then_inc(s_h1, 1)

            def head_out(p):
                pe.wait_ge(s_hid, p * 4 + 4)
                reached(pe, s_h, p)
                for u in range(4):
                    z = mm(yp[32 * u:32 * u + 4, :], q2w[:], hid[:, u, :], start=True, stop=True)
                z.then_inc(s_y, 1)

            def layer(l, last):
                mix(l)
                pe.wait_ge(s_zt, l * 4 + 4)
                pe.wait_ge(s_cwhi, l + 1)
                pe.wait_ge(s_cwlo, l + 1)

                def pair(p, k, first):
                    columns_back(l, p)
                    conv_units(l, p, k, (0, 1))
                    if last and not first:
                        head_hidden(p - 1, 1 - k)
                    elif not first:
                        rows_forward(l * PAIRS + p + (PAIRS - 1))
                    conv_units(l, p, k, (2, 3))
                    if last and not first:
                        head_out(p - 1)
                    elif not first:
                        columns_forward(l * PAIRS + p + (PAIRS - 1))

                over_pairs(pe, pair)
                if last:
                    head_hidden(PAIRS - 1, 1)
                    head_out(PAIRS - 1)
                else:
                    stay_busy(6)
                    rows_forward(l * PAIRS + (2 * PAIRS - 1))
                    stay_busy(6)
                    columns_forward(l * PAIRS + (2 * PAIRS - 1))
                    stay_busy(6)

            over_layers(pe, layer)

        @block.scalar
        def _(act):
            copy = nc.scalar.activation

            def spectrum(T, b):
                act.wait_ge(s_fy, T + 1)
                for q in range(4):
                    g = slice(32 * q, 32 * q + 32)
                    z = copy(spec[g, :, :, q, ds(b, 2)],
                             ap_[g, :].rearrange("p (k b f) -> p k f b", k=4, b=2), ACT.Identity)
                z.then_inc(s_spec, 1)

            def input_hi(p, k, after):
                act.wait_ge(s_xin[k], (p + (2 - k)) * 32)
                if after:
                    act.wait_ge(s_acc, p * 4 - 4)
                copy(xin_part[k], xin[:, k], ACT.Identity).then_inc(s_xhi, 1)

            def project(T, k, first, more=True):
                for u in range(4):
                    act.wait_ge(s_acc, T * 4 + u + 1)
                    if u == 0 and not (isinstance(T, int) and T < 2):
                        act.wait_ge(s_store[k], (T - k) * 8)
                        act.wait_ge(s_xt, T * 2 - 2)
                    copy(x_now[:, k, 16 * u:16 * u + 16, 0:G],
                         acc[u % 2].rearrange("p (i j) -> p i j", j=G), ACT.Identity,
                         bias=pb[:]).then_inc(s_x, 1)
                if not isinstance(T, int):
                    spectrum(T - 2, T * 2 - 4)
                if more:
                    input_hi(T + 2, k, True)

            act.wait_ge(s_const, 16 * 3)
            copy(pw_part[:], pw[:], ACT.Identity).then_inc(s_pw, 1)
            act.wait_ge(s_zxin, 2)
            input_hi(0, 0, False)
            input_hi(1, 1, False)
            act.wait_ge(s_zero, 1)
            project(0, 0, True)
            project(1, 1, False)
            act.wait_ge(s_zspec[0], 1)
            act.wait_ge(s_zspec[1], 2)
            with act.Fori(1, PAIRS // 2 - 1) as it:
                project(it * 2, 0, False)
                project(it * 2 + 1, 1, False)
            for T in (PAIRS - 2, PAIRS - 1):
                project(T, T % 2, False, more=False)
                spectrum(T - 2, T * 2 - 4)
            spectrum(PAIRS - 2, B - 4)
            spectrum(PAIRS - 1, B - 2)

            act.wait_ge(s_const2, 16 * 5)

            def split_hi(T, k, m):
                act.wait_ge(s_raw, (T + 1) * 64)
                act.wait_ge(s_acc, T * 4 + (4 * PAIRS - 4))
                copy(halo_hi[:, k, parts[m]], halo[:, parts[m]], ACT.Identity).then_inc(s_hi, 1)

            def add_bias(T, u):
                act.wait_ge(s_acc, T * 4 + (4 * PAIRS + u + 1))
                copy(biased[:, u % 2, :], acc[u % 2], ACT.Identity, bias=bias_now[:]).then_inc(s_bias, 1)

            def head_bias(p, u):
                act.wait_ge(s_h1, p * 4 + u + 1)
                copy(hbiased[:, u % 2, :], fxp[:, u % 2, :], ACT.Identity, bias=q1b[:]).then_inc(s_h1b, 1)

            def head_read(p, k, early):
                act.wait_ge(s_y, p + 1)
                if not early:
                    act.wait_ge(s_hst[k], (p - k) * 32)
                for u in range(4):
                    z = copy(h_now[32 * u:32 * u + 4, k, :], yp[32 * u:32 * u + 4, :], ACT.Identity,
                             bias=q2b[32 * u:32 * u + 4, :])
                z.then_inc(s_h, 1)

            def layer(l, last):
                act.wait_ge(s_cw, (l + 1) * 16)
                act.wait_ge(s_acc, (l + 1) * (4 * PAIRS))
                copy(conv_hi[:], conv_stage[:], ACT.Identity).then_inc(s_cwhi, 1)
                act.wait_ge(s_cwlo, l + 1)
                split_hi(l * PAIRS, 0, 0)
                split_hi(l * PAIRS, 0, 1)

                def pair(p, k, first, more=True):
                    T = l * PAIRS + p
                    add_bias(T, 0)
                    add_bias(T, 1)
                    if last and not first:
                        for u in range(4):
                            head_bias(p - 1, u)
                    if more:
                        split_hi(T + 1, 1 - k, 0)
                    add_bias(T, 2)
                    add_bias(T, 3)
                    if more:
                        split_hi(T + 1, 1 - k, 1)
                    if last and not first:
                        head_read(p - 1, 1 - k, isinstance(p, int) and p < 3)
                    elif not first:
                        spectrum(T + (PAIRS - 1), p * 2 - 2)

                pair(0, 0, True)
                pair(1, 1, False)
                with act.Fori(1, PAIRS // 2 - 1) as it:
                    pair(it * 2, 0, False)
                    pair(it * 2 + 1, 1, False)
                pair(PAIRS - 2, 0, False)
                pair(PAIRS - 1, 1, False, more=False)
                if last:
                    for u in range(4):
                        head_bias(PAIRS - 1, u)
                    head_read(PAIRS - 1, 1, False)
                else:
                    spectrum(l * PAIRS + (2 * PAIRS - 1), B - 2)

            over_layers(act, layer)

        @block.vector
        def _(dve):
            vec = nc.vector
            vec.memset(xin[:, 1], 0.0).then_inc(s_zxin, 1)

            def turn_x(T, k, h, xt=xt, ring=1):
                dve.wait_ge(s_x, T * 4 + 2 * h + 2)
                reached(dve, s_fx, T - (ring - 1))
                vec.transpose(xt[:, 32 * h:32 * h + 32, :],
                              x_now[:, k, 32 * h:32 * h + 32, 0:G]).then_inc(s_xt, 1)

            def turn_rows(T):
                dve.wait_ge(s_fx, T + 1)
                reached(dve, s_fy, T)
                vec.transpose(ft[:].rearrange("p k c -> p c k"),
                              fxp.rearrange("p a b -> p (a b)").rearrange("p (i c) -> p c i", c=C)
                              ).then_inc(s_ft, 1)

            def input_lo(p, k):
                dve.wait_ge(s_xhi, p + 1)
                vec.tensor_tensor(xin_part[k][64:128, 1], xin[64:128, k, 1],
                                  xin_part[k][64:128, 1].bitcast(F32), ALU.subtract).then_inc(s_xlo[1], 1)

            def project(T, k, first, more=True):
                if not (isinstance(T, int) and T < 2):
                    turn_rows(T - 2)
                turn_x(T, k, 0, (xt, xt_odd)[k], 2)
                if more:
                    input_lo(T + 1, 1 - k)
                turn_x(T, k, 1, (xt, xt_odd)[k], 2)

            dve.wait_ge(s_const, 16 * 3)
            dve.wait_ge(s_pw, 1)
            for g in (32, 96):
                z = vec.tensor_tensor(pw_part[g:g + 32, :], pw[g:g + 32, :], pw_part[g:g + 32, :].bitcast(F32),
                                      ALU.subtract)
            z.then_inc(s_pw, 1)
            input_lo(0, 0)
            project(0, 0, True)
            vec.memset(spec[:, 0:2, MODES:2 * MODES], 0.0).then_inc(s_zspec[1], 1)
            project(1, 1, False)
            vec.memset(spec[:, 2:4, MODES:2 * MODES], 0.0).then_inc(s_zspec[1], 1)
            with dve.Fori(1, PAIRS // 2 - 1) as it:
                project(it * 2, 0, False)
                project(it * 2 + 1, 1, False)
            project(PAIRS - 2, 0, False)
            project(PAIRS - 1, 1, False, more=False)
            turn_rows(PAIRS - 2)
            turn_rows(PAIRS - 1)

            def split_lo(T, k, m):
                dve.wait_ge(s_hi, T * 2 + m + 1)
                dve.wait_ge(s_acc, T * 4 + (4 * PAIRS - 4))
                vec.tensor_tensor(halo_lo[:, k, parts[m]], halo[:, parts[m]], halo_hi[:, k, parts[m]].bitcast(F32),
                                  ALU.subtract).then_inc(s_lo, 1)

            def leaky(out, src, **kw):
                return vec.scalar_tensor_tensor(out=out, in0=src, scalar=0.01, in1=src, op0=ALU.mult, op1=ALU.max)

            def activate(T, l, last, p, k, u):
                dve.wait_ge(s_bias, T * 4 + u + 1)
                if u == 0:
                    early = isinstance(p, int) and p < 2
                    if not last or early:
                        dve.wait_ge(s_store[k], (T + (PAIRS - k)) * 8)
                    else:
                        dve.wait_ge(s_h1, p * 4 - 4)
                leaky(x_now[:, k, 16 * u:16 * u + 16, 0:G],
                      biased[:, u % 2, :].rearrange("p (i j) -> p i j", j=G)).then_inc(s_x, 1)

            def head_activate(p, u):
                dve.wait_ge(s_h1b, p * 4 + u + 1)
                reached(dve, s_y, p)
                leaky(hid[:, u, :], hbiased[:, u % 2, :]).then_inc(s_hid, 1)

            dve.wait_ge(s_const2, 16 * 5)

            def layer(l, last):
                dve.wait_ge(s_cwhi, l + 1)
                vec.tensor_copy(bias_now[:], conv_bias[:, ds(l, 1)])
                vec.tensor_tensor(conv_lo[:], conv_stage[:], conv_hi[:].bitcast(F32),
                                  ALU.subtract).then_inc(s_cwlo, 1)
                split_lo(l * PAIRS, 0, 0)
                split_lo(l * PAIRS, 0, 1)
                dve.wait_ge(s_mix, l + 1)
                dve.wait_ge(s_acc, (l + 1) * (4 * PAIRS))
                for q in range(4):
                    vec.transpose(zt[:, q], zp.rearrange("p (f q b) -> p q b f", q=4, b=B)[:, q]).then_inc(s_zt, 1)

                def pair(p, k, first, more=True):
                    T = l * PAIRS + p
                    dve.wait_ge(s_v, T + 1)
                    dve.wait_ge(s_acc, T * 4 + (4 * PAIRS - 4))
                    vec.transpose(vt[:, k].rearrange("p h r o -> p (h r) o").rearrange("p y o -> p o y"),
                                  vp.rearrange("p (f o) -> p o f", o=C)).then_inc(s_vt, 1)
                    activate(T, l, last, p, k, 0)
                    activate(T, l, last, p, k, 1)
                    if not last:
                        turn_x(T + PAIRS, k, 0)
                        if not first:
                            turn_rows(T + (PAIRS - 1))
                    elif not first:
                        for u in range(4):
                            head_activate(p - 1, u)
                    if more:
                        split_lo(T + 1, 1 - k, 0)
                    activate(T, l, last, p, k, 2)
                    activate(T, l, last, p, k, 3)
                    if more:
                        split_lo(T + 1, 1 - k, 1)
                    if not last:
                        turn_x(T + PAIRS, k, 1)

                pair(0, 0, True)
                pair(1, 1, False)
                with dve.Fori(1, PAIRS // 2 - 1) as it:
                    pair(it * 2, 0, False)
                    pair(it * 2 + 1, 1, False)
                pair(PAIRS - 2, 0, False)
                pair(PAIRS - 1, 1, False, more=False)
                if last:
                    for u in range(4):
                        head_activate(PAIRS - 1, u)
                else:
                    turn_rows(l * PAIRS + (2 * PAIRS - 1))

            over_layers(dve, layer)


NH, NE, D = 4, 4, 16
TOKENS = B * H // 128 * W
NEG = -1e30
TAIL = [("ident", 128), ("w_attn", 128), ("hl", 128), ("hl_b", 1), ("wq", 256), ("wk", 64), ("wvi", 128),
        ("kmask", 4), ("vmask", 4), ("gate", 32), ("gate_b", 16), ("fc1", 128), ("fc1_b", D), ("fc2", 128),
        ("fc2_b", D), ("ln_g", D), ("ln_b", D), ("fnorm_g", D), ("fnorm_b", D), ("fgate", 8), ("fold", 64)]


def build_tail(nc, h_d, tail_d, onehot_d, causal_d, out_d):
    with ExitStack() as ctx:
        def sb(name, shape, dt=F32):
            return ctx.enter_context(nc.sbuf_tensor(name, shape, dt))

        def sem(name):
            return ctx.enter_context(nc.semaphore(name))

        consts = sb("t_consts", [128, sum(n for _, n in TAIL)])
        at, c = 0, {}
        for name, n in TAIL:
            c[name] = consts[:, at:at + n]
            at += n
        ident = c["ident"]

        h_in = sb("t_h_in", [128, 16, 2, G])
        h0 = sb("t_h0", [128, 16, W])
        h1 = sb("t_h1", [128, 16, W])
        z = sb("t_z", [128, 16, W])
        xc = sb("t_xc", [128, 16, W])
        sq = sb("t_sq", [128, 16, W])
        small = sb("t_small", [128, 6, 64])
        zT = sb("t_zT", [128, 8, 128])
        uT = sb("t_uT", [128, 8, 128])
        dif = sb("t_dif", [128, 2, 512])
        ebd = sb("t_ebd", [128, 16, 128])
        ebdT = sb("t_ebdT", [128, 16, 128])
        sxT = sb("t_sxT", [64, B, 2, H])
        lq = sb("t_lq", [128, B, NE, H])
        kr = sb("t_kr", [128, B, NH, H])
        vbd = sb("t_vbd", [128, B, 2, 34])
        sx = sb("t_sx", [128, B, NH * D])
        prob = sb("t_prob", [128, 2, 512])
        probT = sb("t_probT", [128, 2, 512])
        qT = sb("t_qT", [128, 2, 2, 2, H])
        mixed = sb("t_mixed", [128, B, NH * D])
        gs = sb("t_gs", [128, B, NH, NE])
        gsel = sb("t_gsel", [128, B, 2, NH])
        qkv = sb("t_qkv", [128, B, 2, NH * D])
        psum = ctx.enter_context(nc.psum_tensor("t_psum", [128, 8, 512], F32))
        bank = lambda a, n=1: psum[:, a:a + n, :].rearrange("p a b -> p (a b)")

        s_load = sem("t_load")
        s_const = sem("t_const")
        s_mask = sem("t_mask")
        s_zero = sem("t_zero")
        s_dve = sem("t_dve")
        s_var = sem("t_var")
        s_std = sem("t_std")
        s_norm = sem("t_norm")
        s_turn = sem("t_turn")
        s_turned = sem("t_turned")
        s_u = sem("t_u")
        s_uc = sem("t_uc")
        s_s1 = sem("t_s1")
        s_dif = sem("t_dif_ready")
        s_exp = sem("t_exp")
        s_tr = sem("t_tr")
        s_trc = sem("t_trc")
        s_msg = sem("t_msg")
        s_mm = sem("t_mm")
        s_dup = sem("t_dup")
        s_mc = sem("t_mc")
        s_vc = sem("t_vc")
        s_sc = sem("t_sc")
        s_df = sem("t_df")
        s_pr = sem("t_pr")
        s_pt = sem("t_pt")
        s_pc = sem("t_pc")
        s_av = sem("t_av")
        s_oc = sem("t_oc")
        s_q = sem("t_q")
        s_qt = sem("t_qt")
        s_qc = sem("t_qc")
        s_g = sem("t_g")
        s_gd = sem("t_gd")
        s_ge = sem("t_ge")
        s_mx = sem("t_mx")
        s_fold = sem("t_fold")
        s_f = sem("t_f")
        s_fe = sem("t_fe")
        s_fee = sem("t_fee")
        s_out = sem("t_out")
        s_stored = sem("t_stored")

        def reached(eng, which, n):
            if n > 0:
                eng.wait_ge(which, n)

        block = ctx.enter_context(nc.Block())
        CHUNK = 8

        @block.sync
        def _(sp):
            for b2 in range(2):
                for s in range(2):
                    for r in range(2):
                        rows = slice(64 * b2 + r, 64 * b2 + 64, 2)
                        sp.dma_start(h_in[rows, :, s, :],
                                     h_d[:, 2 * s + r, :].rearrange("b (i m j) -> i b m j", m=2, j=G)[:, :, b2, :]
                                     ).then_inc(s_load, 16)
            sp.dma_start(consts[:], tail_d).then_inc(s_const, 16)
            sp.dma_start(lq[64:128].rearrange("p b e s -> p b (e s)"), onehot_d).then_inc(s_mask, 16)
            sp.dma_start(kr[64:128].rearrange("p b n t -> p b (n t)"), causal_d).then_inc(s_mask, 16)
            sp.wait_ge(s_out, 1)
            for b2 in range(2):
                sp.dma_start(out_d[b2:B:2].rearrange("b y x -> y b x"),
                             h1[64 * b2:64 * b2 + 64]).then_inc(s_stored, 16)
            sp.wait_ge(s_stored, 32)

        @block.gpsimd
        def _(pool):
            nc.gpsimd.memset(ebd[:], 0.0).then_inc(s_zero, 1)

        @block.tensor
        def _(pe):
            mm = nc.tensor.matmul

            def stay_busy(b, n):
                for _ in range(n):
                    mm(bank(b)[:, 0:128], ident, ident, start=True, stop=True)

            def turn(src, n):
                pe.wait_ge(s_norm, n)
                for k in range(8):
                    t = nc.tensor.transpose(bank(0, 2)[:, 128 * k:128 * k + 128],
                                            src[:, 2 * k:2 * k + 2, :].rearrange("p a b -> p (a b)"), ident)
                    if k % 4 == 3:
                        t.then_inc(s_turn, 1)

            pe.wait_ge(s_const, 16)
            stay_busy(5, 16)
            turn(z, 1)
            for h in range(2):
                pe.wait_ge(s_turned, 1 + h)
                t = mm(bank(2 + h), c["w_attn"], zT[:, 4 * h:4 * h + 4, :], start=True, stop=True)
            t.then_inc(s_u, 1)
            pe.wait_ge(s_uc, 1)
            for bp in range(16):
                for b2 in range(2):
                    g = slice(64 * (bp % 2), 64 * (bp % 2) + 64)
                    k, col = bp // 2, slice(64 * b2, 64 * b2 + 64)
                    t = mm(bank(4 + bp % 2)[64 * b2:64 * b2 + 64, 64 * k:64 * k + 64], uT[g, k, col], zT[g, k, col],
                           start=True, stop=True)
            t.then_inc(s_s1, 1)
            pe.wait_ge(s_exp, 1)
            for bp in range(16):
                t = nc.tensor.transpose(bank(0, 4)[:, 128 * bp:128 * bp + 128], ebd[:, bp, :], ident)
                if bp % 4 == 3:
                    t.then_inc(s_tr, 1)
            for bp in range(16):
                if bp % 4 == 0:
                    pe.wait_ge(s_trc, bp // 4 + 1)
                t = mm(bank(6, 2)[:, 64 * bp:64 * bp + 64], ebdT[:, bp, :], z[:, bp, :], start=True, stop=True)
                if bp % 8 == 7:
                    t.then_inc(s_msg, 1)

            stay_busy(5, 24)
            turn(z, 2)
            for k in range(4):
                pe.wait_ge(s_turned, 3 + min(k, 1))
                mm(bank(2 + k)[0:64, :], c["hl"][:, 64 * (k // 2):64 * (k // 2) + 64],
                   zT[:, 4 * (k % 2):4 * (k % 2) + 4, :], start=True, stop=True).then_inc(s_mm, 1)
            pe.wait_ge(s_mc, 4)
            pe.wait_ge(s_dup, 4)
            toks = lambda k: sxT[:, CHUNK * k:CHUNK * k + CHUNK, 0, :]
            for k in range(4):
                for h in range(NE // 2):
                    n = 2 * k + h
                    if n >= 4:
                        pe.wait_ge(s_mc, n + 1)
                    mm(bank((6 + n % 4) % 8), c["wq"][0:64, 128 * h:128 * h + 128], toks(k),
                       start=True, stop=True).then_inc(s_mm, 1)
                mm(bank(2 + k)[0:64, :], c["wk"][0:64, :], toks(k), start=True, stop=True).then_inc(s_mm, 1)
            pe.wait_ge(s_vc, 4)
            for k in range(8):
                if k >= 4:
                    pe.wait_ge(s_vc, k + 1)
                for i in range(4):
                    img = 4 * k + i
                    t = mm(bank(2 + k % 4)[:, 128 * i:128 * i + 128],
                           sxT[:, img].rearrange("p a s -> p (a s)"), c["wvi"][0:64, :],
                           start=True, stop=True)
                t.then_inc(s_mm, 1)
            pe.wait_ge(s_mc, 12)
            pe.wait_ge(s_mask, 32)
            pe.wait_ge(s_vc, 12)
            for i in range(B + 5):
                if i < B:
                    if i >= 2:
                        pe.wait_ge(s_df, i - 1)
                    for eh in range(2):
                        t = mm(bank(i % 2)[:, 256 * eh:256 * eh + 256],
                               lq[:, i, 2 * eh:2 * eh + 2, :].rearrange("p a b -> p (a b)"),
                               kr[:, i].rearrange("p a b -> p (a b)"), start=True, stop=True)
                    t.then_inc(s_sc, 1)
                if 1 <= i <= B:
                    pe.wait_ge(s_pr, i)
                    if i >= 3:
                        pe.wait_ge(s_pc, i - 2)
                    for k in range(4):
                        t = nc.tensor.transpose(bank(2 + (i - 1) % 2)[:, 128 * k:128 * k + 128],
                                                prob[:, (i - 1) % 2, 128 * k:128 * k + 128], ident)
                    t.then_inc(s_pt, 1)
                if 2 <= i <= B + 1:
                    j = i - 2
                    pe.wait_ge(s_pc, j + 1)
                    if j >= 2:
                        pe.wait_ge(s_oc, j - 1)
                    for k in range(4):
                        t = mm(bank(4 + j % 2)[:, 34 * k:34 * k + 34], probT[:, j % 2, 128 * k:128 * k + 128],
                               vbd[:, j, k % 2, :], start=True, stop=True)
                    t.then_inc(s_av, 1)
                if 4 <= i <= B + 3:
                    j = i - 4
                    pe.wait_ge(s_q, j + 1)
                    reached(pe, s_qc, j)
                    nc.tensor.transpose(bank(6)[:, 0:128], qkv[:, j, 0:2, :].rearrange("p a b -> p (a b)"),
                                        ident).then_inc(s_qt, 1)
                if i >= 5:
                    j = i - 5
                    pe.wait_ge(s_qc, j + 1)
                    for e2 in range(2):
                        t = mm(bank(7)[:, 16 * j:16 * j + 16],
                               qT[:, j % 2, e2].rearrange("p a s -> p (a s)"),
                               c["gate"][:, 16 * e2:16 * e2 + 16], start=(e2 == 0), stop=(e2 == 1))
                    t.then_inc(s_g, 1)
            for k in range(2):
                pe.wait_ge(s_mx, k + 1)
                for b2 in range(2):
                    t = mm(bank(4 + k)[64 * b2:64 * b2 + 64, :], c["fold"],
                           mixed[:].rearrange("p (k c b) n -> p k c b n", k=2, b=2)[:, k, :, b2, :],
                           start=True, stop=True)
                t.then_inc(s_fold, 1)

            for n, (w, width) in enumerate((("fc1", 128), ("fc2", 128), ("fgate", 8))):
                stay_busy(7, (26, 8, 32)[n])
                turn(z if n != 1 else xc, 3 + n)
                for k in range(8):
                    if k % 4 == 0:
                        pe.wait_ge(s_turned, 2 * n + 5 + k // 4)
                    t = mm(bank(2, 2)[:, width * k:width * k + width], zT[:, k, :], c[w], start=True, stop=True)
                    if k % 4 == 3:
                        t.then_inc(s_f, 1)

        @block.scalar
        def _(act):
            copy = nc.scalar.activation

            def root(n, m):
                act.wait_ge(s_var, n)
                copy(small[:, 3, 0:m], small[:, 2, 0:m], ACT.Sqrt).then_inc(s_std, 1)

            def turned(n):
                for h in range(2):
                    act.wait_ge(s_turn, 2 * n - 1 + h)
                    copy(zT[:, 4 * h:4 * h + 4, :].rearrange("p a b -> p (a b)"), bank(h),
                         ACT.Identity).then_inc(s_turned, 1)

            act.wait_ge(s_const, 16)
            root(1, 16)
            turned(1)
            act.wait_ge(s_dif, 1)
            act.wait_ge(s_zero, 1)
            for b2 in range(2):
                g = slice(64 * b2, 64 * b2 + 64)
                t = copy(ebd[g, :, g], dif[g].rearrange("p a (b m) -> p (a b) m", m=H), ACT.Exp,
                         scale=float(W) ** -0.5)
            t.then_inc(s_exp, 1)
            for k in range(4):
                act.wait_ge(s_tr, k + 1)
                copy(ebdT[:, 4 * k:4 * k + 4].rearrange("p a b -> p (a b)"), bank(k), ACT.Identity).then_inc(s_trc, 1)
            root(2, 16)
            turned(2)
            for k in range(4):
                act.wait_ge(s_mm, k + 1)
                copy(sxT[:, CHUNK * k:CHUNK * k + CHUNK, 0, :],
                     bank(2 + k)[0:64, :].rearrange("p (b s) -> p b s", s=H), ACT.Identity,
                     bias=c["hl_b"][0:64, :]).then_inc(s_mc, 1)
            for k in range(4):
                for h in range(NE // 2):
                    act.wait_ge(s_mm, 4 + 3 * k + h + 1)
                    for e in range(2):
                        t = copy(lq[0:64, CHUNK * k:CHUNK * k + CHUNK, 2 * h + e, :],
                                 bank((6 + (2 * k + h) % 4) % 8)[64 * e:64 * e + 64, :]
                                 .rearrange("p (b s) -> p b s", s=H), ACT.Identity)
                    t.then_inc(s_mc, 1)
            for i in range(B + 4):
                if i < B:
                    act.wait_ge(s_df, i + 1)
                    if i >= 2:
                        act.wait_ge(s_pt, i - 1)
                    copy(prob[:, i % 2, :], dif[:, i % 2, :], ACT.Exp, scale=float(D) ** 0.5).then_inc(s_pr, 1)
                if 1 <= i <= B:
                    j = i - 1
                    act.wait_ge(s_pt, j + 1)
                    if j >= 2:
                        act.wait_ge(s_av, j - 1)
                    copy(probT[:, j % 2, :], bank(2 + j % 2), ACT.Identity).then_inc(s_pc, 1)
                if i >= 4:
                    j = i - 4
                    act.wait_ge(s_qt, j + 1)
                    if j >= 2:
                        act.wait_ge(s_g, j - 1)
                    copy(qT[:, j % 2], bank(6)[:, 0:128].rearrange("p (a s) -> p a s", a=2).unsqueeze(2)
                         .to_broadcast([128, 2, 2, H]), ACT.Identity).then_inc(s_qc, 1)
            act.wait_ge(s_gd, 1)
            copy(gs[:], gs[:], ACT.Exp).then_inc(s_ge, 1)
            root(3, 64)
            turned(3)
            turned(4)
            root(4, 64)
            turned(5)
            act.wait_ge(s_fe, 1)
            copy(gs[:, 0:4].rearrange("p a b c -> p (a b c)"), gs[:, 0:4].rearrange("p a b c -> p (a b c)"),
                 ACT.Exp).then_inc(s_fee, 1)

        @block.vector
        def _(dve):
            vec = nc.vector
            chain = [0]

            def link(ins):
                chain[0] += 1
                ins.then_inc(s_dve, 1)
                dve.wait_ge(s_dve, chain[0])

            def wide(a, n):
                return a.unsqueeze(2).to_broadcast([128, a.shape[1], n])

            def normalise(src, out, n, m, eps, count, last=True):
                total, mean, var, root, inv = (small[:, k, 0:m] for k in range(5))
                cen = xc[:].rearrange("p a b -> p (a b)").rearrange("p (m n) -> p m n", n=n)
                sqv = sq[:].rearrange("p a b -> p (a b)").rearrange("p (m n) -> p m n", n=n)
                link(vec.tensor_reduce(total, src, AX.X, ALU.add))
                link(vec.tensor_scalar(mean, total, 1.0 / n, None, ALU.mult))
                link(vec.tensor_tensor(cen, src, wide(mean, n), ALU.subtract))
                link(vec.tensor_tensor(sqv, cen, cen, ALU.mult))
                link(vec.tensor_reduce(total, sqv, AX.X, ALU.add))
                vec.tensor_scalar(var, total, 1.0 / n, eps, ALU.mult, ALU.add).then_inc(s_var, 1)
                dve.wait_ge(s_std, count)
                link(vec.reciprocal(inv, root))
                ins = vec.tensor_tensor(out, cen, wide(inv, n), ALU.mult)
                if last:
                    ins.then_inc(s_norm, 1)
                link_free(ins) if not last else None

            def link_free(ins):
                link(ins)

            dve.wait_ge(s_load, 8 * 16)
            link(vec.tensor_copy(h0[:].rearrange("p b (j s) -> p b s j", s=2), h_in[:]))
            normalise(h0[:], z[:], W, 16, 1e-5, 1)
            dve.wait_ge(s_u, 1)
            vec.tensor_copy(uT[:].rearrange("p a b -> p (a b)"), bank(2, 2)).then_inc(s_uc, 1)
            dve.wait_ge(s_s1, 1)
            for g in range(2):
                scores = bank(4 + g).rearrange("p (c m) -> p c m", m=H)
                link(vec.tensor_reduce(small[:, 5, 8 * g:8 * g + 8], scores, AX.X, ALU.max))
                t = vec.tensor_tensor(dif[:].rearrange("p a (b m) -> p (a b) m", m=H)[:, g:16:2, :], scores,
                                      wide(small[:, 5, 8 * g:8 * g + 8], H), ALU.subtract)
            t.then_inc(s_dif, 1)
            dve.wait_ge(s_exp, 1)
            link(vec.tensor_reduce(small[:, 0, 0:16], ebd[:], AX.X, ALU.add))
            link(vec.reciprocal(small[:, 1, 0:16], small[:, 0, 0:16]))
            for h in range(2):
                dve.wait_ge(s_msg, h + 1)
                t = vec.tensor_tensor(sq[:, 8 * h:8 * h + 8], bank(6 + h).rearrange("p (b m) -> p b m", m=W),
                                      wide(small[:, 1, 8 * h:8 * h + 8], W), ALU.mult)
            link(t)
            link(vec.tensor_tensor(h1[:], h0[:], sq[:], ALU.add))
            normalise(h1[:], z[:], W, 16, 1e-5, 2)

            dve.wait_ge(s_const, 16)
            for k in range(4):
                dve.wait_ge(s_mc, k + 1)
                vec.tensor_copy(sxT[:, CHUNK * k:CHUNK * k + CHUNK, 1, :],
                                sxT[:, CHUNK * k:CHUNK * k + CHUNK, 0, :]).then_inc(s_dup, 1)

            for k in range(4):
                dve.wait_ge(s_mm, 4 + 3 * k + 3)
                keys = bank(2 + k)[0:64, :].rearrange("p (b t) -> p b t", t=H)
                for n in range(NH):
                    t = vec.tensor_scalar(kr[0:64, CHUNK * k:CHUNK * k + CHUNK, n, :], keys,
                                          c["kmask"][0:64, n:n + 1], None, ALU.mult)
                t.then_inc(s_vc, 1)
            for k in range(2):
                vec.tensor_copy(vbd[:, :, k, 32:34], c["vmask"][:, 0:2].unsqueeze(1).to_broadcast([128, B, 2]))
            for k in range(8):
                dve.wait_ge(s_mm, 16 + k + 1)
                both = bank(2 + k % 4).rearrange("p (b n) -> p b n", b=4)
                for nl in range(2):
                    vec.tensor_scalar(vbd[:, 4 * k:4 * k + 4, :, 16 * nl:16 * nl + 16],
                                      both[:, :, 0:64].rearrange("p b (h l d) -> p b h l d", h=2, l=2)[:, :, :, nl, :],
                                      c["vmask"][:, nl:nl + 1], None, ALU.mult)
                vec.tensor_copy(sx[:, 4 * k:4 * k + 4, :], both[:, :, 64:128]).then_inc(s_vc, 1)

            for i in range(B + 2):
                if i < B:
                    dve.wait_ge(s_sc, i + 1)
                    s4 = bank(i % 2).rearrange("p (a t) -> p a t", t=H)
                    link(vec.tensor_reduce(small[:, i % 2, 0:8], s4, AX.X, ALU.max))
                    if i >= 2:
                        dve.wait_ge(s_pr, i - 1)
                    vec.tensor_tensor(dif[:, i % 2, :].rearrange("p (a t) -> p a t", t=H), s4,
                                      wide(small[:, i % 2, 0:8], H), ALU.subtract).then_inc(s_df, 1)
                if i >= 2:
                    j = i - 2
                    dve.wait_ge(s_av, j + 1)
                    o4 = bank(4 + j % 2)[:, 0:136].rearrange("p (a n) -> p a n", n=34)
                    den = small[:, 2 + j % 2, 0:8]
                    link(vec.reciprocal(den.rearrange("p (a n) -> p a n", n=2), o4[:, :, 32:34]))
                    q8 = qkv[:, j, 0:2, :].rearrange("p e n -> p (e n)")
                    ins = vec.tensor_tensor(q8.rearrange("p (a d) -> p a d", d=D).rearrange("p (a l) d -> p a l d", l=2),
                                            o4[:, :, 0:32].rearrange("p a (l d) -> p a l d", l=2),
                                            den.rearrange("p (a l) -> p a l", l=2).unsqueeze(3)
                                            .to_broadcast([128, 4, 2, D]), ALU.mult)
                    ins.then_inc(s_oc, 1)
                    dve.wait_ge(s_oc, j + 1)
                    q2 = qkv[:, j, 0:2, :]
                    vec.scalar_tensor_tensor(out=q2, in0=sx[:, j, :].unsqueeze(1).to_broadcast([128, 2, 64]),
                                             scalar=0.0, in1=q2, op0=ALU.not_equal, op1=ALU.mult).then_inc(s_q, 1)
            resid = c["wk"]
            for n in range(NH):
                img = (n // 2 % 2) * 16 + (n // 4) * 2 + n % 2
                t = vec.tensor_copy(resid[:, D * n:D * n + D], sx[:, img, D * n:D * n + D])

            dve.wait_ge(s_g, B)
            gl = gs[:].rearrange("p b n e -> p b (n e)")
            link(vec.tensor_tensor(gl, bank(7).rearrange("p (b n) -> p b n", b=B),
                                   c["gate_b"].unsqueeze(1).to_broadcast([128, B, 16]), ALU.add))
            g3 = gs[:].rearrange("p b n e -> p (b n) e")
            gm = ebd[:].rearrange("p a b -> p (a b)")[:, 256:384]
            link(vec.tensor_reduce(gm, g3, AX.X, ALU.max))
            vec.tensor_tensor(g3, g3, wide(gm, NE), ALU.subtract).then_inc(s_gd, 1)
            dve.wait_ge(s_ge, 1)
            link(vec.tensor_reduce(gm, g3, AX.X, ALU.add))
            link(vec.reciprocal(gm, gm))
            link(vec.tensor_tensor(g3, g3, wide(gm, NE), ALU.mult))
            for e2 in range(2):
                g = slice(64 * e2, 64 * e2 + 64)
                for eh in range(2):
                    t = vec.tensor_copy(gsel[g, :, eh, :], gs[g, :, :, 2 * eh + e2])
            link(t)
            for k in range(2):
                half = slice(B // 2 * k, B // 2 * k + B // 2)
                for eh in range(2):
                    q4 = qkv[:, half, eh, :].rearrange("p b (n d) -> p b n d", d=D)
                    t = vec.tensor_tensor(q4, q4, gsel[:, half, eh, :].unsqueeze(3)
                                          .to_broadcast([128, B // 2, NH, D]), ALU.mult)
                link(t)
                vec.tensor_tensor(mixed[:, half], qkv[:, half, 0, :], qkv[:, half, 1, :], ALU.add).then_inc(s_mx, 1)

            y = h_in[:].rearrange("p b s j -> p b (s j)")
            for k in range(2):
                dve.wait_ge(s_fold, k + 1)
                t = vec.tensor_tensor(y[:, k:16:2, :], bank(4 + k).rearrange("p (c n) -> p c n", n=64),
                                      resid.unsqueeze(1).to_broadcast([128, 8, 64]), ALU.add)
            link(t)

            rows = lambda a: a.rearrange("p b (n d) -> p (b n) d", d=D)
            vecs = lambda name: c[name].unsqueeze(1).to_broadcast([128, 64, D])
            fx = rows(z[:])
            t3 = rows(sq[:])
            ffp = bank(2, 2).rearrange("p (m d) -> p m d", d=D)
            normalise(rows(y), fx, D, 64, 1e-8, 3, last=False)
            link(vec.tensor_tensor(fx, fx, vecs("ln_g"), ALU.mult))
            vec.tensor_tensor(fx, fx, vecs("ln_b"), ALU.add).then_inc(s_norm, 1)

            live = sx[:, 0:16, :].rearrange("p b (n d) -> p (b n) d", d=D)
            base = rows(h0[:])
            dve.wait_ge(s_norm, 3)
            link(vec.tensor_scalar(live, fx, 0.0, None, ALU.not_equal))
            link(vec.tensor_tensor(base, live, vecs("fc2_b"), ALU.mult))
            link(vec.tensor_tensor(base, base, fx, ALU.add))
            halves = [slice(0, 32), slice(32, 64)]
            for h, g in enumerate(halves):
                dve.wait_ge(s_f, 1 + h)
                t = vec.tensor_tensor(t3[:, g], ffp[:, g], vecs("fc1_b")[:, g], ALU.add)
            link(t)
            vec.scalar_tensor_tensor(out=rows(xc[:]), in0=t3, scalar=0.0, in1=live, op0=ALU.max,
                                     op1=ALU.mult).then_inc(s_norm, 1)
            hy = rows(h0[:])
            for h, g in enumerate(halves):
                dve.wait_ge(s_f, 3 + h)
                t = vec.tensor_tensor(t3[:, g], ffp[:, g], live[:, g], ALU.mult)
            link(t)
            link(vec.tensor_tensor(hy, t3, base, ALU.add))
            normalise(hy, fx, D, 64, 1e-8, 4, last=False)
            link(vec.tensor_tensor(fx, fx, vecs("fnorm_g"), ALU.mult))
            vec.tensor_tensor(fx, fx, vecs("fnorm_b"), ALU.add).then_inc(s_norm, 1)

            dve.wait_ge(s_f, 6)
            fg = gs[:, 0:4].rearrange("p a b c -> p (a b c)")
            fl = fg.rearrange("p (m n) -> p m n", n=NH)
            lg = bank(2, 2)[:, 0:64].rearrange("p (m n) -> p m n", n=NH)
            fm = small[:, 0, 0:16]
            link(vec.tensor_reduce(fm, lg, AX.X, ALU.max))
            vec.tensor_tensor(fl, lg, wide(fm, NH), ALU.subtract).then_inc(s_fe, 1)
            dve.wait_ge(s_fee, 1)
            link(vec.tensor_reduce(fm, fl, AX.X, ALU.add))
            link(vec.reciprocal(fm, fm))
            link(vec.tensor_tensor(fl, fl, wide(fm, NH), ALU.mult))
            link(vec.tensor_tensor(fx, fx, wide(fg, D), ALU.mult))
            vec.tensor_tensor(h1[:], h1[:], z[:], ALU.add).then_inc(s_out, 1)


def tail_inputs(t):
    t = {k: np.asarray(v) for k, v in t.items()}

    def diag(w, n, rows=128):
        a, b = w.shape
        out = np.zeros((rows, n * b), np.float32)
        for k in range(n):
            out[a * k:a * k + a, b * k:b * k + b] = w
        return out

    def heads(ws, rows=128):
        a, b = ws[0].shape
        out = np.zeros((rows, len(ws) * b), np.float32)
        for k, w in enumerate(ws):
            out[a * k:a * k + a, b * k:b * k + b] = w
        return out

    p = {}
    p["ident"] = np.eye(128, dtype=np.float32)
    p["w_attn"] = diag(t["L0_attn_W"], 2)
    p["hl"] = diag(t["L0_ffn_hl_w"].reshape(64, 64).T, 2)
    hl_b = np.zeros((128, 1), np.float32)
    hl_b[0:64, 0] = t["L0_ffn_hl_b"].reshape(64)
    p["hl_b"] = hl_b
    wq = t["L0_ffn_wq"]
    p["wq"] = np.concatenate([heads([wq[n, e].T for n in range(NH)]) for e in range(NE)], axis=1)
    p["wk"] = heads([w.T for w in t["L0_ffn_wk"]])
    eye64 = np.zeros((128, 64), np.float32)
    eye64[0:64] = np.eye(64)
    p["wvi"] = np.concatenate([heads([w.T for w in t["L0_ffn_wv"]]), eye64], axis=1)
    kmask = np.zeros((128, 4), np.float32)
    for n in range(NH):
        kmask[D * n:D * n + D, n] = 1
    p["kmask"] = kmask
    vmask = np.zeros((128, 4), np.float32)
    vmask[0:64, 0] = 1
    vmask[64:128, 1] = 1
    p["vmask"] = vmask
    gw = t["L0_ffn_gate_w"].reshape(NH, NE, 2, 2, D)
    gate = np.zeros((2, NH, D, 2, NH, NE), np.float32)
    for n in range(NH):
        gate[:, n, :, :, n, :] = gw[n].transpose(1, 3, 2, 0)
    p["gate"] = gate.reshape(128, 32)
    row = lambda a: np.tile(a.reshape(1, -1), (128, 1))
    p["gate_b"] = row(t["L0_ffn_gate_b"])
    p["fc1"] = diag(t["L0_ffn_fc1_w"].T, 8)
    p["fc2"] = diag(t["L0_ffn_fc2_w"].T, 8)
    p["fgate"] = diag(t["L0_ffn_fgate_w"].T, 2)
    for a in ("fc1_b", "fc2_b", "ln_g", "ln_b", "fnorm_g", "fnorm_b"):
        p[a] = row(t["L0_ffn_" + a])
    p["fold"] = np.tile(np.eye(64, dtype=np.float32), (2, 1))
    onehot = np.tile(np.eye(64, dtype=np.float32)[:, None, :], (1, B, NE)).reshape(64, B, NE * H)
    causal = np.where(np.tri(H, dtype=bool), 0.0, NEG).astype(np.float32)
    causal = np.tile(causal[:, None, :], (1, B, NH)).reshape(64, B, NH * H)
    return {"tail": np.concatenate([p[n] for n, _ in TAIL], axis=1), "onehot": onehot, "causal": causal}


def tower_inputs(t):
    x = np.ascontiguousarray(t["x"])
    grid = np.ascontiguousarray(t["L0_tok_input_grid"])
    xin = np.empty((2, 2, 5, B, G, G), np.float32)
    xin[:, :, 0:2] = grid.reshape(G, 2, G, 2, 2).transpose(3, 1, 4, 0, 2)[:, :, :, None]
    xin[:, :, 2:5] = x.reshape(B, G, 2, G, 2, 3).transpose(4, 2, 5, 0, 1, 3)

    def per_pixel(w, rows=128):
        n, m = w.shape
        out = np.zeros((rows, 4 * m), np.float32)
        for g in range(4):
            out[n * g:n * g + n, m * g:m * g + m] = w
        return out

    conv_w = np.asarray(t["L0_tok_conv_w"])
    conv = np.zeros((NL, 2, 2, C, 2, 2, 2, 2, C), np.float32)
    for di in range(2):
        for dj in range(2):
            for r1 in range(2):
                for s1 in range(2):
                    for r in range(2):
                        for s in range(2):
                            ky, kx = 2 * di + r1 - r, 2 * dj + s1 - s
                            if 0 <= ky < 3 and 0 <= kx < 3:
                                conv[:, s1, r1, :, di, dj, s, r, :] = conv_w[:, :, :, ky, kx].transpose(0, 2, 1)
    spec = np.stack([np.asarray(t["L0_tok_spec_wr"]), np.asarray(t["L0_tok_spec_wi"])])
    spec = spec.reshape(2, NL, C, C, MODES, 4, 4).transpose(1, 6, 2, 5, 4, 0, 3)
    four = lambda b: np.tile(np.asarray(b).reshape(-1), 4).reshape(128, 1)
    return {
        "xin": xin.reshape(XIN, B, G * G),
        "pw": np.tile(per_pixel(np.asarray(t["L0_tok_P_w"]), 32), (4, 1)),
        "pb": four(t["L0_tok_P_b"]),
        "dft": dft_constants(),
        "spec": np.ascontiguousarray(spec).reshape(NL, 128, 4 * MODES, 2, C),
        "conv": conv.reshape(NL, 128, 4, 128),
        "convb": np.ascontiguousarray(np.tile(np.asarray(t["L0_tok_conv_b"]), (1, 4)).T),
        "q1w": per_pixel(np.asarray(t["L0_tok_Q1_w"])),
        "q1b": four(t["L0_tok_Q1_b"]),
        "q2w": per_pixel(np.asarray(t["L0_tok_Q2_w"])),
        "q2b": np.tile(np.asarray(t["L0_tok_Q2_b"]).reshape(-1), 128).reshape(128, 1),
    }


def kernel(**inputs):
    import concourse.bacc as bacc
    from concourse.bass_utils import run_bass_kernel_spmd

    nc = bacc.Bacc("TRN2", target_bir_lowering=False, num_devices=1)
    laid = {**tower_inputs(inputs), **tail_inputs(inputs)}
    arrays, args = {}, []
    for name, a in laid.items():
        arrays[f"in_{name}"] = np.ascontiguousarray(a)
        args.append(nc.dram_tensor(f"in_{name}", a.shape, mybir.dt.from_np(a.dtype), kind="ExternalInput").ap())
    args.append(nc.dram_tensor("out", (B, H, W), F32, kind="ExternalOutput").ap())
    build(nc, *args)
    r = run_bass_kernel_spmd(nc, [arrays], core_ids=[0])
    return r.results[0]["out"]
```
